# Optimizing a Trainium2 kernel written in Bass

```python
import numpy as np
import jax
import jax.numpy as jnp

def _softmax(x, axis=-1):
    return jax.nn.softmax(x, axis=axis)

def _gelu(x):
    return jax.nn.gelu(x, approximate=True)

def _silu(x):
    return jax.nn.silu(x)

def _sigmoid(x):
    return jax.nn.sigmoid(x)

def _layernorm(x, axis=-1, eps=1e-05):
    m = jnp.mean(x, axis=axis, keepdims=True)
    v = jnp.var(x, axis=axis, keepdims=True)
    return (x - m) / jnp.sqrt(v + eps)

def _scatter_add(tgt, idx, src, axis=0):
    return tgt.at[idx].add(src)

def _segment_sum(src, seg, n):
    return jax.ops.segment_sum(src, seg, n)
kernel_name = 'mk_decoder_preln_d2_seqx_r4_c89636'

def setup_inputs(seed: int=0):
    np.random.seed(seed)
    _w = jnp.asarray

    def _rec_inputs():
        import jax
        import jax.numpy as jnp
        _rk = jax.random.key(seed)
        x = 7.22e-05 + 1 * jax.random.normal(jax.random.fold_in(_rk, 1), (4, 1024, 256), jnp.float32)
        _lenS = 1024 - jax.random.randint(jax.random.fold_in(_rk, 7), (4,), 0, max(1, 1024 // 4) + 1, jnp.int32)
        _lenS2 = 64 - jax.random.randint(jax.random.fold_in(_rk, 8), (4,), 0, max(1, 64 // 4) + 1, jnp.int32)
        _ctx_768P = jax.random.normal(jax.random.fold_in(_rk, 11), (4, 16, 192), jnp.float32)
        _ctx_768c = jax.random.dirichlet(jax.random.fold_in(_rk, 511), 0.3 * jnp.ones((16,), jnp.float32), (4, 64))
        _ctx_768t = jnp.einsum('bsk,bkd->bsd', _ctx_768c, _ctx_768P)
        _ctx_768t = _ctx_768t * jax.lax.rsqrt(jnp.mean(jnp.square(_ctx_768t)) + 1e-12) * 0.953939
        ctx_768 = -0.000191848 + 0.999787 * (_ctx_768t + 0.3 * jax.random.normal(jax.random.fold_in(_rk, 611), (4, 64, 192), jnp.float32))
        _validS = jnp.arange(1024)[None, :] < _lenS[:, None]
        _validS2 = jnp.arange(64)[None, :] < _lenS2[:, None]
        _causal = jnp.tril(jnp.ones((1024, 1024), dtype=bool))
        mask_BxS2_bk0 = jnp.logical_not(jnp.broadcast_to(_validS2[:, :], (4, 64)))
        return (x, ctx_768, mask_BxS2_bk0)
    x, ctx_768, mask_BxS2_bk0 = _rec_inputs()

    def _L0_attn_setup():
        import jax, jax.numpy as jnp
        import numpy as np
        import math
        B, N, D = (64, 128, 256)
        SHELL_DIM, RFF_DIM, ORDER = (64, 32, 4)
        CHARGE_COUPLING, SHELL_COUPLING = (1.0, 0.5)
        DIST_COUPLING, DIST_SCALE = (0.3, 10.0)
        COMBINED_DIM = 64

        def _forward(x, W_charge, b_charge, W_shell, b_shell, omega, rff_bias, W_combine, W_v, b_v, W_out, b_out, log_temp):
            b, n, d = x.shape
            q = jnp.tanh(x @ W_charge.T + b_charge)[..., 0]
            coeffs = jnp.asarray([(-CHARGE_COUPLING) ** m / math.factorial(m) for m in range(ORDER + 1)], dtype=x.dtype)
            mags = jnp.sqrt(jnp.abs(coeffs) + 1e-10)
            phi_c = mags * q[..., None] ** jnp.arange(ORDER + 1)
            shell = x @ W_shell.T + b_shell
            shell = shell / jnp.maximum(jnp.linalg.norm(shell, axis=-1, keepdims=True), 1e-12)
            proj = shell @ omega.T + rff_bias
            rff_scale = math.sqrt(2.0 / (2 * RFF_DIM)) * math.sqrt(math.exp(-SHELL_COUPLING))
            phi_s = jnp.concatenate([jnp.cos(proj), jnp.sin(proj)], axis=-1) * rff_scale
            tp = (phi_c[..., :, None] * phi_s[..., None, :]).reshape(b, n, -1)
            phi = tp @ W_combine.T
            idx = jnp.arange(n)
            T = jnp.exp(-DIST_COUPLING * jnp.abs(idx[:, None] - idx[None, :]).astype(x.dtype) / DIST_SCALE)
            temp = jax.nn.softplus(log_temp) + 0.1
            logits = jnp.einsum('bnd,bmd->bnm', phi, phi) * T / temp
            causal = idx[:, None] >= idx[None, :]
            logits = jnp.where(causal, logits, -jnp.inf)
            attn = jax.nn.softmax(logits, axis=-1)
            V = x @ W_v.T + b_v
            out = jnp.einsum('bnm,bmd->bnd', attn, V)
            return out @ W_out.T + b_out
        key = jax.random.key(seed)
        ks = jax.random.split(key, 12)
        s = 0.02
        inp = {'x': jax.random.normal(ks[0], (B, N, D), dtype=jnp.float32), 'W_charge': jax.random.normal(ks[1], (1, D), dtype=jnp.float32) * s, 'b_charge': jnp.zeros((1,), dtype=jnp.float32), 'W_shell': jax.random.normal(ks[2], (SHELL_DIM, D), dtype=jnp.float32) * s, 'b_shell': jnp.zeros((SHELL_DIM,), dtype=jnp.float32), 'omega': jax.random.normal(ks[3], (RFF_DIM, SHELL_DIM), dtype=jnp.float32) * math.sqrt(SHELL_COUPLING), 'rff_bias': jax.random.uniform(ks[4], (RFF_DIM,), dtype=jnp.float32) * (2.0 * math.pi), 'W_combine': jax.random.normal(ks[5], (COMBINED_DIM, (ORDER + 1) * 2 * RFF_DIM), dtype=jnp.float32) * s, 'W_v': jax.random.normal(ks[6], (D, D), dtype=jnp.float32) * s, 'b_v': jnp.zeros((D,), dtype=jnp.float32), 'W_out': jax.random.normal(ks[7], (D, D), dtype=jnp.float32) * s, 'b_out': jnp.zeros((D,), dtype=jnp.float32), 'log_temp': jnp.zeros((), dtype=jnp.float32)}
        return inp
    _L0_attn_all = _L0_attn_setup()
    _L0_attn_in = {k: v for k, v in _L0_attn_all.items() if k in ('W_charge', 'b_charge', 'W_shell', 'b_shell', 'omega', 'rff_bias', 'W_combine', 'W_v', 'b_v', 'W_out', 'b_out', 'log_temp')}
    del _L0_attn_all

    def _L0_xattn_setup():
        import jax, jax.numpy as jnp
        import numpy as np
        HEADS = 8
        DIM_HEAD = 64
        QUERY_DIM = 256
        CONTEXT_DIM = 192
        INNER = HEADS * DIM_HEAD
        key = jax.random.key(seed)
        ks = jax.random.split(key, 8)
        b, n, j = (4, 512, 512)
        x = jax.random.normal(ks[0], (b, n, QUERY_DIM), dtype=jnp.float32)
        context = jax.random.normal(ks[1], (b, j, CONTEXT_DIM), dtype=jnp.float32)
        mask = jax.random.randint(ks[2], (b, j), 0, 2).astype(jnp.bool_)
        W_q = jax.random.normal(ks[3], (QUERY_DIM, INNER), dtype=jnp.float32) / np.sqrt(QUERY_DIM)
        W_k = jax.random.normal(ks[4], (CONTEXT_DIM, INNER), dtype=jnp.float32) / np.sqrt(CONTEXT_DIM)
        W_v = jax.random.normal(ks[5], (CONTEXT_DIM, INNER), dtype=jnp.float32) / np.sqrt(CONTEXT_DIM)
        W_o = jax.random.normal(ks[6], (INNER, QUERY_DIM), dtype=jnp.float32) / np.sqrt(INNER)
        b_o = jax.random.normal(ks[7], (QUERY_DIM,), dtype=jnp.float32) * 0.01
        return {'x': x, 'context': context, 'mask': mask, 'W_q': W_q, 'W_k': W_k, 'W_v': W_v, 'W_o': W_o, 'b_o': b_o}
    _L0_xattn_all = _L0_xattn_setup()
    _L0_xattn_in = {k: v for k, v in _L0_xattn_all.items() if k in ('W_q', 'W_k', 'W_v', 'W_o', 'b_o')}
    del _L0_xattn_all

    def _L0_ffn_setup():
        import jax, jax.numpy as jnp
        import numpy as np
        D_MODEL = 256
        D_FF = 1024
        NUM_EXPERTS = 8
        B, N = (16, 256)
        key = jax.random.key(seed)
        ks = jax.random.split(key, 7)
        s_in = 1.0 / np.sqrt(D_MODEL)
        s_ff = 1.0 / np.sqrt(D_FF)
        return {'x': jax.random.normal(ks[0], (B, N, D_MODEL), dtype=jnp.float32), 'Wr': jax.random.uniform(ks[1], (D_MODEL, NUM_EXPERTS), jnp.float32, -s_in, s_in), 'br': jax.random.uniform(ks[2], (NUM_EXPERTS,), jnp.float32, -s_in, s_in), 'W1': jax.random.uniform(ks[3], (NUM_EXPERTS, D_MODEL, D_FF), jnp.float32, -s_in, s_in), 'b1': jax.random.uniform(ks[4], (NUM_EXPERTS, D_FF), jnp.float32, -s_in, s_in), 'W2': jax.random.uniform(ks[5], (NUM_EXPERTS, D_FF, D_MODEL), jnp.float32, -s_ff, s_ff), 'b2': jax.random.uniform(ks[6], (NUM_EXPERTS, D_MODEL), jnp.float32, -s_ff, s_ff)}
    _L0_ffn_all = _L0_ffn_setup()
    _L0_ffn_in = {k: v for k, v in _L0_ffn_all.items() if k in ('Wr', 'br', 'W1', 'b1', 'W2', 'b2')}
    del _L0_ffn_all

    def _L1_attn_setup():
        import jax, jax.numpy as jnp
        import numpy as np
        B, S, D = (2, 512, 256)
        H, DQ, DV = (16, 64, 64)
        key = jax.random.key(seed)
        k1, k2, k3, k4, k5 = jax.random.split(key, 5)
        scale = 0.02
        return {'x': jax.random.normal(k1, (B, S, D), dtype=jnp.float32), 'w_q': jax.random.normal(k2, (H, DQ, D), dtype=jnp.float32) * scale, 'w_k': jax.random.normal(k3, (H, DQ, D), dtype=jnp.float32) * scale, 'w_v': jax.random.normal(k4, (H, DV, D), dtype=jnp.float32) * scale, 'w_o': jax.random.normal(k5, (D, H * DV), dtype=jnp.float32) * scale}
    _L1_attn_all = _L1_attn_setup()
    _L1_attn_in = {k: v for k, v in _L1_attn_all.items() if k in ('w_q', 'w_k', 'w_v', 'w_o')}
    del _L1_attn_all

    def _L1_xattn_setup():
        import jax, jax.numpy as jnp
        import numpy as np
        N_HEADS = 16
        key = jax.random.key(seed)
        ks = jax.random.split(key, 8)
        b, l, m = (8, 256, 256)
        d_embed, d_cross = (256, 192)
        s_q = 1.0 / np.sqrt(d_embed)
        s_kv = 1.0 / np.sqrt(d_cross)
        return {'x': jax.random.normal(ks[0], (b, l, d_embed), jnp.float32), 'y': jax.random.normal(ks[1], (b, m, d_cross), jnp.float32), 'Wq': jax.random.normal(ks[2], (d_embed, d_embed), jnp.float32) * s_q, 'bq': jax.random.normal(ks[3], (d_embed,), jnp.float32) * 0.01, 'Wkv': jax.random.normal(ks[4], (2 * d_embed, d_cross), jnp.float32) * s_kv, 'bkv': jax.random.normal(ks[5], (2 * d_embed,), jnp.float32) * 0.01, 'Wo': jax.random.normal(ks[6], (d_embed, d_embed), jnp.float32) * s_q, 'bo': jax.random.normal(ks[7], (d_embed,), jnp.float32) * 0.01}
    _L1_xattn_all = _L1_xattn_setup()
    _L1_xattn_in = {k: v for k, v in _L1_xattn_all.items() if k in ('Wq', 'bq', 'Wkv', 'bkv', 'Wo', 'bo')}
    del _L1_xattn_all

    def _L1_ffn_setup():
        import jax, jax.numpy as jnp
        import numpy as np
        HIDDEN = 256
        INNER = 1024

        def _weight_quant(w):
            scale = 1.0 / jnp.clip(jnp.mean(jnp.abs(w)), 1e-05)
            wq = jnp.clip(jnp.round(w * scale), -1.0, 1.0) / scale
            return w + jax.lax.stop_gradient(wq - w)

        def _act_quant(x):
            scale = 127.0 / jnp.clip(jnp.max(jnp.abs(x), axis=-1, keepdims=True), 1e-05)
            xq = jnp.clip(jnp.round(x * scale), -128.0, 127.0) / scale
            return x + jax.lax.stop_gradient(xq - x)

        def _bitlinear(x, w):
            return jnp.einsum('bsi,oi->bso', _act_quant(x), _weight_quant(w))
        key = jax.random.key(seed)
        k0, k1, k2, k3 = jax.random.split(key, 4)
        x = jax.random.normal(k0, (4, 512, HIDDEN), dtype=jnp.float32)
        w_gate = jax.random.normal(k1, (INNER, HIDDEN), dtype=jnp.float32) / np.sqrt(HIDDEN)
        w_up = jax.random.normal(k2, (INNER, HIDDEN), dtype=jnp.float32) / np.sqrt(HIDDEN)
        w_down = jax.random.normal(k3, (HIDDEN, INNER), dtype=jnp.float32) / np.sqrt(INNER)
        return {'x': x, 'w_gate': w_gate, 'w_up': w_up, 'w_down': w_down}
    _L1_ffn_all = _L1_ffn_setup()
    _L1_ffn_in = {k: v for k, v in _L1_ffn_all.items() if k in ('w_gate', 'w_up', 'w_down')}
    del _L1_ffn_all
    return {'x': x, 'ctx_768': ctx_768, 'mask_BxS2_bk0': mask_BxS2_bk0, 'L0_attn_W_charge': _L0_attn_in['W_charge'], 'L0_attn_b_charge': _L0_attn_in['b_charge'], 'L0_attn_W_shell': _L0_attn_in['W_shell'], 'L0_attn_b_shell': _L0_attn_in['b_shell'], 'L0_attn_omega': _L0_attn_in['omega'], 'L0_attn_rff_bias': _L0_attn_in['rff_bias'], 'L0_attn_W_combine': _L0_attn_in['W_combine'], 'L0_attn_W_v': _L0_attn_in['W_v'], 'L0_attn_b_v': _L0_attn_in['b_v'], 'L0_attn_W_out': _L0_attn_in['W_out'], 'L0_attn_b_out': _L0_attn_in['b_out'], 'L0_attn_log_temp': _L0_attn_in['log_temp'], 'L0_xattn_W_q': _L0_xattn_in['W_q'], 'L0_xattn_W_k': _L0_xattn_in['W_k'], 'L0_xattn_W_v': _L0_xattn_in['W_v'], 'L0_xattn_W_o': _L0_xattn_in['W_o'], 'L0_xattn_b_o': _L0_xattn_in['b_o'], 'L0_ffn_Wr': _L0_ffn_in['Wr'], 'L0_ffn_br': _L0_ffn_in['br'], 'L0_ffn_W1': _L0_ffn_in['W1'], 'L0_ffn_b1': _L0_ffn_in['b1'], 'L0_ffn_W2': _L0_ffn_in['W2'], 'L0_ffn_b2': _L0_ffn_in['b2'], 'L1_attn_w_q': _L1_attn_in['w_q'], 'L1_attn_w_k': _L1_attn_in['w_k'], 'L1_attn_w_v': _L1_attn_in['w_v'], 'L1_attn_w_o': _L1_attn_in['w_o'], 'L1_xattn_Wq': _L1_xattn_in['Wq'], 'L1_xattn_bq': _L1_xattn_in['bq'], 'L1_xattn_Wkv': _L1_xattn_in['Wkv'], 'L1_xattn_bkv': _L1_xattn_in['bkv'], 'L1_xattn_Wo': _L1_xattn_in['Wo'], 'L1_xattn_bo': _L1_xattn_in['bo'], 'L1_ffn_w_gate': _L1_ffn_in['w_gate'], 'L1_ffn_w_up': _L1_ffn_in['w_up'], 'L1_ffn_w_down': _L1_ffn_in['w_down']}

def reference(x, ctx_768, mask_BxS2_bk0, L0_attn_W_charge, L0_attn_b_charge, L0_attn_W_shell, L0_attn_b_shell, L0_attn_omega, L0_attn_rff_bias, L0_attn_W_combine, L0_attn_W_v, L0_attn_b_v, L0_attn_W_out, L0_attn_b_out, L0_attn_log_temp, L0_xattn_W_q, L0_xattn_W_k, L0_xattn_W_v, L0_xattn_W_o, L0_xattn_b_o, L0_ffn_Wr, L0_ffn_br, L0_ffn_W1, L0_ffn_b1, L0_ffn_W2, L0_ffn_b2, L1_attn_w_q, L1_attn_w_k, L1_attn_w_v, L1_attn_w_o, L1_xattn_Wq, L1_xattn_bq, L1_xattn_Wkv, L1_xattn_bkv, L1_xattn_Wo, L1_xattn_bo, L1_ffn_w_gate, L1_ffn_w_up, L1_ffn_w_down):
    import jax
    import jax.numpy as jnp

    def _L0_attn_ref(x, W_charge, b_charge, W_shell, b_shell, omega, rff_bias, W_combine, W_v, b_v, W_out, b_out, log_temp):
        import jax, jax.numpy as jnp
        import numpy as np
        import math
        B, N, D = (64, 128, 256)
        SHELL_DIM, RFF_DIM, ORDER = (64, 32, 4)
        CHARGE_COUPLING, SHELL_COUPLING = (1.0, 0.5)
        DIST_COUPLING, DIST_SCALE = (0.3, 10.0)
        COMBINED_DIM = 64

        def _forward(x, W_charge, b_charge, W_shell, b_shell, omega, rff_bias, W_combine, W_v, b_v, W_out, b_out, log_temp):
            b, n, d = x.shape
            q = jnp.tanh(x @ W_charge.T + b_charge)[..., 0]
            coeffs = jnp.asarray([(-CHARGE_COUPLING) ** m / math.factorial(m) for m in range(ORDER + 1)], dtype=x.dtype)
            mags = jnp.sqrt(jnp.abs(coeffs) + 1e-10)
            phi_c = mags * q[..., None] ** jnp.arange(ORDER + 1)
            shell = x @ W_shell.T + b_shell
            shell = shell / jnp.maximum(jnp.linalg.norm(shell, axis=-1, keepdims=True), 1e-12)
            proj = shell @ omega.T + rff_bias
            rff_scale = math.sqrt(2.0 / (2 * RFF_DIM)) * math.sqrt(math.exp(-SHELL_COUPLING))
            phi_s = jnp.concatenate([jnp.cos(proj), jnp.sin(proj)], axis=-1) * rff_scale
            tp = (phi_c[..., :, None] * phi_s[..., None, :]).reshape(b, n, -1)
            phi = tp @ W_combine.T
            idx = jnp.arange(n)
            T = jnp.exp(-DIST_COUPLING * jnp.abs(idx[:, None] - idx[None, :]).astype(x.dtype) / DIST_SCALE)
            temp = jax.nn.softplus(log_temp) + 0.1
            logits = jnp.einsum('bnd,bmd->bnm', phi, phi) * T / temp
            causal = idx[:, None] >= idx[None, :]
            logits = jnp.where(causal, logits, -jnp.inf)
            attn = jax.nn.softmax(logits, axis=-1)
            V = x @ W_v.T + b_v
            out = jnp.einsum('bnm,bmd->bnd', attn, V)
            return out @ W_out.T + b_out
        return _forward(x, W_charge, b_charge, W_shell, b_shell, omega, rff_bias, W_combine, W_v, b_v, W_out, b_out, log_temp)

    def _L0_xattn_ref(x, context, mask, W_q, W_k, W_v, W_o, b_o):
        import jax, jax.numpy as jnp
        import numpy as np
        HEADS = 8
        DIM_HEAD = 64
        QUERY_DIM = 256
        CONTEXT_DIM = 192
        INNER = HEADS * DIM_HEAD
        b, n, _ = x.shape
        j = context.shape[1]
        scale = DIM_HEAD ** (-0.5)
        q = (x @ W_q).reshape(b, n, HEADS, DIM_HEAD)
        k = (context @ W_k).reshape(b, j, HEADS, DIM_HEAD)
        v = (context @ W_v).reshape(b, j, HEADS, DIM_HEAD)
        sim = jnp.einsum('bihd,bjhd->bhij', q, k) * scale
        max_neg = -jnp.finfo(sim.dtype).max
        sim = jnp.where(mask[:, None, None, :], sim, max_neg)
        attn = jax.nn.softmax(sim, axis=-1)
        out = jnp.einsum('bhij,bjhd->bihd', attn, v).reshape(b, n, INNER)
        return out @ W_o + b_o

    def _L0_ffn_ref(x, Wr, br, W1, b1, W2, b2):
        import jax, jax.numpy as jnp
        import numpy as np
        D_MODEL = 256
        D_FF = 1024
        NUM_EXPERTS = 8
        B, N = (16, 256)
        scores = jnp.einsum('bh,he->be', x.mean(axis=1), Wr) + br
        top1 = jnp.argmax(scores, axis=-1)
        w1 = W1[top1]
        c1 = b1[top1]
        w2 = W2[top1]
        c2 = b2[top1]
        h = jax.nn.relu(jnp.einsum('bnh,bhf->bnf', x, w1) + c1[:, None, :])
        out = jnp.einsum('bnf,bfh->bnh', h, w2) + c2[:, None, :]
        return out

    def _L1_attn_ref(x, w_q, w_k, w_v, w_o):
        import jax, jax.numpy as jnp
        import numpy as np
        B, S, D = (2, 512, 256)
        H, DQ, DV = (16, 64, 64)
        b, s, d = x.shape
        q = jnp.einsum('bsd,hqd->bhsq', x, w_q)
        k = jnp.einsum('bsd,hqd->bhsq', x, w_k)
        v = jnp.einsum('bsd,hvd->bhsv', x, w_v)
        scores = jnp.einsum('bhsq,bhtq->bhst', q, k)
        causal = jnp.triu(jnp.ones((s, s), dtype=bool), k=1)
        masked = jnp.where(causal, -jnp.inf, scores)
        dq = w_q.shape[1]
        weights = jax.nn.softmax(masked / jnp.sqrt(jnp.float32(dq)), axis=-1)
        out = jnp.einsum('bhst,bhtv->bhsv', weights, v)
        cat = out.transpose(0, 2, 1, 3).reshape(b, s, -1)
        return jnp.einsum('bsf,df->bsd', cat, w_o)

    def _L1_xattn_ref(x, y, Wq, bq, Wkv, bkv, Wo, bo):
        import jax, jax.numpy as jnp
        import numpy as np
        N_HEADS = 16
        b, l, d = x.shape
        m = y.shape[1]
        h = N_HEADS
        dh = d // h
        q = (jnp.einsum('bld,ed->ble', x, Wq) + bq).reshape(b, l, h, dh)
        kv = (jnp.einsum('bmc,ec->bme', y, Wkv) + bkv).reshape(b, m, h, 2 * dh)
        k, v = (kv[..., :dh], kv[..., dh:])
        scale = 1.0 / jnp.sqrt(jnp.asarray(dh, x.dtype))
        att = jax.nn.softmax(jnp.einsum('blhd,bmhd->blmh', q, k) * scale, axis=2)
        out = jnp.einsum('blmh,bmhd->blhd', att, v).reshape(b, l, d)
        return jnp.einsum('bld,ed->ble', out, Wo) + bo

    def _L1_ffn_ref(x, w_gate, w_up, w_down):
        import jax, jax.numpy as jnp
        import numpy as np
        HIDDEN = 256
        INNER = 1024

        def _weight_quant(w):
            scale = 1.0 / jnp.clip(jnp.mean(jnp.abs(w)), 1e-05)
            wq = jnp.clip(jnp.round(w * scale), -1.0, 1.0) / scale
            return w + jax.lax.stop_gradient(wq - w)

        def _act_quant(x):
            scale = 127.0 / jnp.clip(jnp.max(jnp.abs(x), axis=-1, keepdims=True), 1e-05)
            xq = jnp.clip(jnp.round(x * scale), -128.0, 127.0) / scale
            return x + jax.lax.stop_gradient(xq - x)

        def _bitlinear(x, w):
            return jnp.einsum('bsi,oi->bso', _act_quant(x), _weight_quant(w))
        gate = jax.nn.silu(_bitlinear(x, w_gate))
        up = _bitlinear(x, w_up)
        return _bitlinear(gate * up, w_down)
    x = x + _L0_attn_ref(_layernorm(x, axis=-1), L0_attn_W_charge, L0_attn_b_charge, L0_attn_W_shell, L0_attn_b_shell, L0_attn_omega, L0_attn_rff_bias, L0_attn_W_combine, L0_attn_W_v, L0_attn_b_v, L0_attn_W_out, L0_attn_b_out, L0_attn_log_temp)
    x = x + _L0_xattn_ref(_layernorm(x, axis=-1), ctx_768, mask_BxS2_bk0, L0_xattn_W_q, L0_xattn_W_k, L0_xattn_W_v, L0_xattn_W_o, L0_xattn_b_o)
    x = x + _L0_ffn_ref(_layernorm(x, axis=-1), L0_ffn_Wr, L0_ffn_br, L0_ffn_W1, L0_ffn_b1, L0_ffn_W2, L0_ffn_b2)
    x = x + _L1_attn_ref(_layernorm(x, axis=-1), L1_attn_w_q, L1_attn_w_k, L1_attn_w_v, L1_attn_w_o)
    x = x + _L1_xattn_ref(_layernorm(x, axis=-1), ctx_768, L1_xattn_Wq, L1_xattn_bq, L1_xattn_Wkv, L1_xattn_bkv, L1_xattn_Wo, L1_xattn_bo)
    x = x + _L1_ffn_ref(_layernorm(x, axis=-1), L1_ffn_w_gate, L1_ffn_w_up, L1_ffn_w_down)
    return x

_drawn_inputs = setup_inputs


def setup_inputs(seed=0):
    import zlib

    import numpy as np

    out = dict(_drawn_inputs(seed))
    spreads = {'L0_attn_b_shell': (0.0, 0.8), 'L0_attn_b_v': (0.0, 0.1), 'L0_attn_b_out': (0.0, 0.1)}
    factors = {'L0_attn_W_charge': 8.0,
     'L0_attn_W_shell': 8.0,
     'L0_attn_omega': 8.0,
     'L0_attn_rff_bias': 8.0,
     'L0_attn_W_combine': 8.0,
     'L0_attn_W_v': 7.491,
     'L0_xattn_b_o': 6.805,
     'L0_ffn_b1': 4.812,
     'L0_ffn_b2': 3.961,
     'L1_attn_w_q': 8.0,
     'L1_attn_w_k': 8.0,
     'L1_xattn_bq': 33.178,
     'L1_xattn_bkv': 7.666,
     'L1_xattn_bo': 7.061}
    for name, (base, spread) in spreads.items():
        noise = np.random.default_rng([zlib.crc32(name.encode()), seed]).standard_normal(out[name].shape)
        drawn = base * np.exp(spread * noise) if base else spread * noise
        out[name] = jnp.asarray(drawn.astype(out[name].dtype))
    for name, factor in factors.items():
        out[name] = (out[name] * factor).astype(out[name].dtype)
    return out
```

```python
from contextlib import ExitStack
import math

import concourse.bass as bass
from concourse import mybir

P = 128
B, T, D = 4, 1024, 256
NT = T // P
DC = D // P
HALF = 512
CTX, CK = 192, 64
SHELL, RFF, ORDERS, COMB = 64, 32, 5, 64
FF = 1024
FC = FF // P
EXPERTS = 8
XH0, XD0 = 8, 64
XH1, XD1 = 16, 16
SD = 64
HP = 8
NPH = 6

NEG = -1.0e30
MASKED = -float(2.0 ** 127)
MAGIC = 12582912.0
TWO_PI_HI = 6.28125
TWO_PI_LO = 2.0 * math.pi - 6.28125
PI_BELOW = 3.1415925
EPS = 1e-5

F32 = mybir.dt.float32
F32R = mybir.dt.float32r
BF16 = mybir.dt.bfloat16
I32 = mybir.dt.int32
U32 = mybir.dt.uint32
U8 = mybir.dt.uint8
ALU = mybir.AluOpType
ACT = mybir.ActivationFunctionType
AX = mybir.AxisListType


def rows(ap):
    return ap.rearrange("(o n) -> o n", o=1).to_broadcast([P, ap.shape[0]])


def decoder_kernel(nc, a, out):
    ctx = ExitStack()
    with ctx:
        def sb(name, shape, dt=F32, stack=ctx):
            return stack.enter_context(nc.sbuf_tensor(name, shape, dt))

        def sem(name):
            return ctx.enter_context(nc.semaphore(name))

        xin = sb("xin", [P, NT, D])
        x = sb("x", [P, NT, D])
        xn = sb("xn", [P, NT, D])
        xTh = sb("xTh", [P, DC, T], F32R)
        xTl = sb("xTl", [P, DC, T], F32R)
        idf = sb("idf", [P, P])
        idb = sb("idb", [P, P], BF16)
        causal = sb("causal", [P, P], BF16)
        ones_b = sb("ones_b", [1, P], BF16)
        ones_r = sb("ones_r", [2, P], F32R)
        ones_f = sb("ones_f", [P, P])
        decay = sb("decay", [P, T])
        wsh_h = sb("wsh_h", [P, DC, 66], F32R)
        wsh_l = sb("wsh_l", [P, DC, 66], F32R)
        bsh = sb("bsh", [P, 66])
        om_h = sb("om_h", [SHELL, P], F32R)
        om_l = sb("om_l", [SHELL, P], F32R)
        rbias = sb("rbias", [SHELL, 1])
        cosb = sb("cosb", [SHELL, 1])
        coss = sb("coss", [SHELL, 1])
        wc_h = sb("wc_h", [SHELL, ORDERS * COMB], F32R)
        wc_l = sb("wc_l", [SHELL, ORDERS * COMB], F32R)
        wvo_h = sb("wvo_h", [P, DC, D], F32R)
        wvo_l = sb("wvo_l", [P, DC, D], F32R)
        bvo = sb("bvo", [P, D])
        x0_wq = sb("x0_wq", [P, 4, D])
        x0_wk = sb("x0_wk", [P, 2, 512])
        x0_wv = sb("x0_wv", [P, 2, 512])
        x0_wo = sb("x0_wo", [P, 4, D])
        x0_bo = sb("x0_bo", [P, D])
        x1_wq = sb("x1_wq", [P, 2, D])
        x1_wk = sb("x1_wk", [P, 2, D])
        x1_wv = sb("x1_wv", [P, 2, D])
        x1_wo = sb("x1_wo", [P, 2, D])
        x1_bo = sb("x1_bo", [P, D])
        x1_bk = sb("x1_bk", [P, 2])
        x1_bv = sb("x1_bv", [P, 2])
        x1_bq = sb("x1_bq", [P, 2])
        x1_bqb = sb("x1_bqb", [P, 2, P])
        blk0 = sb("blk0", [P, 2])
        blk1 = sb("blk1", [P, 8])
        row01 = sb("row01", [P, 2])
        wr = sb("wr", [P, DC, EXPERTS])
        br = sb("br", [1, EXPERTS])
        wo = sb("wo", [P, HP, D])
        wg_q = sb("wg_q", [P, DC, FF], BF16)
        wu_q = sb("wu_q", [P, DC, FF], BF16)
        wd_q = sb("wd_q", [P, FC, D], BF16)
        wsc = sb("wsc", [P, 4])
        st = sb("st", [P, NT, 6])
        ag = sb("ag", [P, NT, 2])
        rsd = sb("rsd", [P, NT])
        nv = sb("nv", [P, NT])
        nt1 = sb("nt1", [P, NT])
        ctxT = sb("ctxT", [P, 2, CK])
        mrow4 = sb("mrow4", [1, CK // 4], I32)
        mrow = sb("mrow", [1, XH0 * CK], BF16)
        sums = sb("sums", [P, 4])
        nmax = sb("nmax", [P, 4])
        rec = sb("rec", [P, 4])
        ps = ctx.enter_context(nc.psum_tensor("ps", [P, 8, HALF], F32))

        base_names = []

        def arena(names_shapes):
            with ExitStack() as phase:
                made = {n: phase.enter_context(nc.sbuf_tensor(n, s, d)) for n, s, d in names_shapes}
                base_names.append(nc.sbuf_bytes_remaining)
            return made

        S = arena([
            ("s_wsh", [P, DC, 66], F32), ("s_om", [SHELL, P], F32), ("s_wc", [SHELL, ORDERS, COMB], F32),
            ("s_wv", [P, DC, D], F32), ("s_wo", [P, DC, D], F32), ("s_bv", [P, DC], F32), ("s_bo", [P, D], F32),
            ("s_bvb", [P, DC, P], F32), ("s_lt", [P, 1], F32), ("s_t", [P, 4], F32),
            ("s_iota", [P, T], I32), ("s_dist", [P, T], F32),
            ("s_g", [P, 2048], F32), ("s_u", [P, 2048], F32), ("s_d", [P, 2048], F32),
            ("s_q", [P, 2048], F32), ("s_abs", [P, 4], F32), ("s_i8", [P, 8], F32), ("s_p", [P, 2], F32),
            ("s_pi", [P, 1], I32), ("s_m", [P, 1], F32)])
        A = arena([
            ("a_sh", [P, NT, 66], F32), ("a_q", [P, NT], F32), ("a_sq", [P, NT, SHELL], F32), ("a_ss", [P, NT], F32),
            ("a_rn", [P, NT], F32), ("a_shn", [P, NT, P], F32),
            ("a_shTh", [SHELL, T], F32R), ("a_shTl", [SHELL, T], F32R),
            ("a_p", [SHELL, T], F32), ("a_k", [SHELL, T], F32), ("a_r", [SHELL, T], F32), ("a_phs", [SHELL, T], F32),
            ("a_phh", [SHELL, T], F32R), ("a_phl", [SHELL, T], F32R),
            ("a_y", [P, NT, ORDERS * COMB], F32), ("a_acc", [P, NT, COMB], F32), ("a_phi", [P, NT, P], F32),
            ("a_v", [P, NT, D], F32),
            ("a_qs", [P, T], F32R), ("a_k1", [P, T], F32R), ("a_k2", [P, T], F32R),
            ("a_sm", [P, 2, T], F32), ("a_pe", [P, 2, T], F32), ("a_pt", [P, 2, T], F32)])
        X = arena([
            ("c_kT", [P, 4, CK], F32), ("c_vT", [P, 4, CK], F32),
            ("c_kB", [P, 4, P], F32), ("c_vB", [P, 4, P], F32), ("c_kC", [P, 2, HALF], F32), ("c_vC", [P, 2, HALF], F32),
            ("c_mh", [P, DC, 1024], F32R), ("c_ml", [P, DC, 1024], F32R),
            ("c_uh", [P, 8, D], F32R), ("c_ul", [P, 8, D], F32R),
            ("c_b2", [P, 1024], F32R), ("c_bh", [P, 1024], F32R), ("c_bl", [P, 1024], F32),
            ("c_mx", [P, 2, 16], F32), ("c_sm", [P, 2, 1024], F32), ("c_pe", [P, 2, 1024], F32),
            ("c_su", [P, 2, 16], F32), ("c_re", [P, 2, 16], F32), ("c_pn", [P, 2, 1024], F32),
            ("c_th", [P, 2, 1024], F32R), ("c_tl", [P, 2, 1024], F32R)])
        M = arena([
            ("m_mean", [P, DC], F32), ("m_sc", [1, EXPERTS], F32), ("m_top", [1, 8], F32), ("m_idx", [1, 8], U32),
            ("m_w1", [P, DC, FF], F32), ("m_w2", [P, FC, D], F32), ("m_b1", [P, FC], F32), ("m_b2", [P, D], F32),
            ("m_w1h", [P, DC, FF], F32R), ("m_w1l", [P, DC, FF], F32R),
            ("m_w2h", [P, FC, D], F32R), ("m_w2l", [P, FC, D], F32R),
            ("m_h", [P, 2, HALF], F32),
            ("m_hh", [P, FC, HALF], F32R), ("m_hl", [P, FC, HALF], F32R)])
        L = arena([
            ("l_w", [P, 3, DC, P], F32), ("l_wh", [P, 3, DC, P], F32R), ("l_wl", [P, 3, DC, P], F32R),
            ("l_q0", [P, T], F32R), ("l_q1", [P, T], F32R),
            ("l_k10", [P, T], F32R), ("l_k11", [P, T], F32R), ("l_k20", [P, T], F32R), ("l_k21", [P, T], F32R),
            ("l_v", [P, NT, P], F32), ("l_pe", [P, 2, T], F32), ("l_pt", [P, 2, T], F32), ("l_o", [P, NT, P], F32),
            ("l_oT", [P, HP, T], F32)])
        G = arena([
            ("g_amx", [P, NT], F32), ("g_s", [P, NT], F32), ("g_inv", [P, NT], F32), ("g_ig", [P, NT], F32), ("g_iu", [P, NT], F32),
            ("g_t", [P, 2, D], F32), ("g_xq", [P, NT, D], BF16), ("g_xT", [P, DC, T], BF16),
            ("g_g", [P, 2, FF], F32), ("g_h", [P, 2, FF], F32), ("g_r", [P, 2, FF], F32), ("g_hq", [P, 2, FF], BF16),
            ("g_hT", [P, 2, FF], BF16), ("g_hm", [P, 2], F32), ("g_hs", [P, 2], F32), ("g_hi", [P, 2], F32)])
        print("left", nc.sbuf_bytes_remaining, base_names)

        s_w = sem("s_w")
        s_gc = sem("s_gc")
        s_sa = sem("s_sa")
        s_sv = sem("s_sv")
        s_sp = sem("s_sp")
        s_xin = sem("s_xin")
        s_ctx = sem("s_ctx")
        s_xu = sem("s_xu")
        s_xb = sem("s_xb")
        s_out = sem("s_out")
        s_xn = sem("s_xn")
        s_tr = sem("s_tr")
        s_hi = sem("s_hi")
        s_lo = sem("s_lo")

        def mm3(pe, o, lh, ll, rh, rl, start, stop):
            pe.matmul(o, lh, rh, start=start, stop=False)
            pe.matmul(o, lh, rl, start=False, stop=False)
            return pe.matmul(o, ll, rh, start=False, stop=stop)

        def f32(ap):
            return ap.bitcast(F32)

        def rsqrt(v, dst, src):
            t1 = nt1[:, 0:src.shape[-1]]
            v.drain()
            v.tensor_scalar(dst.bitcast(I32), src.bitcast(I32), 1, None, ALU.logical_shift_right)
            v.drain()
            v.tensor_scalar(dst.bitcast(I32), dst.bitcast(I32), -1.0, 1597463007.0, ALU.mult, ALU.add)
            for _ in range(3):
                v.drain()
                v.tensor_tensor(t1, dst, dst, ALU.mult)
                v.drain()
                v.scalar_tensor_tensor(out=t1, in0=t1, scalar=-0.5, in1=src, op0=ALU.mult, op1=ALU.mult)
                v.drain()
                v.scalar_tensor_tensor(out=dst, in0=t1, scalar=1.5, in1=dst, op0=ALU.add, op1=ALU.mult)
            v.drain()

        NG = NT // 2

        def ln_v(v, b, n, src):
            for t in range(NT):
                if n == 0:
                    if t == 0:
                        v.wait_ge(s_xin, b * 16 + 16)
                else:
                    v.wait_ge(s_xu, b * (NPH * NT) + (n - 1) * NT + t + 1)
                v.bn_stats(st[:, t, :], src[:, t, :])
            v.drain()
            for t in range(NT):
                v.bn_aggr(ag[:, t, :], st[:, t, :])
            v.drain()
            v.tensor_scalar(nv[:], ag[:, :, 1], EPS, None, ALU.add)
            rsqrt(v, rsd[:], nv[:])
            for t in range(NT):
                v.tensor_scalar(xn[:, t, :], src[:, t, :], ag[:, t, 0:1], rsd[:, t:t + 1],
                                ALU.subtract, ALU.mult).then_inc(s_xn, 1)

        NTR = NPH - 1

        def ln_pe(pe, b, n):
            if n == 0:
                pe.wait_ge(s_xu, b * (NPH * NT))
            for g in range(NG):
                pe.wait_ge(s_xn, b * (NPH * NT) + n * NT + 2 * g + 2)
                if g >= 2:
                    pe.wait_ge(s_lo, b * (NTR * NG) + n * NG + g - 1)
                bank = ps[:, 6 + g % 2, :]
                for c in range(DC):
                    for t in range(2):
                        o = bank[:, c * 256 + t * P:c * 256 + (t + 1) * P]
                        last = pe.transpose(o, xn[:, 2 * g + t, c * P:(c + 1) * P], idf[:])
                last.then_inc(s_tr, 1)

        def ln_group(g):
            bank = ps[:, 6 + g % 2, :].rearrange("p (c t) -> p c t", c=DC)
            cols = slice(g * 256, (g + 1) * 256)
            return bank, cols

        def ln_a(s, b, n):
            for g in range(NG):
                bank, cols = ln_group(g)
                s.wait_ge(s_tr, b * (NTR * NG) + n * NG + g + 1)
                s.copy(xTh[:, :, cols], bank).then_inc(s_hi, 1)

        def ln_lo(v, b, n):
            for g in range(NG):
                bank, cols = ln_group(g)
                v.wait_ge(s_hi, b * (NTR * NG) + n * NG + g + 1)
                v.tensor_tensor(xTl[:, :, cols], bank, f32(xTh[:, :, cols]), ALU.subtract).then_inc(s_lo, 1)

        def ln_done(b, n):
            return b * (NTR * NG) + n * NG + NG

        class Attention:
            def __init__(self, name, width, probs, probsT, free):
                self.w = width
                self.pe_, self.pt_ = probs, probsT
                self.free = free
                self.s = {k: sem(f"{name}_{k}") for k in ("score", "soft", "max", "exp", "tp", "eva", "evv", "pv", "o", "rc")}

        def blocks(heads):
            return [(h, i) for h in range(heads) for i in range(NT - 1, -1, -1)]

        def banks_of(k):
            return ps[:, 2 * (k % 2):2 * (k % 2) + 2, :].rearrange("p a b -> p (a b)")

        def pieces(i):
            n = i + 1
            return [(j0, min(n, j0 + 4), (j0 // 4 + i) % 2 == 0) for j0 in range(0, n, 4)]

        def count_pieces(bl, upto):
            act = sum(1 for _, i in bl[:upto] for p_ in pieces(i) if p_[2])
            vec = sum(1 for _, i in bl[:upto] for p_ in pieces(i) if not p_[2])
            return act, vec

        def att_pe(pe, at, bl, base, q, k1, k2, val, ocol, extra=None, extra_at=-1):
            n_bl = len(bl)
            n_act, n_vec = count_pieces(bl, n_bl)

            def score(k):
                h, i = bl[k]
                n = (i + 1) * P
                if k >= 2:
                    pe.wait_ge(at.s[at.free], base * n_bl + k - 1)
                s = banks_of(k)
                for c0 in range(0, n, HALF):
                    c1 = min(n, c0 + HALF)
                    lhs = q(h)[:, i * P:(i + 1) * P]
                    pe.matmul(s[:, c0:c1], lhs, k1(h)[:, c0:c1], start=True, stop=False)
                    last = pe.matmul(s[:, c0:c1], lhs, k2(h)[:, c0:c1], start=False, stop=c1 < n)
                last = pe.matmul(s[:, n - P:n], idb[:], causal[:], start=False, stop=True)
                last.then_inc(at.s["score"], 1)

            def turn(k):
                h, i = bl[k]
                pe.wait_ge(at.s["exp"], base * n_bl + k + 1)
                a0, v0 = count_pieces(bl, k)
                if k >= 1:
                    if a0:
                        pe.wait_ge(at.s["eva"], base * n_act + a0)
                    if v0:
                        pe.wait_ge(at.s["evv"], base * n_vec + v0)
                for j in range(i + 1):
                    o = ps[:, 4 + j // 4, (j % 4) * P:(j % 4 + 1) * P]
                    last = pe.transpose(o, at.pe_[:, k % 2, j * P:(j + 1) * P], idf[:])
                last.then_inc(at.s["tp"], 1)

            def pv(k):
                h, i = bl[k]
                a1, v1 = count_pieces(bl, k + 1)
                if a1:
                    pe.wait_ge(at.s["eva"], base * n_act + a1)
                if v1:
                    pe.wait_ge(at.s["evv"], base * n_vec + v1)
                if k >= 2:
                    pe.wait_ge(at.s["o"], base * n_bl + k - 1)
                o = ps[:, 6 + k % 2, 0:at.w]
                for j in range(i + 1):
                    last = pe.matmul(o, at.pt_[:, k % 2, j * P:(j + 1) * P], val(h, j), start=j == 0, stop=j == i)
                last.then_inc(at.s["pv"], 1)

            score(0)
            score(1)
            if extra is not None:
                extra()
            for k in range(n_bl):
                turn(k)
                if k + 2 < n_bl:
                    score(k + 2)
                pv(k)

        def att_a(s, at, bl, base, src):
            n_bl = len(bl)
            n_act, n_vec = count_pieces(bl, n_bl)

            def exp(k):
                h, i = bl[k]
                n = (i + 1) * P
                s.wait_ge(at.s["max"], base * n_bl + k + 1)
                if k >= 2:
                    s.wait_ge(at.s["tp"], base * n_bl + k - 1)
                    s.wait_ge(at.s["rc"], base * n_bl + k - 1)
                ins = s.activation(at.pe_[:, k % 2, 0:n], src(k)[:, 0:n], ACT.Exp, bias=nmax[:, k % 2:k % 2 + 1],
                                   accum_out=sums[:, k % 2:k % 2 + 1])
                ins.then_inc(at.s["exp"], 1)

            def copy_out(k):
                for j0, j1, mine in pieces(bl[k][1]):
                    if mine:
                        s.wait_ge(at.s["tp"], base * n_bl + k + 1)
                        if k >= 2:
                            s.wait_ge(at.s["pv"], base * n_bl + k - 1)
                        s.copy(at.pt_[:, k % 2, j0 * P:j1 * P], ps[:, 4 + j0 // 4, 0:(j1 - j0) * P]).then_inc(at.s["eva"], 1)

            exp(0)
            if n_bl > 1:
                exp(1)
            for k in range(n_bl):
                copy_out(k)
                if k + 2 < n_bl:
                    exp(k + 2)

        def att_v(v, at, bl, base, scale_rows, finish, soft_on_max):
            n_bl = len(bl)

            def maximum(k):
                h, i = bl[k]
                n = (i + 1) * P
                v.wait_ge(at.s["score"], base * n_bl + k + 1)
                if k >= 2:
                    v.wait_ge(at.s["exp"], base * n_bl + k - 1)
                src = scale_rows(k, i, n)
                v.tensor_reduce(nmax[:, k % 2:k % 2 + 1], src, AX.X, ALU.max, negate=True).then_inc(at.s["max"], 1)

            def copy_out(k):
                for j0, j1, mine in pieces(bl[k][1]):
                    if not mine:
                        v.wait_ge(at.s["tp"], base * n_bl + k + 1)
                        if k >= 2:
                            v.wait_ge(at.s["pv"], base * n_bl + k - 1)
                        v.tensor_copy(at.pt_[:, k % 2, j0 * P:j1 * P], ps[:, 4 + j0 // 4, 0:(j1 - j0) * P]).then_inc(at.s["evv"], 1)

            def out_(k):
                v.wait_ge(at.s["exp"], base * n_bl + k + 1)
                v.reciprocal(rec[:, k % 2:k % 2 + 1], sums[:, k % 2:k % 2 + 1]).then_inc(at.s["rc"], 1)
                v.wait_ge(at.s["rc"], base * n_bl + k + 1)
                v.wait_ge(at.s["pv"], base * n_bl + k + 1)
                finish(k, bl[k][0], bl[k][1], ps[:, 6 + k % 2, 0:at.w], rec[:, k % 2:k % 2 + 1]).then_inc(at.s["o"], 1)

            maximum(0)
            if n_bl > 1:
                maximum(1)
            for k in range(n_bl):
                copy_out(k)
                if k + 2 < n_bl:
                    maximum(k + 2)
                out_(k)

        a_sem = {k: sem(f"a_{k}") for k in
                 ("sh", "shv", "q", "shn", "st", "sth", "stl", "pr", "u", "ab", "sin", "ph", "y", "ya", "v", "va", "phi", "phd",
                  "pt", "k1", "k2", "qs", "drop")}
        AT0 = Attention("at0", D, A["a_pe"], A["a_pt"], "soft")
        bl0 = blocks(1)

        def a_pe(pe, b):
            pe.wait_ge(s_lo, ln_done(b, 0))
            for g in range(2):
                for t in range(4):
                    tok = slice((4 * g + t) * P, (4 * g + t + 1) * P)
                    o = ps[:, g, t * 66:(t + 1) * 66]
                    for c in range(DC):
                        last = mm3(pe, o, xTh[:, c, tok], xTl[:, c, tok], wsh_h[:, c, :], wsh_l[:, c, :], c == 0, c == DC - 1)
                last.then_inc(a_sem["sh"], 1)
            for g in range(4):
                if g >= 2:
                    pe.wait_ge(a_sem["va"], b * 4 + g - 1)
                for t in range(2):
                    tok = slice((2 * g + t) * P, (2 * g + t + 1) * P)
                    o = ps[:, 2 + g % 2, t * D:(t + 1) * D]
                    for c in range(DC):
                        last = mm3(pe, o, xTh[:, c, tok], xTl[:, c, tok], wvo_h[:, c, :], wvo_l[:, c, :], c == 0, c == DC - 1)
                last.then_inc(a_sem["v"], 1)
            pe.wait_ge(a_sem["shn"], b + 1)
            for g in range(2):
                for t in range(4):
                    last = pe.transpose(ps[:, 4 + g, t * P:(t + 1) * P], A["a_shn"][:, 4 * g + t, :], idf[:])
                last.then_inc(a_sem["st"], 1)
            pe.wait_ge(a_sem["stl"], b * 2 + 2)
            for g in range(2):
                cols = slice(g * HALF, (g + 1) * HALF)
                last = mm3(pe, ps[:, g, :], om_h[:], om_l[:], A["a_shTh"][:, cols], A["a_shTl"][:, cols], True, True)
                last.then_inc(a_sem["pr"], 1)
            pe.wait_ge(a_sem["ph"], b + 1)
            pe.wait_ge(a_sem["va"], b * 4 + 4)
            for t in range(NT):
                tok = slice(t * P, (t + 1) * P)
                if t >= 2:
                    pe.wait_ge(a_sem["ya"], b * NT + t - 1)
                last = mm3(pe, ps[:, 2 + t % 2, 0:ORDERS * COMB], A["a_phh"][:, tok], A["a_phl"][:, tok], wc_h[:], wc_l[:], True, True)
                last.then_inc(a_sem["y"], 1)
            pe.wait_ge(a_sem["phd"], b + 1)
            for g in range(2):
                for t in range(4):
                    last = pe.transpose(ps[:, 4 + g, t * P:(t + 1) * P], A["a_phi"][:, 4 * g + t, :], idf[:])
                last.then_inc(a_sem["pt"], 1)
            pe.wait_ge(a_sem["qs"], b * 2 + 2)
            att_pe(pe, AT0, bl0, b, lambda h: A["a_qs"], lambda h: A["a_k1"], lambda h: A["a_k2"],
                   lambda h, j: A["a_v"][:, j, :], None)

        def a_a(s, b):
            for g in range(4):
                s.wait_ge(a_sem["v"], b * 4 + g + 1)
                s.copy(A["a_v"][:, 2 * g:2 * g + 2, :].rearrange("p t d -> p (t d)"), ps[:, 2 + g % 2, :]).then_inc(a_sem["va"], 1)
            s.wait_ge(a_sem["shv"], b * 2 + 2)
            s.activation(A["a_q"][:], A["a_sh"][:, :, 64], ACT.Tanh).then_inc(a_sem["q"], 1)
            for g in range(2):
                s.wait_ge(a_sem["st"], b * 2 + g + 1)
                s.copy(A["a_shTh"][:, g * HALF:(g + 1) * HALF], ps[0:SHELL, 4 + g, :]).then_inc(a_sem["sth"], 1)
            s.wait_ge(a_sem["u"], b + 1)
            s.activation(A["a_r"][0:RFF, :], A["a_r"][0:RFF, :], ACT.Abs).then_inc(a_sem["ab"], 1)
            s.wait_ge(a_sem["ab"], b + 1)
            s.activation(A["a_phs"][:], A["a_r"][:], ACT.Sin, bias=cosb[:], scale=coss[:]).then_inc(a_sem["sin"], 1)
            s.wait_ge(a_sem["sin"], b + 1)
            s.copy(A["a_phh"][:], A["a_phs"][:]).then_inc(a_sem["drop"], 1)
            for t in range(NT):
                s.wait_ge(a_sem["y"], b * NT + t + 1)
                s.copy(A["a_y"][:, t, :], ps[:, 2 + t % 2, 0:ORDERS * COMB]).then_inc(a_sem["ya"], 1)
            for g in range(2):
                cols = slice(g * HALF, (g + 1) * HALF)
                s.wait_ge(a_sem["pt"], b * 2 + g + 1)
                s.copy(A["a_k1"][:, cols], ps[:, 4 + g, :]).then_inc(a_sem["k1"], 1)
            s.wait_ge(a_sem["k1"], b * 2 + 2)
            s.copy(A["a_qs"][0:64, :], f32(A["a_k1"][0:64, :])).then_inc(a_sem["qs"], 1)
            att_a(s, AT0, bl0, b, lambda k: A["a_sm"][:, k % 2, :])

        def a_v(v, b):
            for g in range(2):
                v.wait_ge(a_sem["sh"], b * 2 + g + 1)
                v.tensor_tensor(A["a_sh"][:, 4 * g:4 * g + 4, :], ps[:, g, 0:4 * 66].rearrange("p (t n) -> p t n", t=4),
                                bsh[:].unsqueeze(1).to_broadcast([P, 4, 66]), ALU.add).then_inc(a_sem["shv"], 1)
            v.drain()
            v.tensor_tensor(A["a_sq"][:], A["a_sh"][:, :, 0:SHELL], A["a_sh"][:, :, 0:SHELL], ALU.mult)
            v.drain()
            v.tensor_reduce(A["a_ss"][:], A["a_sq"][:], AX.X, ALU.add)
            v.drain()
            v.tensor_scalar(A["a_ss"][:], A["a_ss"][:], 1e-24, None, ALU.max)
            rsqrt(v, A["a_rn"][:], A["a_ss"][:])
            for o in (slice(0, SHELL), slice(SHELL, P)):
                last = v.tensor_tensor(A["a_shn"][:, :, o], A["a_sh"][:, :, 0:SHELL],
                                       A["a_rn"][:].unsqueeze(2).to_broadcast([P, NT, SHELL]), ALU.mult)
            last.then_inc(a_sem["shn"], 1)
            for g in range(2):
                cols = slice(g * HALF, (g + 1) * HALF)
                v.wait_ge(a_sem["sth"], b * 2 + g + 1)
                v.tensor_tensor(A["a_shTl"][:, cols], ps[0:SHELL, 4 + g, :], f32(A["a_shTh"][:, cols]),
                                ALU.subtract).then_inc(a_sem["stl"], 1)
            for g in range(2):
                v.wait_ge(a_sem["pr"], b * 2 + g + 1)
                v.tensor_scalar(A["a_p"][:, g * HALF:(g + 1) * HALF], ps[0:SHELL, g, :], rbias[:, 0:1], None, ALU.add)
            v.drain()
            v.tensor_scalar(A["a_k"][:], A["a_p"][:], 1.0 / (2.0 * math.pi), MAGIC, ALU.mult, ALU.add)
            v.drain()
            v.tensor_scalar(A["a_k"][:], A["a_k"][:], MAGIC, None, ALU.subtract)
            v.drain()
            v.scalar_tensor_tensor(out=A["a_p"][:], in0=A["a_k"][:], scalar=-TWO_PI_HI, in1=A["a_p"][:], op0=ALU.mult, op1=ALU.add)
            v.drain()
            v.scalar_tensor_tensor(out=A["a_p"][:], in0=A["a_k"][:], scalar=-TWO_PI_LO, in1=A["a_p"][:], op0=ALU.mult, op1=ALU.add)
            v.drain()
            v.tensor_scalar(A["a_r"][:], A["a_p"][:], -PI_BELOW, PI_BELOW, ALU.max, ALU.min).then_inc(a_sem["u"], 1)
            v.wait_ge(a_sem["drop"], b + 1)
            v.tensor_tensor(A["a_phl"][:], A["a_phs"][:], f32(A["a_phh"][:]), ALU.subtract).then_inc(a_sem["ph"], 1)
            v.wait_ge(a_sem["q"], b + 1)
            for m in range(ORDERS - 2, -1, -1):
                for t in range(NT):
                    if m == ORDERS - 2:
                        v.wait_ge(a_sem["ya"], b * NT + t + 1)
                    src = A["a_y"][:, t, (m + 1) * COMB:(m + 2) * COMB] if m == ORDERS - 2 else A["a_acc"][:, t, :]
                    dst = A["a_phi"][:, t, 0:COMB] if m == 0 else A["a_acc"][:, t, :]
                    v.scalar_tensor_tensor(out=dst, in0=src, scalar=A["a_q"][:, t:t + 1],
                                           in1=A["a_y"][:, t, m * COMB:(m + 1) * COMB], op0=ALU.mult, op1=ALU.add)
                v.drain()
            v.tensor_copy(A["a_phi"][:, :, COMB:2 * COMB], A["a_phi"][:, :, 0:COMB]).then_inc(a_sem["phd"], 1)
            for g in range(2):
                cols = slice(g * HALF, (g + 1) * HALF)
                v.wait_ge(a_sem["k1"], b * 2 + g + 1)
                v.tensor_tensor(A["a_k2"][:, cols], ps[:, 4 + g, :], f32(A["a_k1"][:, cols]), ALU.subtract)
            v.drain()
            v.tensor_copy(A["a_qs"][64:128, :], f32(A["a_k2"][64:128, :])).then_inc(a_sem["qs"], 1)
            v.wait_ge(s_xb, b * 4 + 1)

            def rows_scaled(k, i, n):
                v.tensor_tensor(A["a_sm"][:, k % 2, 0:n], banks_of(k)[:, 0:n], decay[:, T - n:T], ALU.mult).then_inc(AT0.s["soft"], 1)
                v.wait_ge(AT0.s["soft"], b * len(bl0) + k + 1)
                return A["a_sm"][:, k % 2, 0:n]

            def finish(k, h, i, o, r):
                v.scalar_tensor_tensor(out=x[:, i, :], in0=o, scalar=r, in1=x[:, i, :], op0=ALU.mult, op1=ALU.add).then_inc(s_xu, 1)
                return v.engine_nop() if False else v.drain()

            att_v(v, AT0, bl0, b, rows_scaled, finish, False)

        class Cross:
            def __init__(self, name, n, heads, hd):
                self.n, self.h, self.hd = n, heads, hd
                self.hpc = P // hd
                self.nc_ = heads // self.hpc
                self.W = heads * CK
                self.nb = self.W // HALF
                self.pairs = heads // 2
                self.s = {k: sem(f"{name}_{k}") for k in
                          ("kv", "kvT", "bd", "m", "mh", "ml", "u", "uh", "ul", "br", "bh", "b2",
                           "sc", "mx", "sm", "ex", "su", "pn", "tp", "th", "tl", "pv")}

        C0 = Cross("x0", 1, XH0, XD0)
        C1 = Cross("x1", 4, XH1, XD1)

        def cross_w(cr):
            if cr is C0:
                return x0_wq, x0_wk, x0_wv, x0_wo, X["c_kB"], X["c_vB"], blk0
            return x1_wq, x1_wk, x1_wv, x1_wo, X["c_kC"], X["c_vC"], blk1

        def x_pe_prep(pe, cr, b):
            wq, wk, wv, wo, kB, vB, _ = cross_w(cr)
            q = cr.s
            pe.wait_ge(s_ctx, b * 48 + 48)
            pe.wait_ge(s_xu, b * (NPH * NT) + cr.n * NT)
            for j, w in enumerate((wk, wv)):
                for c in range(cr.nc_):
                    o = ps[:, j, c * CK:(c + 1) * CK]
                    pe.matmul(o, w[:, 0, c * P:(c + 1) * P], ctxT[:, 0, :], start=True, stop=False)
                    last = pe.matmul(o, w[0:64, 1, c * P:(c + 1) * P], ctxT[0:64, 1, :], start=False, stop=True)
            last.then_inc(q["kv"], 1)
            pe.wait_ge(q["bd"], b * 2 + 2)
            cw = cr.hpc * CK
            for dc in range(DC):
                for c in range(cr.nc_):
                    col = c * cw
                    o = ps[:, 2 + dc * cr.nb + col // HALF, col % HALF:col % HALF + cw]
                    last = pe.matmul(o, wq[:, c, dc * P:(dc + 1) * P], kB[:, c, 0:cw], start=True, stop=True)
            last.then_inc(q["m"], 1)
            if cr is C1:
                for c in range(2):
                    last = pe.matmul(ps[:, c, :], x1_bqb[:, c, :], kB[:, c, 0:cw], start=True, stop=True)
                last.then_inc(q["br"], 1)
            pe.wait_ge(q["ml"], b + 1)
            for g in range(cr.pairs // 2):
                for j in (2 * g, 2 * g + 1):
                    c, off = (2 * j) // cr.hpc, ((2 * j) % cr.hpc) * CK
                    o = ps[:, 2 + g, (j % 2) * D:(j % 2 + 1) * D]
                    last = pe.matmul(o, vB[:, c, off:off + P], wo[:, c, :], start=True, stop=True)
            last.then_inc(q["u"], 1)

        def x_a_prep(s, cr, b):
            q = cr.s
            sc = float(cr.hd) ** -0.5
            s.wait_ge(q["m"], b + 1)
            src = ps[:, 2:2 + DC * cr.nb, :].rearrange("p (c n) w -> p c (n w)", c=DC)
            s.activation(X["c_mh"][:, :, 0:cr.W], src, ACT.Copy, scale=sc).then_inc(q["mh"], 1)
            if cr is C1:
                s.wait_ge(q["br"], b + 1)
                s.activation(X["c_bh"][:], ps[:, 0:2, :].rearrange("p a w -> p (a w)"), ACT.Copy, scale=sc).then_inc(q["bh"], 1)
            s.wait_ge(q["u"], b + 1)
            nu = cr.pairs // 2
            s.copy(X["c_uh"][:, 0:cr.pairs, :].rearrange("p (g j) d -> p g (j d)", j=2), ps[:, 2:2 + nu, :]).then_inc(q["uh"], 1)

        def x_v_prep(v, cr, b):
            _, _, _, _, kB, vB, blk = cross_w(cr)
            q = cr.s
            sc = float(cr.hd) ** -0.5
            kT, vT = X["c_kT"][:, 0:cr.nc_, :], X["c_vT"][:, 0:cr.nc_, :]
            v.wait_ge(q["kv"], b + 1)
            pk = ps[:, 0, 0:cr.nc_ * CK].rearrange("p (c k) -> p c k", k=CK)
            pvv = ps[:, 1, 0:cr.nc_ * CK].rearrange("p (c k) -> p c k", k=CK)
            if cr is C1:
                for c in range(2):
                    v.tensor_scalar(kT[:, c, :], pk[:, c, :], x1_bk[:, c:c + 1], None, ALU.add)
                    v.tensor_scalar(vT[:, c, :], pvv[:, c, :], x1_bv[:, c:c + 1], None, ALU.add)
            else:
                v.tensor_copy(kT, pk)
                v.tensor_copy(vT, pvv)
            v.drain()
            for src, dst in ((kT, kB), (vT, vB)):
                for c in range(cr.nc_):
                    o = dst[:, c, 0:cr.hpc * CK].rearrange("p (h k) -> p h k", k=CK)
                    last = v.tensor_tensor(o, src[:, c, :].unsqueeze(1).to_broadcast([P, cr.hpc, CK]),
                                           blk[:].unsqueeze(2).to_broadcast([P, cr.hpc, CK]), ALU.mult)
                last.then_inc(q["bd"], 1)
            v.wait_ge(q["mh"], b + 1)
            for dc in range(DC):
                src = ps[:, 2 + dc * cr.nb:2 + (dc + 1) * cr.nb, :].rearrange("p n w -> p (n w)")
                last = v.scalar_tensor_tensor(out=X["c_ml"][:, dc, 0:cr.W], in0=src, scalar=sc, in1=f32(X["c_mh"][:, dc, 0:cr.W]),
                                              op0=ALU.mult, op1=ALU.subtract)
            last.then_inc(q["ml"], 1)
            if cr is C1:
                v.wait_ge(q["bh"], b + 1)
                v.scalar_tensor_tensor(out=X["c_bl"][:], in0=ps[:, 0:2, :].rearrange("p a w -> p (a w)"), scalar=sc,
                                       in1=f32(X["c_bh"][:]), op0=ALU.mult, op1=ALU.subtract)
                v.drain()
                v.tensor_scalar(X["c_bl"][:], X["c_bl"][:], row01[:, 1:2], None, ALU.mult)
                v.drain()
                v.scalar_tensor_tensor(out=X["c_b2"][:], in0=f32(X["c_bh"][:]), scalar=row01[:, 0:1], in1=X["c_bl"][:],
                                       op0=ALU.mult, op1=ALU.add).then_inc(q["b2"], 1)
            else:
                v.wait_ge(s_ctx, b * 48 + 48)
                v.tensor_scalar(mrow[:].rearrange("p (h k) -> p h k", k=CK), mrow4[:].bitcast(U8).unsqueeze(1).to_broadcast([1, XH0, CK]),
                                -MASKED, MASKED, ALU.mult, ALU.add).then_inc(q["b2"], 1)
            v.wait_ge(q["uh"], b + 1)
            nu = cr.pairs // 2
            v.tensor_tensor(X["c_ul"][:, 0:cr.pairs, :].rearrange("p (g j) d -> p g (j d)", j=2), ps[:, 2:2 + nu, :],
                            f32(X["c_uh"][:, 0:cr.pairs, :]).rearrange("p (g j) d -> p g (j d)", j=2), ALU.subtract).then_inc(q["ul"], 1)

        def x_banks(cr, t):
            return ps[:, cr.nb * (t % 2):cr.nb * (t % 2) + cr.nb, :].rearrange("p a w -> p (a w)")

        def x_pe(pe, cr, b):
            q = cr.s
            pe.wait_ge(s_lo, ln_done(b, cr.n))
            pe.wait_ge(q["ul"], b + 1)
            pe.wait_ge(q["b2"], b + 1)

            def score(t):
                tok = slice(t * P, (t + 1) * P)
                if t >= 2:
                    pe.wait_ge(q["sm"], b * NT + t - 1)
                for n in range(cr.nb):
                    cols = slice(n * HALF, (n + 1) * HALF)
                    o = x_banks(cr, t)[:, cols]
                    for c in range(DC):
                        mm3(pe, o, xTh[:, c, tok], xTl[:, c, tok], X["c_mh"][:, c, cols], X["c_ml"][:, c, cols], c == 0, False)
                    if cr is C1:
                        last = pe.matmul(o, ones_r[0:2, :], X["c_b2"][0:2, cols], start=False, stop=True)
                    else:
                        last = pe.matmul(o, ones_b[:], mrow[:], start=False, stop=True)
                last.then_inc(q["sc"], 1)

            def turn(t):
                pe.wait_ge(q["pn"], b * NT + t + 1)
                if t >= 1:
                    pe.wait_ge(q["tl"], b * NT + t)
                for j in range(cr.pairs):
                    last = pe.transpose(ps[:, 4 + j // 4, (j % 4) * P:(j % 4 + 1) * P], X["c_pn"][:, t % 2, j * P:(j + 1) * P], idf[:])
                last.then_inc(q["tp"], 1)

            def pv(t):
                pe.wait_ge(q["tl"], b * NT + t + 1)
                if t >= 2:
                    pe.wait_ge(s_xu, b * (NPH * NT) + cr.n * NT + t - 1)
                o = ps[:, 6 + t % 2, 0:D]
                for j in range(cr.pairs):
                    cols = slice(j * P, (j + 1) * P)
                    last = mm3(pe, o, X["c_th"][:, t % 2, cols], X["c_tl"][:, t % 2, cols], X["c_uh"][:, j, :], X["c_ul"][:, j, :],
                               j == 0, j == cr.pairs - 1)
                last.then_inc(q["pv"], 1)

            score(0)
            score(1)
            for t in range(NT):
                turn(t)
                if t + 2 < NT:
                    score(t + 2)
                pv(t)

        def x_a(s, cr, b):
            q = cr.s
            nb4 = cr.pairs // 4

            def exp(t):
                s.wait_ge(q["sm"], b * NT + t + 1)
                if t >= 2:
                    s.wait_ge(q["pn"], b * NT + t - 1)
                s.activation(X["c_pe"][:, t % 2, 0:cr.W], X["c_sm"][:, t % 2, 0:cr.W], ACT.Exp).then_inc(q["ex"], 1)

            exp(0)
            exp(1)
            for t in range(NT):
                s.wait_ge(q["tp"], b * NT + t + 1)
                if t >= 2:
                    s.wait_ge(q["pv"], b * NT + t - 1)
                s.copy(X["c_th"][:, t % 2, 0:cr.W], ps[:, 4:4 + nb4, :].rearrange("p a w -> p (a w)")).then_inc(q["th"], 1)
                if t + 2 < NT:
                    exp(t + 2)

        def x_v(v, cr, b):
            q = cr.s
            nb4 = cr.pairs // 4

            def soft(t):
                v.wait_ge(q["sc"], b * NT + t + 1)
                src = x_banks(cr, t).rearrange("p (h k) -> p h k", k=CK)
                v.tensor_reduce(X["c_mx"][:, t % 2, 0:cr.h], src, AX.X, ALU.max).then_inc(q["mx"], 1)
                v.wait_ge(q["mx"], b * NT + t + 1)
                if t >= 2:
                    v.wait_ge(q["ex"], b * NT + t - 1)
                v.tensor_tensor(X["c_sm"][:, t % 2, 0:cr.W].rearrange("p (h k) -> p h k", k=CK), src,
                                X["c_mx"][:, t % 2, 0:cr.h].unsqueeze(2).to_broadcast([P, cr.h, CK]), ALU.subtract).then_inc(q["sm"], 1)

            def sum_(t):
                v.wait_ge(q["ex"], b * NT + t + 1)
                if t >= 2:
                    v.wait_ge(q["pn"], b * NT + t - 1)
                v.tensor_reduce(X["c_su"][:, t % 2, 0:cr.h], X["c_pe"][:, t % 2, 0:cr.W].rearrange("p (h k) -> p h k", k=CK), AX.X, ALU.add)
                v.drain()
                v.reciprocal(X["c_re"][:, t % 2, 0:cr.h], X["c_su"][:, t % 2, 0:cr.h]).then_inc(q["su"], 1)

            soft(0)
            soft(1)
            sum_(0)
            for t in range(NT):
                if t + 1 < NT:
                    sum_(t + 1)
                v.wait_ge(q["th"], b * NT + t + 1)
                if t >= 2:
                    v.wait_ge(q["pv"], b * NT + t - 1)
                v.tensor_tensor(X["c_tl"][:, t % 2, 0:cr.W], ps[:, 4:4 + nb4, :].rearrange("p a w -> p (a w)"),
                                f32(X["c_th"][:, t % 2, 0:cr.W]), ALU.subtract).then_inc(q["tl"], 1)
                if t + 2 < NT:
                    soft(t + 2)
                if t == 0:
                    v.wait_ge(s_xb, b * 4 + (2 if cr is C0 else 4))
                v.wait_ge(q["pv"], b * NT + t + 1)
                v.tensor_tensor(x[:, t, :], x[:, t, :], ps[:, 6 + t % 2, 0:D], ALU.add).then_inc(s_xu, 1)

        def x_g(g, cr, b, bias):
            q = cr.s
            g.wait_ge(s_xn, b * (NPH * NT) + (cr.n + 1) * NT)
            g.tensor_tensor(x[:], x[:], bias[:].unsqueeze(1).to_broadcast([P, NT, D]), ALU.add).then_inc(s_xb, 1)
            for t in range(NT):
                g.wait_ge(q["su"], b * NT + t + 1)
                if t >= 2:
                    g.wait_ge(q["tp"], b * NT + t - 1)
                g.tensor_tensor(X["c_pn"][:, t % 2, 0:cr.W].rearrange("p (h k) -> p h k", k=CK),
                                X["c_pe"][:, t % 2, 0:cr.W].rearrange("p (h k) -> p h k", k=CK),
                                X["c_re"][:, t % 2, 0:cr.h].unsqueeze(2).to_broadcast([P, cr.h, CK]), ALU.mult).then_inc(q["pn"], 1)

        m_sem = {k: sem(f"m_{k}") for k in
                 ("mean", "meanv", "sc", "idx", "w1", "w2", "w1h", "w1l", "w2h", "w2l", "up", "h", "hh", "hl", "dn", "seen")}

        def m_pe(pe, b):
            pe.wait_ge(s_xn, b * (NPH * NT) + 3 * NT)
            pe.wait_ge(s_xu, b * (NPH * NT) + 2 * NT)
            for c in range(DC):
                for t in range(NT):
                    last = pe.matmul(ps[:, c, 0:1], xn[:, t, c * P:(c + 1) * P], ones_f[:, 0:1], start=t == 0, stop=t == NT - 1)
            last.then_inc(m_sem["mean"], 1)
            pe.wait_ge(m_sem["meanv"], b + 1)
            for c in range(DC):
                last = pe.matmul(ps[0:1, 2, 0:EXPERTS], M["m_mean"][:, c:c + 1], wr[:, c, :], start=c == 0, stop=c == DC - 1)
            last.then_inc(m_sem["sc"], 1)
            ln_pe(pe, b, 2)
            pe.wait_ge(s_lo, ln_done(b, 2))
            pe.wait_ge(m_sem["w1l"], b + 1)
            for hf in range(2):
                cols = slice(hf * HALF, (hf + 1) * HALF)
                for f in range(FC):
                    n = hf * FC + f
                    if n >= 4:
                        pe.wait_ge(m_sem["h"], b * 2 * FC + n - 3)
                    o = ps[:, n % 4, :]
                    fs = slice(f * P, (f + 1) * P)
                    for c in range(DC):
                        last = mm3(pe, o, M["m_w1h"][:, c, fs], M["m_w1l"][:, c, fs], xTh[:, c, cols], xTl[:, c, cols], c == 0, c == DC - 1)
                    last.then_inc(m_sem["up"], 1)
                if hf == 0:
                    pe.wait_ge(m_sem["w2l"], b + 1)
                pe.wait_ge(m_sem["hl"], b * 2 * FC + (hf + 1) * FC)
                for t in range(4):
                    n = hf * 4 + t
                    if n >= 2:
                        pe.wait_ge(s_xu, b * (NPH * NT) + 2 * NT + n - 1)
                    o = ps[:, 4 + n % 2, 0:D]
                    for f in range(FC):
                        tok = slice(t * P, (t + 1) * P)
                        last = mm3(pe, o, M["m_hh"][:, f, tok], M["m_hl"][:, f, tok], M["m_w2h"][:, f, :], M["m_w2l"][:, f, :],
                                   f == 0, f == FC - 1)
                    last.then_inc(m_sem["dn"], 1)

        def m_a(s, b):
            ln_a(s, b, 2)
            s.wait_ge(m_sem["w1"], b * 48 + 48)
            s.copy(M["m_w1h"][:], M["m_w1"][:]).then_inc(m_sem["w1h"], 1)
            s.wait_ge(m_sem["w2"], b * 16 + 16)
            s.copy(M["m_w2h"][:], M["m_w2"][:]).then_inc(m_sem["w2h"], 1)
            for n in range(2 * FC):
                s.wait_ge(m_sem["up"], b * 2 * FC + n + 1)
                if n >= 2:
                    s.wait_ge(m_sem["hl"], b * 2 * FC + n - 1)
                s.activation(M["m_h"][:, n % 2, :], ps[:, n % 4, :], ACT.Relu, bias=M["m_b1"][:, n % FC:n % FC + 1]).then_inc(m_sem["h"], 1)

        def m_v(v, b):
            v.wait_ge(m_sem["mean"], b + 1)
            v.tensor_scalar(M["m_mean"][:], ps[:, 0:2, 0], 1.0 / T, None, ALU.mult).then_inc(m_sem["meanv"], 1)
            v.wait_ge(m_sem["sc"], b + 1)
            v.tensor_tensor(M["m_sc"][:], ps[0:1, 2, 0:EXPERTS], br[:], ALU.add)
            v.drain()
            v.max(M["m_top"][:], M["m_sc"][:])
            v.drain()
            v.max_index(M["m_idx"][:], M["m_top"][:], M["m_sc"][:]).then_inc(m_sem["idx"], 1)
            ln_lo(v, b, 2)
            v.wait_ge(m_sem["w1h"], b + 1)
            v.tensor_tensor(M["m_w1l"][:], M["m_w1"][:], f32(M["m_w1h"][:]), ALU.subtract).then_inc(m_sem["w1l"], 1)
            v.wait_ge(m_sem["w2h"], b + 1)
            v.tensor_tensor(M["m_w2l"][:], M["m_w2"][:], f32(M["m_w2h"][:]), ALU.subtract).then_inc(m_sem["w2l"], 1)
            v.wait_ge(s_xb, b * 4 + 3)
            for n in range(2 * FC):
                v.wait_ge(m_sem["h"], b * 2 * FC + n + 1)
                if n == FC:
                    v.wait_ge(m_sem["dn"], b * NT + 4)
                v.tensor_copy(M["m_hh"][:, n % FC, :], M["m_h"][:, n % 2, :]).then_inc(m_sem["hh"], 1)
                v.wait_ge(m_sem["hh"], b * 2 * FC + n + 1)
                v.tensor_tensor(M["m_hl"][:, n % FC, :], M["m_h"][:, n % 2, :], f32(M["m_hh"][:, n % FC, :]), ALU.subtract).then_inc(m_sem["hl"], 1)
                if n % FC == FC - 1:
                    for t in range(4):
                        k = n // FC * 4 + t
                        v.wait_ge(m_sem["dn"], b * NT + k + 1)
                        v.tensor_tensor(x[:, k, :], x[:, k, :], ps[:, 4 + k % 2, 0:D], ALU.add).then_inc(s_xu, 1)

        def m_g(g, b):
            g.wait_ge(s_xn, b * (NPH * NT) + 3 * NT)
            g.wait_ge(m_sem["w1"], b * 48 + 48)
            g.tensor_tensor(x[:], x[:], M["m_b2"][:].unsqueeze(1).to_broadcast([P, NT, D]), ALU.add).then_inc(s_xb, 1)

        def m_sp(sp, b):
            sp.wait_ge(m_sem["idx"], b + 1)
            sp.sem_inc(m_sem["seen"], 1)
            e = sp.value_load(M["m_idx"][0:1, 0:1], min_val=0, max_val=EXPERTS - 1)
            sp.dma_start(M["m_w1"][:], a["m_w1"][bass.ds(e, 1)].rearrange("o (c p) f -> p (o c) f", p=P)).then_inc(m_sem["w1"], 16)
            sp.dma_start(M["m_b1"][:], a["m_b1"][bass.ds(e, 1)].rearrange("o p f -> p (o f)")).then_inc(m_sem["w1"], 16)
            sp.dma_start(M["m_b2"][:], a["m_b2"][bass.ds(e, 1)].to_broadcast([P, D])).then_inc(m_sem["w1"], 16)
            sp.dma_start(M["m_w2"][:], a["m_w2"][bass.ds(e, 1)].rearrange("o (c p) f -> p (o c) f", p=P)).then_inc(m_sem["w2"], 16)

        AT1 = Attention("at1", SD, L["l_pe"], L["l_pt"], "exp")
        bl1 = blocks(2)
        l_sem = {k: sem(f"l_{k}") for k in ("w", "wh", "wl", "qk", "hi", "lo", "v", "va", "ot", "oh", "wo")}
        LQ = [L["l_q0"], L["l_q1"]]
        LK1 = [L["l_k10"], L["l_k11"]]
        LK2 = [L["l_k20"], L["l_k21"]]

        def l_pe_body(pe, it):
            pe.wait_ge(l_sem["wl"], it + 1)
            for m in range(2):
                for hf in range(2):
                    cols = slice(hf * HALF, (hf + 1) * HALF)
                    for c in range(DC):
                        last = mm3(pe, ps[:, 2 * m + hf, :], L["l_wh"][:, m, c, :], L["l_wl"][:, m, c, :], xTh[:, c, cols], xTl[:, c, cols],
                                   c == 0, c == DC - 1)
                last.then_inc(l_sem["qk"], 1)

            def values():
                for g in range(2):
                    for t in range(4):
                        tok = slice((4 * g + t) * P, (4 * g + t + 1) * P)
                        for c in range(DC):
                            last = mm3(pe, ps[:, 4 + g, t * P:(t + 1) * P], xTh[:, c, tok], xTl[:, c, tok], L["l_wh"][:, 2, c, :],
                                       L["l_wl"][:, 2, c, :], c == 0, c == DC - 1)
                    last.then_inc(l_sem["v"], 1)
                pe.wait_ge(l_sem["va"], it * 2 + 2)

            pe.wait_ge(l_sem["lo"], it * 6 + 6)
            att_pe(pe, AT1, bl1, it, lambda h: LQ[h], lambda h: LK1[h], lambda h: LK2[h],
                   lambda h, j: L["l_v"][:, j, h * SD:(h + 1) * SD], None, extra=values)
            pe.wait_ge(AT1.s["o"], (it + 1) * len(bl1))
            for g in range(2):
                for t in range(4):
                    last = pe.transpose(ps[:, 4 + g, t * P:(t + 1) * P], L["l_o"][:, 4 * g + t, :], idf[:])
                last.then_inc(l_sem["ot"], 1)
            pe.wait_ge(l_sem["oh"], it * 2 + 2)

        def l_a_body(s, it, hp):
            s.wait_ge(l_sem["w"], it * 16 + 16)
            s.copy(L["l_wh"][:], L["l_w"][:]).then_inc(l_sem["wh"], 1)
            for m in range(2):
                src = ps[:, 2 * m:2 * m + 2, :].rearrange("p a w -> p (a w)")
                s.wait_ge(l_sem["qk"], it * 2 + m + 1)
                for h in range(2):
                    hr = src[h * SD:(h + 1) * SD, :]
                    if m == 0:
                        s.activation(LQ[h][0:64, :], hr, ACT.Copy, scale=0.125).then_inc(l_sem["hi"], 1)
                    else:
                        s.copy(LK1[h][0:64, :], hr).then_inc(l_sem["hi"], 1)
                        s.copy(LK1[h][64:128, :], hr).then_inc(l_sem["hi"], 1)
            for g in range(2):
                s.wait_ge(l_sem["v"], it * 2 + g + 1)
                s.copy(L["l_v"][:, 4 * g:4 * g + 4, :].rearrange("p t d -> p (t d)"), ps[:, 4 + g, :]).then_inc(l_sem["va"], 1)
            att_a(s, AT1, bl1, it, lambda k: banks_of(k))
            for g in range(2):
                s.wait_ge(l_sem["ot"], it * 2 + g + 1)
                s.copy(L["l_oT"][:, bass.ds(hp, 1), g * HALF:(g + 1) * HALF].rearrange("p o w -> p (o w)"),
                       ps[:, 4 + g, :]).then_inc(l_sem["oh"], 1)

        def l_v_body(v, it, hp):
            v.wait_ge(l_sem["wh"], it + 1)
            v.tensor_tensor(L["l_wl"][:], L["l_w"][:], f32(L["l_wh"][:]), ALU.subtract).then_inc(l_sem["wl"], 1)
            n = 0
            for m in range(2):
                src = ps[:, 2 * m:2 * m + 2, :].rearrange("p a w -> p (a w)")
                for h in range(2):
                    hr = src[h * SD:(h + 1) * SD, :]
                    if m == 0:
                        n += 1
                        v.wait_ge(l_sem["hi"], it * 6 + n)
                        v.scalar_tensor_tensor(out=LQ[h][64:128, :], in0=hr, scalar=0.125, in1=f32(LQ[h][0:64, :]),
                                               op0=ALU.mult, op1=ALU.subtract).then_inc(l_sem["lo"], 1)
                    else:
                        n += 2
                        v.wait_ge(l_sem["hi"], it * 6 + n)
                        v.tensor_tensor(LK2[h][0:64, :], hr, f32(LK1[h][0:64, :]), ALU.subtract).then_inc(l_sem["lo"], 1)
                        v.tensor_tensor(LK2[h][64:128, :], hr, f32(LK1[h][64:128, :]), ALU.subtract).then_inc(l_sem["lo"], 1)

            def plain(k, i, n_):
                return banks_of(k)[:, 0:n_]

            def finish(k, h, i, o, r):
                return v.tensor_scalar(L["l_o"][:, i, h * SD:(h + 1) * SD], o, r, None, ALU.mult)

            att_v(v, AT1, bl1, it, plain, finish, True)

        def l_pe_end(pe, b):
            for t in range(NT):
                tok = slice(t * P, (t + 1) * P)
                if t >= 2:
                    pe.wait_ge(s_xu, b * (NPH * NT) + 3 * NT + t - 1)
                for c in range(HP):
                    last = pe.matmul(ps[:, 6 + t % 2, 0:D], L["l_oT"][:, c, tok], wo[:, c, :], start=c == 0, stop=c == HP - 1)
                last.then_inc(l_sem["wo"], 1)

        def l_v_end(v, b):
            for t in range(NT):
                v.wait_ge(l_sem["wo"], b * NT + t + 1)
                v.tensor_tensor(x[:, t, :], x[:, t, :], ps[:, 6 + t % 2, 0:D], ALU.add).then_inc(s_xu, 1)

        g_sem = {k: sem(f"g_{k}") for k in ("xq", "tp", "xT", "gt", "up", "si", "gh", "h", "hq", "ht", "hT", "dn")}

        def psb(bank):
            return ps[:, bank, :].bitcast(BF16)

        def g_pe(pe, b):
            for g in range(2):
                pe.wait_ge(g_sem["xq"], b * NT + 4 * g + 4)
                o = psb(6 + g)
                for c in range(DC):
                    for t in range(4):
                        last = pe.transpose(o[:, c * HALF + t * P:c * HALF + (t + 1) * P], G["g_xq"][:, 4 * g + t, c * P:(c + 1) * P], idb[:])
                last.then_inc(g_sem["tp"], 1)
            pe.wait_ge(g_sem["xT"], b * 2 + 2)

            def updown(t):
                tok = slice(t * P, (t + 1) * P)
                for m, w in ((0, wg_q), (1, wu_q)):
                    if t >= 1:
                        pe.wait_ge(g_sem["si" if m == 0 else "gh"], b * NT + t)
                    for n in range(2):
                        for c in range(DC):
                            last = pe.matmul(ps[:, 2 * m + n, :], G["g_xT"][:, c, tok], w[:, c, n * HALF:(n + 1) * HALF],
                                             start=c == 0, stop=c == DC - 1)
                    last.then_inc(g_sem["gt" if m == 0 else "up"], 1)

            def rest(t):
                pe.wait_ge(g_sem["hq"], b * NT + t + 1)
                if t >= 2:
                    pe.wait_ge(g_sem["hT"], b * NT + t - 1)
                for f in range(FC):
                    last = pe.transpose(psb(4 + t % 2)[:, f * P:(f + 1) * P], G["g_hq"][:, t % 2, f * P:(f + 1) * P], idb[:])
                last.then_inc(g_sem["ht"], 1)
                pe.wait_ge(g_sem["hT"], b * NT + t + 1)
                if t >= 2:
                    pe.wait_ge(s_xu, b * (NPH * NT) + 5 * NT + t - 1)
                for f in range(FC):
                    last = pe.matmul(ps[:, 6 + t % 2, 0:D], G["g_hT"][:, t % 2, f * P:(f + 1) * P], wd_q[:, f, :], start=f == 0, stop=f == FC - 1)
                last.then_inc(g_sem["dn"], 1)

            updown(0)
            for t in range(NT):
                if t + 1 < NT:
                    updown(t + 1)
                rest(t)

        def g_v(v, b):
            v.drain()
            v.tensor_reduce(G["g_amx"][:], xn[:], AX.X, ALU.max, apply_absolute_value=True)
            v.drain()
            v.tensor_scalar(G["g_amx"][:], G["g_amx"][:], EPS, None, ALU.max)
            v.drain()
            v.tensor_scalar(G["g_inv"][:], G["g_amx"][:], 1.0 / 127.0, None, ALU.mult)
            v.drain()
            v.reciprocal(G["g_s"][:], G["g_inv"][:])
            v.tensor_scalar(G["g_ig"][:], G["g_inv"][:], wsc[:, 0:1], None, ALU.mult)
            v.tensor_scalar(G["g_iu"][:], G["g_inv"][:], wsc[:, 1:2], None, ALU.mult)
            v.drain()
            for t in range(NT):
                v.tensor_scalar(G["g_t"][:, t % 2, :], xn[:, t, :], G["g_s"][:, t:t + 1], MAGIC, ALU.mult, ALU.add)
                v.drain()
                v.tensor_scalar(G["g_xq"][:, t, :], G["g_t"][:, t % 2, :], MAGIC, 127.0, ALU.subtract, ALU.min).then_inc(g_sem["xq"], 1)

            def hidden(t):
                v.wait_ge(g_sem["up"], b * NT + t + 1)
                v.wait_ge(g_sem["si"], b * NT + t + 1)
                v.scalar_tensor_tensor(out=G["g_h"][:, t % 2, :], in0=ps[:, 2:4, :].rearrange("p a w -> p (a w)"), scalar=G["g_iu"][:, t:t + 1],
                                       in1=G["g_g"][:, t % 2, :], op0=ALU.mult, op1=ALU.mult).then_inc(g_sem["gh"], 1)
                hm, hs, hi = G["g_hm"][:, t % 2:t % 2 + 1], G["g_hs"][:, t % 2:t % 2 + 1], G["g_hi"][:, t % 2:t % 2 + 1]
                v.drain()
                v.tensor_reduce(hm, G["g_h"][:, t % 2, :], AX.X, ALU.max, apply_absolute_value=True)
                v.drain()
                v.tensor_scalar(hm, hm, EPS, 1.0 / 127.0, ALU.max, ALU.mult)
                v.drain()
                v.reciprocal(hs, hm)
                v.tensor_scalar(hi, hm, wsc[:, 2:3], None, ALU.mult)
                v.drain()
                v.tensor_scalar(G["g_r"][:, t % 2, :], G["g_h"][:, t % 2, :], hs, MAGIC, ALU.mult, ALU.add)
                v.drain()
                v.tensor_scalar(G["g_hq"][:, t % 2, :], G["g_r"][:, t % 2, :], MAGIC, 127.0, ALU.subtract, ALU.min).then_inc(g_sem["hq"], 1)

            hidden(0)
            for t in range(NT):
                if t + 1 < NT:
                    hidden(t + 1)
                v.wait_ge(g_sem["dn"], b * NT + t + 1)
                v.scalar_tensor_tensor(out=x[:, t, :], in0=ps[:, 6 + t % 2, 0:D], scalar=G["g_hi"][:, t % 2:t % 2 + 1],
                                       in1=x[:, t, :], op0=ALU.mult, op1=ALU.add).then_inc(s_xu, 1)

        def g_a(s, b):
            for g in range(2):
                s.wait_ge(g_sem["tp"], b * 2 + g + 1)
                s.copy(G["g_xT"][:, :, g * HALF:(g + 1) * HALF], psb(6 + g).rearrange("p (c w) -> p c w", c=DC)).then_inc(g_sem["xT"], 1)

            def silu(t):
                s.wait_ge(g_sem["gt"], b * NT + t + 1)
                if t >= 2:
                    s.wait_ge(g_sem["gh"], b * NT + t - 1)
                s.activation(G["g_g"][:, t % 2, :], ps[:, 0:2, :].rearrange("p a w -> p (a w)"), ACT.Silu,
                             scale=G["g_ig"][:, t:t + 1]).then_inc(g_sem["si"], 1)

            silu(0)
            for t in range(NT):
                if t + 1 < NT:
                    silu(t + 1)
                s.wait_ge(g_sem["ht"], b * NT + t + 1)
                if t >= 2:
                    s.wait_ge(g_sem["dn"], b * NT + t - 1)
                s.copy(G["g_hT"][:, t % 2, :], psb(4 + t % 2)).then_inc(g_sem["hT"], 1)

        loads = [
            (S["s_wsh"][:], a["a_wsh"].rearrange("(c p) n -> p c n", p=P)), (S["s_om"][:], a["a_om"]), (S["s_wc"][:], a["a_wc"]),
            (S["s_wv"][:], a["a_wv"].rearrange("(c p) n -> p c n", p=P)), (S["s_wo"][:], a["a_wo"].rearrange("(c p) n -> p c n", p=P)),
            (S["s_bv"][:], a["a_bv"]), (S["s_bo"][:], rows(a["a_bo"])), (S["s_lt"][:], rows(a["a_lt"])),
            (bsh[:], rows(a["a_bsh"])), (rbias[:], a["a_rb"].rearrange("(p o) -> p o", o=1)),
            (S["s_g"][:].rearrange("p (c n) -> p c n", c=DC), a["g_wg"].rearrange("(c p) n -> p c n", p=P)),
            (S["s_u"][:].rearrange("p (c n) -> p c n", c=DC), a["g_wu"].rearrange("(c p) n -> p c n", p=P)),
            (S["s_d"][:].rearrange("p (c n) -> p c n", c=FC), a["g_wd"].rearrange("(c p) n -> p c n", p=P)),
            (wo[:], a["l_wo"].rearrange("(c p) n -> p c n", p=P)),
            (x0_wq[:], a["x0_wq"].rearrange("(c p) n -> p c n", p=P)), (x0_wk[:, 0, :], a["x0_wk"][0:P]), (x0_wk[0:64, 1, :], a["x0_wk"][P:CTX]),
            (x0_wv[:, 0, :], a["x0_wv"][0:P]), (x0_wv[0:64, 1, :], a["x0_wv"][P:CTX]),
            (x0_wo[:], a["x0_wo"].rearrange("(c p) n -> p c n", p=P)), (x0_bo[:], rows(a["x0_bo"])),
            (x1_wq[:], a["x1_wq"].rearrange("(c p) n -> p c n", p=P)), (x1_wk[:, 0, :], a["x1_wk"][0:P]), (x1_wk[0:64, 1, :], a["x1_wk"][P:CTX]),
            (x1_wv[:, 0, :], a["x1_wv"][0:P]), (x1_wv[0:64, 1, :], a["x1_wv"][P:CTX]),
            (x1_wo[:], a["x1_wo"].rearrange("(c p) n -> p c n", p=P)), (x1_bo[:], rows(a["x1_bo"])),
            (x1_bk[:], a["x1_bk"]), (x1_bv[:], a["x1_bv"]),
            (x1_bq[:], a["x1_bq"]),
            (wr[:], a["m_wr"].rearrange("(c p) n -> p c n", p=P)), (br[:], a["m_br"].rearrange("(o n) -> o n", o=1)),
        ]

        def setup_g(g):
            g.iota(S["s_iota"][:], pattern=[[-1, T]], base=T - P, channel_multiplier=1)
            g.iota(S["s_pi"][:], pattern=[[0, 1]], base=0, channel_multiplier=1)
            g.memset(idf[:], 0.0).then_inc(s_gc, 1)
            g.memset(ones_f[:], 1.0).then_inc(s_gc, 1)
            g.memset(S["s_m"][:], 0.0).then_inc(s_gc, 1)
            g.memset(causal[:], 0.0).then_inc(s_gc, 1)
            g.memset(row01[:], 0.0).then_inc(s_gc, 1)
            g.memset(blk0[:], 1.0).then_inc(s_gc, 1)
            g.memset(blk1[:], 1.0).then_inc(s_gc, 1)
            g.memset(cosb[:], 0.0).then_inc(s_gc, 1)
            g.memset(ones_b[:], 1.0).then_inc(s_gc, 1)
            g.memset(coss[:], 1.0).then_inc(s_gc, 1)
            g.wait_ge(s_gc, 10)
            g.affine_select(out=idf[:], in_=idf[:], compare_op=ALU.not_equal, fill=1.0, base=0, pattern=[[-1, P]], channel_multiplier=1).then_inc(s_gc, 1)
            g.affine_select(out=causal[:], in_=causal[:], compare_op=ALU.is_ge, fill=NEG, base=0, pattern=[[-1, P]], channel_multiplier=1).then_inc(s_gc, 1)
            g.affine_select(out=row01[:], in_=row01[:], compare_op=ALU.not_equal, fill=1.0, base=0, pattern=[[-1, 2]], channel_multiplier=1).then_inc(s_gc, 1)
            for blk, n, w in ((blk0, 2, XD0), (blk1, 8, XD1)):
                g.affine_select(out=blk[:], in_=blk[:], compare_op=ALU.is_ge, fill=0.0, base=0, pattern=[[-w, n]], channel_multiplier=1).then_inc(s_gc, 1)
            g.affine_select(out=cosb[:], in_=cosb[:], compare_op=ALU.is_ge, fill=math.pi / 2, base=-RFF, pattern=[[0, 1]], channel_multiplier=1).then_inc(s_gc, 1)
            g.affine_select(out=coss[:], in_=coss[:], compare_op=ALU.is_ge, fill=-1.0, base=-RFF, pattern=[[0, 1]], channel_multiplier=1).then_inc(s_gc, 1)
            g.wait_ge(s_gc, 17)
            for blk, n, w in ((blk0, 2, XD0), (blk1, 8, XD1)):
                g.affine_select(out=blk[:], in_=blk[:], compare_op=ALU.is_ge, fill=0.0, base=w - 1, pattern=[[w, n]], channel_multiplier=-1).then_inc(s_gc, 1)
            g.tensor_copy(idb[:], idf[:]).then_inc(s_gc, 1)

        GC = 20

        def setup_a(s):
            s.wait_ge(s_w, 16 * len(loads))
            s.wait_ge(s_gc, GC)
            s.activation(S["s_t"][:, 0:1], S["s_lt"][:], ACT.Abs).then_inc(s_sa, 1)
            s.wait_ge(s_sa, 1)
            s.activation(S["s_t"][:, 1:2], S["s_t"][:, 0:1], ACT.Exp, scale=-1.0).then_inc(s_sa, 1)
            s.wait_ge(s_sa, 2)
            s.activation(S["s_t"][:, 2:3], S["s_t"][:, 1:2], ACT.Ln, bias=1.0).then_inc(s_sa, 1)
            s.wait_ge(s_sv, 1)
            s.activation(S["s_dist"][:], S["s_dist"][:], ACT.Abs)
            s.drain()
            s.activation(S["s_dist"][:], S["s_dist"][:], ACT.Exp, scale=-0.3 / 10.0).then_inc(s_sa, 1)
            s.copy(wsh_h[:], S["s_wsh"][:]).then_inc(s_sa, 1)
            s.copy(om_h[:], S["s_om"][:]).then_inc(s_sa, 1)
            s.wait_ge(s_sv, 2)
            s.copy(wc_h[:], S["s_wc"][:].rearrange("p m o -> p (m o)")).then_inc(s_sa, 1)
            s.copy(ones_r[:], ones_f[0:2, :]).then_inc(s_sa, 1)
            s.wait_ge(s_sp, 1)
            s.copy(wvo_h[:], ps[:, 0, :].rearrange("p (c d) -> p c d", c=DC)).then_inc(s_sa, 1)

        SA = 9

        def setup_v(v):
            v.wait_ge(s_w, 16 * len(loads))
            v.wait_ge(s_gc, GC)
            v.tensor_copy(S["s_dist"][:], S["s_iota"][:]).then_inc(s_sv, 1)
            scale = math.sqrt(2.0 / (2 * RFF)) * math.sqrt(math.exp(-0.5))
            for m in range(ORDERS):
                last = v.tensor_scalar(S["s_wc"][:, m, :], S["s_wc"][:, m, :], scale * math.sqrt(1.0 / math.factorial(m) + 1e-10), None, ALU.mult)
            last.then_inc(s_sv, 1)
            for c in range(DC):
                v.tensor_scalar(S["s_bvb"][:, c, :], ones_f[:], S["s_bv"][:, c:c + 1], None, ALU.mult)
                last = v.tensor_scalar(x1_bqb[:, c, :], ones_f[:], x1_bq[:, c:c + 1], None, ALU.mult)
            last.then_inc(s_sv, 1)
            v.wait_ge(s_sa, 4)
            v.tensor_scalar(S["s_t"][:, 3:4], S["s_lt"][:], 0.0, 0.1, ALU.max, ALU.add)
            v.drain()
            v.tensor_tensor(S["s_t"][:, 3:4], S["s_t"][:, 3:4], S["s_t"][:, 2:3], ALU.add)
            v.drain()
            v.reciprocal(S["s_t"][:, 0:1], S["s_t"][:, 3:4])
            v.drain()
            v.tensor_scalar(decay[:], S["s_dist"][:], S["s_t"][:, 0:1], None, ALU.mult)
            v.wait_ge(s_sa, 7)
            v.tensor_tensor(wsh_l[:], S["s_wsh"][:], f32(wsh_h[:]), ALU.subtract)
            v.tensor_tensor(om_l[:], S["s_om"][:], f32(om_h[:]), ALU.subtract)
            v.tensor_tensor(wc_l[:], S["s_wc"][:].rearrange("p m o -> p (m o)"), f32(wc_h[:]), ALU.subtract)
            for n, w in enumerate(("s_g", "s_u", "s_d")):
                last = v.tensor_reduce(S["s_abs"][:, n:n + 1], S[w][:], AX.X, ALU.add, apply_absolute_value=True)
            last.then_inc(s_sv, 1)
            v.wait_ge(s_sp, 1)
            v.tensor_scalar(wsc[:, 0:3], ps[:, 1, 0:3], 1.0 / (D * FF), EPS, ALU.mult, ALU.max)
            v.drain()
            v.reciprocal(S["s_i8"][:, 0:3], wsc[:, 0:3])
            v.drain()
            for n, (w, q) in enumerate((("s_g", wg_q), ("s_u", wu_q), ("s_d", wd_q))):
                v.tensor_scalar(S["s_q"][:], S[w][:], S["s_i8"][:, n:n + 1], MAGIC, ALU.mult, ALU.add)
                v.drain()
                v.tensor_scalar(S["s_q"][:], S["s_q"][:], MAGIC, 1.0, ALU.subtract, ALU.min)
                v.drain()
                v.tensor_scalar(q[:].rearrange("p c n -> p (c n)"), S["s_q"][:], -1.0, None, ALU.max)
                v.drain()
            v.wait_ge(s_sa, SA)
            v.tensor_tensor(wvo_l[:], ps[:, 0, :].rearrange("p (c d) -> p c d", c=DC), f32(wvo_h[:]), ALU.subtract)
            v.tensor_tensor(bvo[:], ps[:, 2, 0:D], S["s_bo"][:], ALU.add).then_inc(s_sv, 1)

        SV = 5

        def setup_pe(pe):
            pe.wait_ge(s_w, 16 * len(loads))
            pe.wait_ge(s_sv, 4)
            for c in range(DC):
                for k in range(DC):
                    pe.matmul(ps[:, 0, c * D:(c + 1) * D], S["s_wv"][:, k, c * P:(c + 1) * P], S["s_wo"][:, k, :], start=k == 0, stop=k == DC - 1)
            for k in range(DC):
                pe.matmul(ps[:, 2, 0:D], S["s_bvb"][:, k, :], S["s_wo"][:, k, :], start=k == 0, stop=k == DC - 1)
            pe.matmul(ps[:, 1, 0:3], ones_f[:], S["s_abs"][:, 0:3], start=True, stop=True).then_inc(s_sp, 1)

        block = ctx.enter_context(nc.Block())

        @block.sync
        def _(sp):
            for dst, src in loads:
                sp.dma_start(dst, src).then_inc(s_w, 16)
            with sp.Fori(0, B) as b:
                sp.wait_ge(s_xb, b * 4)
                sp.dma_start(xin[:], a["x"][bass.ds(b, 1)].rearrange("o (t p) d -> p (o t) d", p=P)).then_inc(s_xin, 16)
                sp.wait_ge(C1.s["kv"], b)
                sp.wait_ge(C0.s["b2"], b)
                sp.dma_start(ctxT[:, 0, :], a["ctxT"][bass.ds(b, 1), 0:P].rearrange("o c k -> (o c) k")).then_inc(s_ctx, 16)
                sp.dma_start(ctxT[0:64, 1, :], a["ctxT"][bass.ds(b, 1), P:CTX].rearrange("o c k -> (o c) k")).then_inc(s_ctx, 16)
                sp.dma_start(mrow4[:], a["mask"][bass.ds(b, 1)]).then_inc(s_ctx, 16)
                m_sp(sp, b)
                with sp.Fori(0, HP) as hp:
                    sp.wait_ge(s_xu, b * (NPH * NT) + 3 * NT)
                    it = b * HP + hp
                    sp.wait_ge(l_sem["wl"], it)
                    sp.dma_start(L["l_w"][:], a["l_w"][bass.ds(hp, 1)].rearrange("o p m c e -> p (o m) c e")).then_inc(l_sem["w"], 16)
            sp.wait_ge(s_out, 16 * B)

        @block.gpsimd
        def _(g):
            setup_g(g)
            g.wait_ge(s_sv, SV)
            with g.Fori(0, B) as b:
                g.wait_ge(s_out, b * 16)
                g.wait_ge(s_xn, b * (NPH * NT) + NT)
                g.tensor_tensor(x[:], xin[:], bvo[:].unsqueeze(1).to_broadcast([P, NT, D]), ALU.add).then_inc(s_xb, 1)
                x_g(g, C0, b, x0_bo)
                m_g(g, b)
                x_g(g, C1, b, x1_bo)

        @block.scalar
        def _(s):
            setup_a(s)
            s.wait_ge(s_sv, SV)
            with s.Fori(0, B) as b:
                ln_a(s, b, 0)
                a_a(s, b)
                x_a_prep(s, C0, b)
                ln_a(s, b, 1)
                x_a(s, C0, b)
                m_a(s, b)
                ln_a(s, b, 3)
                with s.Fori(0, HP) as hp:
                    l_a_body(s, b * HP + hp, hp)
                x_a_prep(s, C1, b)
                ln_a(s, b, 4)
                x_a(s, C1, b)
                g_a(s, b)
                s.wait_ge(s_xu, b * (NPH * NT) + NPH * NT)
                s.dma_start(out[bass.ds(b, 1)].rearrange("o (t p) d -> p (o t) d", p=P), x[:]).then_inc(s_out, 16)

        @block.vector
        def _(v):
            setup_v(v)
            with v.Fori(0, B) as b:
                ln_v(v, b, 0, xin)
                ln_lo(v, b, 0)
                a_v(v, b)
                x_v_prep(v, C0, b)
                ln_v(v, b, 1, x)
                ln_lo(v, b, 1)
                x_v(v, C0, b)
                ln_v(v, b, 2, x)
                m_v(v, b)
                ln_v(v, b, 3, x)
                ln_lo(v, b, 3)
                with v.Fori(0, HP) as hp:
                    l_v_body(v, b * HP + hp, hp)
                l_v_end(v, b)
                x_v_prep(v, C1, b)
                ln_v(v, b, 4, x)
                ln_lo(v, b, 4)
                x_v(v, C1, b)
                ln_v(v, b, 5, x)
                g_v(v, b)

        @block.tensor
        def _(pe):
            setup_pe(pe)
            pe.wait_ge(s_sv, SV)
            with pe.Fori(0, B) as b:
                ln_pe(pe, b, 0)
                a_pe(pe, b)
                x_pe_prep(pe, C0, b)
                ln_pe(pe, b, 1)
                x_pe(pe, C0, b)
                m_pe(pe, b)
                ln_pe(pe, b, 3)
                with pe.Fori(0, HP) as hp:
                    pe.wait_ge(s_lo, ln_done(b, 3))
                    l_pe_body(pe, b * HP + hp)
                l_pe_end(pe, b)
                x_pe_prep(pe, C1, b)
                ln_pe(pe, b, 4)
                x_pe(pe, C1, b)
                g_pe(pe, b)


def kernel(**inputs):
    import numpy as np
    import concourse.bacc as bacc
    from concourse.bass_utils import run_bass_kernel_spmd

    i = {k: np.asarray(v) for k, v in inputs.items()}
    c = np.ascontiguousarray
    la, lx, lf = "L0_attn_", "L0_xattn_", "L0_ffn_"
    kx, kf = "L1_xattn_", "L1_ffn_"
    wkv = i[kx + "Wkv"].reshape(XH1, 2, XD1, CTX)
    bkv = i[kx + "bkv"].reshape(XH1, 2, XD1)
    qkv = np.stack([i["L1_attn_" + n].reshape(HP, 2 * SD, DC, P) for n in ("w_q", "w_k", "w_v")])
    arrays = {
        "x": c(i["x"]),
        "ctxT": c(i["ctx_768"].transpose(0, 2, 1)),
        "mask": c(i["mask_BxS2_bk0"]).view(np.int32),
        "a_wsh": c(np.concatenate([i[la + "W_shell"], i[la + "W_charge"], i[la + "W_charge"]]).T),
        "a_bsh": c(np.concatenate([i[la + "b_shell"], i[la + "b_charge"], i[la + "b_charge"]])),
        "a_om": c(np.concatenate([i[la + "omega"]] * 4).T),
        "a_rb": c(np.concatenate([i[la + "rff_bias"]] * 2)),
        "a_wc": c(i[la + "W_combine"].reshape(COMB, ORDERS, SHELL).transpose(2, 1, 0)),
        "a_wv": c(i[la + "W_v"]),
        "a_wo": c(i[la + "W_out"].T),
        "a_bv": c(i[la + "b_v"].reshape(DC, P).T),
        "a_bo": c(i[la + "b_out"]),
        "a_lt": c(i[la + "log_temp"].reshape(1)),
        "x0_wq": c(i[lx + "W_q"].T),
        "x0_wk": c(i[lx + "W_k"]),
        "x0_wv": c(i[lx + "W_v"]),
        "x0_wo": c(i[lx + "W_o"]),
        "x0_bo": c(i[lx + "b_o"]),
        "m_wr": c(i[lf + "Wr"]),
        "m_br": c(i[lf + "br"]),
        "m_w1": c(i[lf + "W1"]),
        "m_b1": c(i[lf + "b1"].reshape(EXPERTS, FC, P).transpose(0, 2, 1)),
        "m_w2": c(i[lf + "W2"]),
        "m_b2": c(i[lf + "b2"]),
        "l_w": c(qkv.transpose(1, 4, 0, 3, 2)),
        "l_wo": c(i["L1_attn_w_o"].T),
        "x1_wq": c(i[kx + "Wq"]),
        "x1_bq": c(i[kx + "bq"].reshape(DC, P).T),
        "x1_wk": c(wkv[:, 0].reshape(D, CTX).T),
        "x1_wv": c(wkv[:, 1].reshape(D, CTX).T),
        "x1_bk": c(bkv[:, 0].reshape(DC, P).T),
        "x1_bv": c(bkv[:, 1].reshape(DC, P).T),
        "x1_wo": c(i[kx + "Wo"].T),
        "x1_bo": c(i[kx + "bo"]),
        "g_wg": c(i[kf + "w_gate"].T),
        "g_wu": c(i[kf + "w_up"].T),
        "g_wd": c(i[kf + "w_down"].T),
    }
    nc = bacc.Bacc("TRN2", target_bir_lowering=False, num_devices=1)
    given = {f"in_{k}": v for k, v in arrays.items()}
    aps = {k: nc.dram_tensor(f"in_{k}", v.shape, mybir.dt.from_np(v.dtype), kind="ExternalInput").ap() for k, v in arrays.items()}
    out = nc.dram_tensor("out_x", (B, T, D), F32, kind="ExternalOutput").ap()
    decoder_kernel(nc, aps, out)
    r = run_bass_kernel_spmd(nc, [given], core_ids=[0])
    return r.results[0]["out_x"]
```

```python
from contextlib import ExitStack
import math

import concourse.bass as bass
from concourse import mybir

P = 128
B, T, D = 4, 1024, 256
NT = T // P
DC = D // P
HALF = 512
CTX, CK = 192, 64
SHELL, RFF, ORDERS, COMB = 64, 32, 5, 64
FF = 1024
FC = FF // P
EXPERTS = 8
XH0, XD0 = 8, 64
XH1, XD1 = 16, 16
SD = 64
HP = 8
NPH = 6

NEG = -1.0e30
MASKED = -float(2.0 ** 127)
MAGIC = 12582912.0
TWO_PI_HI = 6.28125
TWO_PI_LO = 2.0 * math.pi - 6.28125
PI_BELOW = 3.1415925
EPS = 1e-5

F32 = mybir.dt.float32
F32R = mybir.dt.float32r
BF16 = mybir.dt.bfloat16
F16 = mybir.dt.float16
I32 = mybir.dt.int32
U32 = mybir.dt.uint32
U8 = mybir.dt.uint8
ALU = mybir.AluOpType
ACT = mybir.ActivationFunctionType
AX = mybir.AxisListType


def rows(ap):
    return ap.rearrange("(o n) -> o n", o=1).to_broadcast([P, ap.shape[0]])


def decoder_kernel(nc, a, out):
    ctx = ExitStack()
    with ctx:
        def sb(name, shape, dt=F32, stack=ctx):
            return stack.enter_context(nc.sbuf_tensor(name, shape, dt))

        def sem(name):
            return ctx.enter_context(nc.semaphore(name))

        xin = sb("xin", [P, NT, D])
        x = sb("x", [P, NT, D])
        xn = sb("xn", [P, NT, D])
        xTh = sb("xTh", [P, DC, T], F32R)
        xTl = sb("xTl", [P, DC, T], F32R)
        idf = sb("idf", [P, P])
        idb = sb("idb", [P, P], BF16)
        causal = sb("causal", [P, P], BF16)
        ones_b = sb("ones_b", [1, P], BF16)
        ones_r = sb("ones_r", [2, P], F32R)
        ones_f = sb("ones_f", [P, P])
        decay = sb("decay", [P, T])
        wsh_h = sb("wsh_h", [P, DC, 66], F32R)
        wsh_l = sb("wsh_l", [P, DC, 66], F32R)
        bsh = sb("bsh", [P, 66])
        om_h = sb("om_h", [SHELL, P], F32R)
        om_l = sb("om_l", [SHELL, P], F32R)
        rbias = sb("rbias", [SHELL, 1])
        cosb = sb("cosb", [SHELL, 1])
        coss = sb("coss", [SHELL, 1])
        wc_h = sb("wc_h", [SHELL, ORDERS * COMB], F32R)
        wc_l = sb("wc_l", [SHELL, ORDERS * COMB], F32R)
        wvo_h = sb("wvo_h", [P, DC, D], F32R)
        wvo_l = sb("wvo_l", [P, DC, D], F32R)
        bvo = sb("bvo", [P, D])
        x0_wq = sb("x0_wq", [P, 4, D])
        x0_wk = sb("x0_wk", [P, 2, 512])
        x0_wv = sb("x0_wv", [P, 2, 512])
        x0_wo = sb("x0_wo", [P, 4, D])
        x0_bo = sb("x0_bo", [P, D])
        x1_wq = sb("x1_wq", [P, 2, D])
        x1_wk = sb("x1_wk", [P, 2, D])
        x1_wv = sb("x1_wv", [P, 2, D])
        x1_wo = sb("x1_wo", [P, 2, D])
        x1_bo = sb("x1_bo", [P, D])
        x1_bk = sb("x1_bk", [P, 2])
        x1_bv = sb("x1_bv", [P, 2])
        x1_bq = sb("x1_bq", [P, 2])
        x1_bqb = sb("x1_bqb", [P, 2, P])
        blk0 = sb("blk0", [P, 2])
        blk1 = sb("blk1", [P, 8])
        row01 = sb("row01", [P, 2])
        wr = sb("wr", [P, DC, EXPERTS])
        br = sb("br", [1, EXPERTS])
        wo = sb("wo", [P, HP, D])
        wg_q = sb("wg_q", [P, DC, FF], BF16)
        wu_q = sb("wu_q", [P, DC, FF], BF16)
        wd_q = sb("wd_q", [P, FC, D], BF16)
        wsc = sb("wsc", [P, 4])
        st = sb("st", [P, NT, 6])
        ag = sb("ag", [P, NT, 2])
        rsd = sb("rsd", [P, NT])
        nv = sb("nv", [P, NT])
        nt1 = sb("nt1", [P, NT])
        ctxT = sb("ctxT", [P, 2, CK])
        mrow4 = sb("mrow4", [1, CK // 4], I32)
        mrow = sb("mrow", [1, XH0 * CK], BF16)
        sums = sb("sums", [P, 4])
        nmax = sb("nmax", [P, 4])
        rec = sb("rec", [P, 4])
        ps = ctx.enter_context(nc.psum_tensor("ps", [P, 8, HALF], F32))

        def arena(names_shapes):
            with ExitStack() as phase:
                made = {n: phase.enter_context(nc.sbuf_tensor(n, s, d)) for n, s, d in names_shapes}
            return made

        S = arena([
            ("s_wsh", [P, DC, 66], F32), ("s_om", [SHELL, P], F32), ("s_wc", [SHELL, ORDERS, COMB], F32),
            ("s_wv", [P, DC, D], F32), ("s_wo", [P, DC, D], F32), ("s_bv", [P, DC], F32), ("s_bo", [P, D], F32),
            ("s_bvb", [P, DC, P], F32), ("s_lt", [P, 1], F32), ("s_t", [P, 4], F32),
            ("s_iota", [P, T], I32), ("s_dist", [P, T], F32),
            ("s_g", [P, 2048], F32), ("s_u", [P, 2048], F32), ("s_d", [P, 2048], F32),
            ("s_q", [P, 2048], F32), ("s_abs", [P, 4], F32), ("s_i8", [P, 8], F32), ("s_p", [P, 2], F32),
            ("s_pi", [P, 1], I32), ("s_m", [P, 1], F32)])
        A = arena([
            ("a_sh", [P, NT, 66], F32), ("a_q", [P, NT], F32), ("a_sq", [P, NT, SHELL], F32), ("a_ss", [P, NT], F32),
            ("a_rn", [P, NT], F32), ("a_shn", [P, NT, P], F32),
            ("a_shTh", [SHELL, T], F32R), ("a_shTl", [SHELL, T], F32R),
            ("a_p", [SHELL, T], F32), ("a_k", [SHELL, T], F32), ("a_r", [SHELL, T], F32), ("a_phs", [SHELL, T], F32),
            ("a_phh", [SHELL, T], F32R), ("a_phl", [SHELL, T], F32R),
            ("a_y", [P, NT, ORDERS * COMB], F32), ("a_acc", [P, NT, COMB], F32), ("a_phi", [P, NT, P], F32),
            ("a_v", [P, NT, D], F32),
            ("a_qs", [P, T], F32R), ("a_k1", [P, T], F32R), ("a_k2", [P, T], F32R),
            ("a_sm", [P, 2, T], F32), ("a_pe", [P, 2, T], F32), ("a_pt", [P, 2, T], F32)])
        X = arena([
            ("c_kT", [P, 4, CK], F32), ("c_vT", [P, 4, CK], F32),
            ("c_kB", [P, 4, P], F32), ("c_vB", [P, 4, P], F32), ("c_kC", [P, 2, HALF], F32), ("c_vC", [P, 2, HALF], F32),
            ("c_mh", [P, DC, 1024], F32R), ("c_ml", [P, DC, 1024], F32R),
            ("c_uh", [P, 8, D], F32R), ("c_ul", [P, 8, D], F32R),
            ("c_b2", [P, 1024], F32R), ("c_bh", [P, 1024], F32R), ("c_bl", [P, 1024], F32),
            ("c_mx", [P, 2, 16], F32), ("c_sm", [P, 2, 1024], F32), ("c_pe", [P, 2, 1024], F32),
            ("c_su", [P, 2, 16], F32), ("c_re", [P, 2, 16], F32), ("c_pn", [P, 2, 1024], F32),
            ("c_th", [P, 2, 1024], F32R), ("c_tl", [P, 2, 1024], F32R)])
        M = arena([
            ("m_mean", [P, DC], F32), ("m_sc", [1, EXPERTS], F32), ("m_top", [1, 8], F32), ("m_idx", [1, 8], U32),
            ("m_w1", [P, DC, FF], F32), ("m_w2", [P, FC, D], F32), ("m_b1", [P, FC], F32), ("m_b2", [P, D], F32),
            ("m_w1h", [P, DC, FF], F32R), ("m_w1l", [P, DC, FF], F32R),
            ("m_w2h", [P, FC, D], F32R), ("m_w2l", [P, FC, D], F32R),
            ("m_h", [P, 2, HALF], F32),
            ("m_hh", [P, FC, HALF], F32R), ("m_hl", [P, FC, HALF], F32R)])
        L = arena([
            ("l_w", [P, 3, DC, P], F32), ("l_wh", [P, 3, DC, P], F32R), ("l_wl", [P, 3, DC, P], F32R),
            ("l_q0", [P, T], F32R), ("l_q1", [P, T], F32R),
            ("l_k10", [P, T], F32R), ("l_k11", [P, T], F32R), ("l_k20", [P, T], F32R), ("l_k21", [P, T], F32R),
            ("l_v", [P, 3, NT, P], BF16), ("l_vr", [P, NT, P], F32),
            ("l_pe", [P, 2, T], F32), ("l_pt", [P, 2, 2, T], F16), ("l_o", [P, NT, P], F32),
            ("l_oT", [P, HP, T], F32)])
        G = arena([
            ("g_amx", [P, NT], F32), ("g_s", [P, NT], F32), ("g_inv", [P, NT], F32), ("g_ig", [P, NT], F32), ("g_iu", [P, NT], F32),
            ("g_t", [P, 2, D], F32), ("g_xq", [P, NT, D], BF16), ("g_xT", [P, DC, T], BF16),
            ("g_g", [P, 2, FF], F32), ("g_h", [P, 2, FF], F32), ("g_r", [P, 2, FF], F32), ("g_hq", [P, 2, FF], BF16),
            ("g_hT", [P, 2, FF], BF16), ("g_hm", [P, 2], F32), ("g_hs", [P, 2], F32), ("g_hi", [P, 2], F32)])

        s_w = sem("s_w")
        s_gc = sem("s_gc")
        s_sa = sem("s_sa")
        s_sv = sem("s_sv")
        s_sp = sem("s_sp")
        s_xin = sem("s_xin")
        s_ctx = sem("s_ctx")
        s_xu = sem("s_xu")
        s_xb = sem("s_xb")
        s_out = sem("s_out")
        s_used = sem("s_used")
        s_xn = sem("s_xn")
        s_tr = sem("s_tr")
        s_hi = sem("s_hi")
        s_lo = sem("s_lo")

        def mm3(pe, o, lh, ll, rh, rl, start, stop):
            pe.matmul(o, lh, rh, start=start, stop=False)
            pe.matmul(o, lh, rl, start=False, stop=False)
            return pe.matmul(o, ll, rh, start=False, stop=stop)

        def f32(ap):
            return ap.bitcast(F32)

        def rsqrt(v, dst, src):
            t1 = nt1[:, 0:src.shape[-1]]
            v.drain()
            v.tensor_scalar(dst.bitcast(I32), src.bitcast(I32), 1, None, ALU.logical_shift_right)
            v.drain()
            v.tensor_scalar(dst.bitcast(I32), dst.bitcast(I32), -1.0, 1597463007.0, ALU.mult, ALU.add)
            for _ in range(3):
                v.drain()
                v.tensor_tensor(t1, dst, dst, ALU.mult)
                v.drain()
                v.scalar_tensor_tensor(out=t1, in0=t1, scalar=-0.5, in1=src, op0=ALU.mult, op1=ALU.mult)
                v.drain()
                v.scalar_tensor_tensor(out=dst, in0=t1, scalar=1.5, in1=dst, op0=ALU.add, op1=ALU.mult)
            v.drain()

        NG = NT // 2

        def ln_order(n):
            return list(range(NT - 1, -1, -1)) if n == 1 else list(range(NT))

        def ln_step(v, b, n, src, k):
            order = ln_order(n)
            if n == 0:
                if k == 0:
                    v.wait_ge(s_xin, b * 16 + 16)
            else:
                v.wait_ge(s_xu, b * (NPH * NT) + (n - 1) * NT + k + 1)
            v.bn_stats(st[:, order[k], :], src[:, order[k], :])
            if k % 4 < 3:
                return
            four = order[k - 3:k + 1]
            lo = min(four)
            v.drain()
            for t in four:
                v.bn_aggr(ag[:, t, :], st[:, t, :])
            v.drain()
            v.tensor_scalar(nv[:, lo:lo + 4], ag[:, lo:lo + 4, 1], EPS, None, ALU.add)
            rsqrt(v, rsd[:, lo:lo + 4], nv[:, lo:lo + 4])
            for t in four:
                v.tensor_scalar(xn[:, t, :], src[:, t, :], ag[:, t, 0:1], rsd[:, t:t + 1],
                                ALU.subtract, ALU.mult).then_inc(s_xn, 1)

        def ln_v(v, b, n, src):
            for k in range(NT):
                ln_step(v, b, n, src, k)

        NTR = NPH - 1

        def ln_pe(pe, b, n):
            for g in range(NG):
                pe.wait_ge(s_xn, b * (NPH * NT) + n * NT + 2 * g + 2)
                if g >= 2:
                    pe.wait_ge(s_lo, b * (NTR * NG) + n * NG + g - 1)
                bank = ps[:, 6 + g % 2, :]
                for c in range(DC):
                    for t in range(2):
                        o = bank[:, c * 256 + t * P:c * 256 + (t + 1) * P]
                        tile = min(ln_order(n)[2 * g:2 * g + 2]) + t
                        last = pe.transpose(o, xn[:, tile, c * P:(c + 1) * P], idf[:])
                last.then_inc(s_tr, 1)

        def ln_group(n, g):
            bank = ps[:, 6 + g % 2, :].rearrange("p (c t) -> p c t", c=DC)
            first = min(ln_order(n)[2 * g:2 * g + 2])
            cols = slice(first * P, (first + 2) * P)
            return bank, cols

        def ln_a(s, b, n):
            for g in range(NG):
                bank, cols = ln_group(n, g)
                s.wait_ge(s_tr, b * (NTR * NG) + n * NG + g + 1)
                s.copy(xTh[:, :, cols], bank).then_inc(s_hi, 1)

        def ln_lo(v, b, n):
            for g in range(NG):
                bank, cols = ln_group(n, g)
                v.wait_ge(s_hi, b * (NTR * NG) + n * NG + g + 1)
                v.tensor_tensor(xTl[:, :, cols], bank, f32(xTh[:, :, cols]), ALU.subtract).then_inc(s_lo, 1)

        def ln_done(b, n):
            return b * (NTR * NG) + n * NG + NG

        class Attention:
            def __init__(self, name, width, probs, probsT, free, split):
                self.w = width
                self.pe_, self.pt_ = probs, probsT
                self.free = free
                self.split = split
                self.s = {k: sem(f"{name}_{k}") for k in ("score", "soft", "max", "exp", "tp", "eva", "evv", "pv", "o", "rc", "p1", "p2")}

        def blocks(heads):
            return [(h, i) for h in range(heads) for i in range(NT - 1, -1, -1)]

        def banks_of(k):
            return ps[:, 2 * (k % 2):2 * (k % 2) + 2, :].rearrange("p a b -> p (a b)")

        def pieces(i):
            n = i + 1
            return [(j0, min(n, j0 + 4), (j0 // 4 + i) % 2 == 0) for j0 in range(0, n, 4)]

        def banks_used(i):
            return i // 4 + 1

        def parts_before(bl, k):
            return sum(banks_used(i) for _, i in bl[:k])

        def count_pieces(bl, upto):
            act = sum(1 for _, i in bl[:upto] for p_ in pieces(i) if p_[2])
            vec = sum(1 for _, i in bl[:upto] for p_ in pieces(i) if not p_[2])
            return act, vec

        def att_pe(pe, at, bl, base, q, k1, k2, val, hooks={}):
            n_bl = len(bl)
            n_act, n_vec = count_pieces(bl, n_bl)
            n_pc = parts_before(bl, n_bl)

            def hook(name, k):
                if (name, k) in hooks:
                    hooks[name, k]()

            def score(k):
                h, i = bl[k]
                n = (i + 1) * P
                if k >= 2:
                    pe.wait_ge(at.s[at.free], base * n_bl + k - 1)
                s = banks_of(k)
                for c0 in range(0, n, HALF):
                    c1 = min(n, c0 + HALF)
                    lhs = q(h)[:, i * P:(i + 1) * P]
                    pe.matmul(s[:, c0:c1], lhs, k1(h)[:, c0:c1], start=True, stop=False)
                    last = pe.matmul(s[:, c0:c1], lhs, k2(h)[:, c0:c1], start=False, stop=c1 < n)
                last = pe.matmul(s[:, n - P:n], idb[:], causal[:], start=False, stop=True)
                last.then_inc(at.s["score"], 1)

            def copied(k):
                if at.split:
                    pe.wait_ge(at.s["p2"], base * n_pc + parts_before(bl, k))
                    return
                a, v = count_pieces(bl, k)
                if a:
                    pe.wait_ge(at.s["eva"], base * n_act + a)
                if v:
                    pe.wait_ge(at.s["evv"], base * n_vec + v)

            def turn(k):
                h, i = bl[k]
                pe.wait_ge(at.s["exp"], base * n_bl + k + 1)
                if k >= 1 and not at.split:
                    copied(k)
                for j in range(i + 1):
                    if at.split and j % 4 == 0 and k >= 1 and j <= bl[k - 1][1]:
                        pe.wait_ge(at.s["p2"], base * n_pc + parts_before(bl, k - 1) + j // 4 + 1)
                    o = ps[:, 4 + j // 4, (j % 4) * P:(j % 4 + 1) * P]
                    last = pe.transpose(o, at.pe_[:, k % 2, j * P:(j + 1) * P], idf[:])
                    if at.split and (j == i or j % 4 == 3):
                        last.then_inc(at.s["tp"], 1)
                if not at.split:
                    last.then_inc(at.s["tp"], 1)

            def pv(k):
                h, i = bl[k]
                copied(k + 1)
                if k >= 2:
                    pe.wait_ge(at.s["o"], base * n_bl + k - 1)
                o = ps[:, 6 + k % 2, 0:at.w]
                for j in range(i + 1):
                    cols = slice(j * P, (j + 1) * P)
                    if at.split:
                        parts = [(0, 0), (0, 1), (0, 2), (1, 0), (1, 1)]
                        for n, (pp, vv) in enumerate(parts):
                            last = pe.matmul(o, at.pt_[:, k % 2, pp, cols], val(h, j, vv), start=j == 0 and n == 0,
                                             stop=j == i and n == len(parts) - 1)
                    else:
                        last = pe.matmul(o, at.pt_[:, k % 2, cols], val(h, j), start=j == 0, stop=j == i)
                last.then_inc(at.s["pv"], 1)

            score(0)
            score(1)
            hook("turn", 0)
            turn(0)
            score(2)
            for k in range(n_bl):
                if k + 1 < n_bl:
                    turn(k + 1)
                hook("pv", k)
                pv(k)
                if k + 3 < n_bl:
                    score(k + 3)
                hook("end", k)

        def att_a(s, at, bl, base, src, hooks={}):
            n_bl = len(bl)

            def exp(k):
                h, i = bl[k]
                n = (i + 1) * P
                s.wait_ge(at.s["max"], base * n_bl + k + 1)
                if k >= 2:
                    s.wait_ge(at.s["tp"], base * parts_before(bl, n_bl) + parts_before(bl, k - 1) if at.split else base * n_bl + k - 1)
                    s.wait_ge(at.s["rc"], base * n_bl + k - 1)
                ins = s.activation(at.pe_[:, k % 2, 0:n], src(k)[:, 0:n], ACT.Exp, bias=nmax[:, k % 2:k % 2 + 1],
                                   accum_out=sums[:, k % 2:k % 2 + 1])
                ins.then_inc(at.s["exp"], 1)

            def copy_out(k):
                if at.split:
                    if k >= 2:
                        s.wait_ge(at.s["pv"], base * n_bl + k - 1)
                    for j in range(banks_used(bl[k][1])):
                        here = turned(bl[k][1], j)
                        s.wait_ge(at.s["tp"], base * parts_before(bl, n_bl) + parts_before(bl, k) + j + 1)
                        s.copy(at.pt_[:, k % 2, 0, here], turned_in(j, here)).then_inc(at.s["p1"], 1)
                    return
                for j0, j1, mine in pieces(bl[k][1]):
                    if mine:
                        s.wait_ge(at.s["tp"], base * n_bl + k + 1)
                        if k >= 2:
                            s.wait_ge(at.s["pv"], base * n_bl + k - 1)
                        s.copy(at.pt_[:, k % 2, j0 * P:j1 * P], ps[:, 4 + j0 // 4, 0:(j1 - j0) * P]).then_inc(at.s["eva"], 1)

            exp(0)
            exp(1)
            for k in range(n_bl):
                copy_out(k)
                if 1 <= k < n_bl - 1:
                    exp(k + 1)
                if k in hooks:
                    hooks[k]()

        def turned(i, j):
            return slice(j * HALF, min((j + 1) * HALF, (i + 1) * P))

        def turned_in(j, here):
            return ps[:, 4 + j, 0:here.stop - here.start]

        def att_v(v, at, bl, base, scale_rows, finish, hooks={}):
            n_bl = len(bl)

            def maximum(k):
                h, i = bl[k]
                n = (i + 1) * P
                v.wait_ge(at.s["score"], base * n_bl + k + 1)
                if k >= 2:
                    v.wait_ge(at.s["exp"], base * n_bl + k - 1)
                src = scale_rows(k, i, n)
                v.tensor_reduce(nmax[:, k % 2:k % 2 + 1], src, AX.X, ALU.max, negate=True).then_inc(at.s["max"], 1)

            def copy_out(k):
                if at.split:
                    for j in range(banks_used(bl[k][1])):
                        here = turned(bl[k][1], j)
                        v.wait_ge(at.s["p1"], base * parts_before(bl, n_bl) + parts_before(bl, k) + j + 1)
                        v.tensor_tensor(at.pt_[:, k % 2, 1, here], turned_in(j, here), at.pt_[:, k % 2, 0, here], ALU.subtract).then_inc(at.s["p2"], 1)
                    return
                for j0, j1, mine in pieces(bl[k][1]):
                    if not mine:
                        v.wait_ge(at.s["tp"], base * n_bl + k + 1)
                        if k >= 2:
                            v.wait_ge(at.s["pv"], base * n_bl + k - 1)
                        v.tensor_copy(at.pt_[:, k % 2, j0 * P:j1 * P], ps[:, 4 + j0 // 4, 0:(j1 - j0) * P]).then_inc(at.s["evv"], 1)

            def inverse(k):
                v.wait_ge(at.s["exp"], base * n_bl + k + 1)
                if k >= 2:
                    v.wait_ge(at.s["o"], base * n_bl + k - 1)
                v.reciprocal(rec[:, k % 2:k % 2 + 1], sums[:, k % 2:k % 2 + 1]).then_inc(at.s["rc"], 1)

            def out_(k):
                v.wait_ge(at.s["rc"], base * n_bl + k + 1)
                v.wait_ge(at.s["pv"], base * n_bl + k + 1)
                finish(k, bl[k][0], bl[k][1], ps[:, 6 + k % 2, 0:at.w], rec[:, k % 2:k % 2 + 1]).then_inc(at.s["o"], 1)

            maximum(0)
            maximum(1)
            for k in range(n_bl):
                copy_out(k)
                inverse(k)
                if k + 2 < n_bl:
                    maximum(k + 2)
                if k >= 1:
                    out_(k - 1)
                if k in hooks:
                    hooks[k]()
            out_(n_bl - 1)

        a_sem = {k: sem(f"a_{k}") for k in
                 ("sh", "shv", "q", "shn", "st", "sth", "stl", "pr", "u", "ab", "sin", "ph", "y", "ya", "v", "va", "phi", "phd",
                  "pt", "k1", "k2", "qs", "drop")}
        AT0 = Attention("at0", D, A["a_pe"], A["a_pt"], "soft", False)
        bl0 = blocks(1)

        def a_pe(pe, b):
            pe.wait_ge(s_lo, ln_done(b, 0))
            for g in range(2):
                for t in range(4):
                    tok = slice((4 * g + t) * P, (4 * g + t + 1) * P)
                    o = ps[:, g, t * 66:(t + 1) * 66]
                    for c in range(DC):
                        last = mm3(pe, o, xTh[:, c, tok], xTl[:, c, tok], wsh_h[:, c, :], wsh_l[:, c, :], c == 0, c == DC - 1)
                last.then_inc(a_sem["sh"], 1)
            for g in range(4):
                if g >= 2:
                    pe.wait_ge(a_sem["va"], b * 4 + g - 1)
                for t in range(2):
                    tok = slice((2 * g + t) * P, (2 * g + t + 1) * P)
                    o = ps[:, 2 + g % 2, t * D:(t + 1) * D]
                    for c in range(DC):
                        last = mm3(pe, o, xTh[:, c, tok], xTl[:, c, tok], wvo_h[:, c, :], wvo_l[:, c, :], c == 0, c == DC - 1)
                last.then_inc(a_sem["v"], 1)
            pe.wait_ge(a_sem["shn"], b + 1)
            for g in range(2):
                for t in range(4):
                    last = pe.transpose(ps[:, 4 + g, t * P:(t + 1) * P], A["a_shn"][:, 4 * g + t, :], idf[:])
                last.then_inc(a_sem["st"], 1)
            pe.wait_ge(a_sem["stl"], b * 2 + 2)
            for g in range(2):
                cols = slice(g * HALF, (g + 1) * HALF)
                last = mm3(pe, ps[:, g, :], om_h[:], om_l[:], A["a_shTh"][:, cols], A["a_shTl"][:, cols], True, True)
                last.then_inc(a_sem["pr"], 1)
            pe.wait_ge(a_sem["ph"], b + 1)
            pe.wait_ge(a_sem["va"], b * 4 + 4)
            for t in range(NT):
                tok = slice(t * P, (t + 1) * P)
                if t >= 2:
                    pe.wait_ge(a_sem["ya"], b * NT + t - 1)
                last = mm3(pe, ps[:, 2 + t % 2, 0:ORDERS * COMB], A["a_phh"][:, tok], A["a_phl"][:, tok], wc_h[:], wc_l[:], True, True)
                last.then_inc(a_sem["y"], 1)
            pe.wait_ge(a_sem["phd"], b + 1)
            for g in range(2):
                for t in range(4):
                    last = pe.transpose(ps[:, 4 + g, t * P:(t + 1) * P], A["a_phi"][:, 4 * g + t, :], idf[:])
                last.then_inc(a_sem["pt"], 1)
            pe.wait_ge(a_sem["qs"], b * 2 + 2)
            att_pe(pe, AT0, bl0, b, lambda h: A["a_qs"], lambda h: A["a_k1"], lambda h: A["a_k2"],
                   lambda h, j: A["a_v"][:, j, :])

        def a_a(s, b):
            for g in range(4):
                s.wait_ge(a_sem["v"], b * 4 + g + 1)
                s.copy(A["a_v"][:, 2 * g:2 * g + 2, :].rearrange("p t d -> p (t d)"), ps[:, 2 + g % 2, :]).then_inc(a_sem["va"], 1)
            s.wait_ge(a_sem["shv"], b * 2 + 2)
            s.activation(A["a_q"][:], A["a_sh"][:, :, 64], ACT.Tanh).then_inc(a_sem["q"], 1)
            for g in range(2):
                s.wait_ge(a_sem["st"], b * 2 + g + 1)
                s.copy(A["a_shTh"][:, g * HALF:(g + 1) * HALF], ps[0:SHELL, 4 + g, :]).then_inc(a_sem["sth"], 1)
            s.wait_ge(a_sem["u"], b + 1)
            s.activation(A["a_r"][0:RFF, :], A["a_r"][0:RFF, :], ACT.Abs).then_inc(a_sem["ab"], 1)
            s.wait_ge(a_sem["ab"], b + 1)
            s.activation(A["a_phs"][:], A["a_r"][:], ACT.Sin, bias=cosb[:], scale=coss[:]).then_inc(a_sem["sin"], 1)
            s.wait_ge(a_sem["sin"], b + 1)
            s.copy(A["a_phh"][:], A["a_phs"][:]).then_inc(a_sem["drop"], 1)
            for t in range(NT):
                s.wait_ge(a_sem["y"], b * NT + t + 1)
                s.copy(A["a_y"][:, t, :], ps[:, 2 + t % 2, 0:ORDERS * COMB]).then_inc(a_sem["ya"], 1)
            for g in range(2):
                cols = slice(g * HALF, (g + 1) * HALF)
                s.wait_ge(a_sem["pt"], b * 2 + g + 1)
                s.copy(A["a_k1"][:, cols], ps[:, 4 + g, :]).then_inc(a_sem["k1"], 1)
            s.wait_ge(a_sem["k1"], b * 2 + 2)
            s.copy(A["a_qs"][0:64, :], f32(A["a_k1"][0:64, :])).then_inc(a_sem["qs"], 1)
            att_a(s, AT0, bl0, b, lambda k: A["a_sm"][:, k % 2, :])

        def a_v(v, b):
            for g in range(2):
                v.wait_ge(a_sem["sh"], b * 2 + g + 1)
                v.tensor_tensor(A["a_sh"][:, 4 * g:4 * g + 4, :], ps[:, g, 0:4 * 66].rearrange("p (t n) -> p t n", t=4),
                                bsh[:].unsqueeze(1).to_broadcast([P, 4, 66]), ALU.add).then_inc(a_sem["shv"], 1)
            v.drain()
            v.tensor_tensor(A["a_sq"][:], A["a_sh"][:, :, 0:SHELL], A["a_sh"][:, :, 0:SHELL], ALU.mult)
            v.drain()
            v.tensor_reduce(A["a_ss"][:], A["a_sq"][:], AX.X, ALU.add)
            v.drain()
            v.tensor_scalar(A["a_ss"][:], A["a_ss"][:], 1e-24, None, ALU.max)
            rsqrt(v, A["a_rn"][:], A["a_ss"][:])
            for o in (slice(0, SHELL), slice(SHELL, P)):
                last = v.tensor_tensor(A["a_shn"][:, :, o], A["a_sh"][:, :, 0:SHELL],
                                       A["a_rn"][:].unsqueeze(2).to_broadcast([P, NT, SHELL]), ALU.mult)
            last.then_inc(a_sem["shn"], 1)
            for g in range(2):
                cols = slice(g * HALF, (g + 1) * HALF)
                v.wait_ge(a_sem["sth"], b * 2 + g + 1)
                v.tensor_tensor(A["a_shTl"][:, cols], ps[0:SHELL, 4 + g, :], f32(A["a_shTh"][:, cols]),
                                ALU.subtract).then_inc(a_sem["stl"], 1)
            for g in range(2):
                v.wait_ge(a_sem["pr"], b * 2 + g + 1)
                v.tensor_scalar(A["a_p"][:, g * HALF:(g + 1) * HALF], ps[0:SHELL, g, :], rbias[:, 0:1], None, ALU.add)
            v.drain()
            v.tensor_scalar(A["a_k"][:], A["a_p"][:], 1.0 / (2.0 * math.pi), MAGIC, ALU.mult, ALU.add)
            v.drain()
            v.tensor_scalar(A["a_k"][:], A["a_k"][:], MAGIC, None, ALU.subtract)
            v.drain()
            v.scalar_tensor_tensor(out=A["a_p"][:], in0=A["a_k"][:], scalar=-TWO_PI_HI, in1=A["a_p"][:], op0=ALU.mult, op1=ALU.add)
            v.drain()
            v.scalar_tensor_tensor(out=A["a_p"][:], in0=A["a_k"][:], scalar=-TWO_PI_LO, in1=A["a_p"][:], op0=ALU.mult, op1=ALU.add)
            v.drain()
            v.tensor_scalar(A["a_r"][:], A["a_p"][:], -PI_BELOW, PI_BELOW, ALU.max, ALU.min).then_inc(a_sem["u"], 1)
            v.wait_ge(a_sem["drop"], b + 1)
            v.tensor_tensor(A["a_phl"][:], A["a_phs"][:], f32(A["a_phh"][:]), ALU.subtract).then_inc(a_sem["ph"], 1)
            v.wait_ge(a_sem["q"], b + 1)
            for m in range(ORDERS - 2, -1, -1):
                for t in range(NT):
                    if m == ORDERS - 2:
                        v.wait_ge(a_sem["ya"], b * NT + t + 1)
                    src = A["a_y"][:, t, (m + 1) * COMB:(m + 2) * COMB] if m == ORDERS - 2 else A["a_acc"][:, t, :]
                    dst = A["a_phi"][:, t, 0:COMB] if m == 0 else A["a_acc"][:, t, :]
                    v.scalar_tensor_tensor(out=dst, in0=src, scalar=A["a_q"][:, t:t + 1],
                                           in1=A["a_y"][:, t, m * COMB:(m + 1) * COMB], op0=ALU.mult, op1=ALU.add)
                v.drain()
            v.tensor_copy(A["a_phi"][:, :, COMB:2 * COMB], A["a_phi"][:, :, 0:COMB]).then_inc(a_sem["phd"], 1)
            for g in range(2):
                cols = slice(g * HALF, (g + 1) * HALF)
                v.wait_ge(a_sem["k1"], b * 2 + g + 1)
                v.tensor_tensor(A["a_k2"][:, cols], ps[:, 4 + g, :], f32(A["a_k1"][:, cols]), ALU.subtract)
            v.drain()
            v.tensor_copy(A["a_qs"][64:128, :], f32(A["a_k2"][64:128, :])).then_inc(a_sem["qs"], 1)
            v.wait_ge(s_xb, b * 4 + 1)

            def rows_scaled(k, i, n):
                v.tensor_tensor(A["a_sm"][:, k % 2, 0:n], banks_of(k)[:, 0:n], decay[:, T - n:T], ALU.mult).then_inc(AT0.s["soft"], 1)
                v.wait_ge(AT0.s["soft"], b * len(bl0) + k + 1)
                return A["a_sm"][:, k % 2, 0:n]

            def finish(k, h, i, o, r):
                v.scalar_tensor_tensor(out=x[:, i, :], in0=o, scalar=r, in1=x[:, i, :], op0=ALU.mult, op1=ALU.add).then_inc(s_xu, 1)
                return v.drain()

            att_v(v, AT0, bl0, b, rows_scaled, finish,
                  hooks={k: (lambda k=k: ln_step(v, b, 1, x, k - 1)) for k in range(1, NT)})
            ln_step(v, b, 1, x, NT - 1)

        class Cross:
            def __init__(self, name, n, heads, hd):
                self.n, self.h, self.hd = n, heads, hd
                self.hpc = P // hd
                self.nc_ = heads // self.hpc
                self.W = heads * CK
                self.nb = self.W // HALF
                self.pairs = heads // 2
                self.s = {k: sem(f"{name}_{k}") for k in
                          ("kv", "kvT", "bd", "m", "mh", "ml", "u", "uh", "ul", "br", "bh", "b2",
                           "sc", "mx", "sm", "ex", "su", "pn", "tp", "th", "tl", "pv")}

        C0 = Cross("x0", 1, XH0, XD0)
        C1 = Cross("x1", 4, XH1, XD1)

        def cross_w(cr):
            if cr is C0:
                return x0_wq, x0_wk, x0_wv, x0_wo, X["c_kB"], X["c_vB"], blk0
            return x1_wq, x1_wk, x1_wv, x1_wo, X["c_kC"], X["c_vC"], blk1

        def x_pe_prep(pe, cr, b):
            wq, wk, wv, wo, kB, vB, _ = cross_w(cr)
            q = cr.s
            pe.wait_ge(s_ctx, b * 48 + 48)
            pe.wait_ge(s_xu, b * (NPH * NT) + cr.n * NT)
            for j, w in enumerate((wk, wv)):
                for c in range(cr.nc_):
                    o = ps[:, j, c * CK:(c + 1) * CK]
                    pe.matmul(o, w[:, 0, c * P:(c + 1) * P], ctxT[:, 0, :], start=True, stop=False)
                    last = pe.matmul(o, w[0:64, 1, c * P:(c + 1) * P], ctxT[0:64, 1, :], start=False, stop=True)
            last.then_inc(q["kv"], 1)
            pe.wait_ge(q["bd"], b * 2 + 2)
            cw = cr.hpc * CK
            for dc in range(DC):
                for c in range(cr.nc_):
                    col = c * cw
                    o = ps[:, 2 + dc * cr.nb + col // HALF, col % HALF:col % HALF + cw]
                    last = pe.matmul(o, wq[:, c, dc * P:(dc + 1) * P], kB[:, c, 0:cw], start=True, stop=True)
            last.then_inc(q["m"], 1)
            if cr is C1:
                for c in range(2):
                    last = pe.matmul(ps[:, c, :], x1_bqb[:, c, :], kB[:, c, 0:cw], start=True, stop=True)
                last.then_inc(q["br"], 1)
            pe.wait_ge(q["ml"], b + 1)
            for g in range(cr.pairs // 2):
                for j in (2 * g, 2 * g + 1):
                    c, off = (2 * j) // cr.hpc, ((2 * j) % cr.hpc) * CK
                    o = ps[:, 2 + g, (j % 2) * D:(j % 2 + 1) * D]
                    last = pe.matmul(o, vB[:, c, off:off + P], wo[:, c, :], start=True, stop=True)
            last.then_inc(q["u"], 1)

        def x_a_prep(s, cr, b):
            q = cr.s
            sc = float(cr.hd) ** -0.5
            s.wait_ge(q["m"], b + 1)
            src = ps[:, 2:2 + DC * cr.nb, :].rearrange("p (c n) w -> p c (n w)", c=DC)
            s.activation(X["c_mh"][:, :, 0:cr.W], src, ACT.Copy, scale=sc).then_inc(q["mh"], 1)
            if cr is C1:
                s.wait_ge(q["br"], b + 1)
                s.activation(X["c_bh"][:], ps[:, 0:2, :].rearrange("p a w -> p (a w)"), ACT.Copy, scale=sc).then_inc(q["bh"], 1)
            s.wait_ge(q["u"], b + 1)
            nu = cr.pairs // 2
            s.copy(X["c_uh"][:, 0:cr.pairs, :].rearrange("p (g j) d -> p g (j d)", j=2), ps[:, 2:2 + nu, :]).then_inc(q["uh"], 1)

        def x_v_prep(v, cr, b):
            _, _, _, _, kB, vB, blk = cross_w(cr)
            q = cr.s
            sc = float(cr.hd) ** -0.5
            kT, vT = X["c_kT"][:, 0:cr.nc_, :], X["c_vT"][:, 0:cr.nc_, :]
            v.wait_ge(q["kv"], b + 1)
            pk = ps[:, 0, 0:cr.nc_ * CK].rearrange("p (c k) -> p c k", k=CK)
            pvv = ps[:, 1, 0:cr.nc_ * CK].rearrange("p (c k) -> p c k", k=CK)
            if cr is C1:
                for c in range(2):
                    v.tensor_scalar(kT[:, c, :], pk[:, c, :], x1_bk[:, c:c + 1], None, ALU.add)
                    v.tensor_scalar(vT[:, c, :], pvv[:, c, :], x1_bv[:, c:c + 1], None, ALU.add)
            else:
                v.tensor_copy(kT, pk)
                v.tensor_copy(vT, pvv)
            if cr is C1:
                v.drain().then_inc(s_used, 1)
            else:
                v.drain()
            for src, dst in ((kT, kB), (vT, vB)):
                for c in range(cr.nc_):
                    o = dst[:, c, 0:cr.hpc * CK].rearrange("p (h k) -> p h k", k=CK)
                    last = v.tensor_tensor(o, src[:, c, :].unsqueeze(1).to_broadcast([P, cr.hpc, CK]),
                                           blk[:].unsqueeze(2).to_broadcast([P, cr.hpc, CK]), ALU.mult)
                last.then_inc(q["bd"], 1)
            v.wait_ge(q["mh"], b + 1)
            for dc in range(DC):
                src = ps[:, 2 + dc * cr.nb:2 + (dc + 1) * cr.nb, :].rearrange("p n w -> p (n w)")
                last = v.scalar_tensor_tensor(out=X["c_ml"][:, dc, 0:cr.W], in0=src, scalar=sc, in1=f32(X["c_mh"][:, dc, 0:cr.W]),
                                              op0=ALU.mult, op1=ALU.subtract)
            last.then_inc(q["ml"], 1)
            if cr is C1:
                v.wait_ge(q["bh"], b + 1)
                v.scalar_tensor_tensor(out=X["c_bl"][:], in0=ps[:, 0:2, :].rearrange("p a w -> p (a w)"), scalar=sc,
                                       in1=f32(X["c_bh"][:]), op0=ALU.mult, op1=ALU.subtract)
                v.drain()
                v.tensor_scalar(X["c_bl"][:], X["c_bl"][:], row01[:, 1:2], None, ALU.mult)
                v.drain()
                v.scalar_tensor_tensor(out=X["c_b2"][:], in0=f32(X["c_bh"][:]), scalar=row01[:, 0:1], in1=X["c_bl"][:],
                                       op0=ALU.mult, op1=ALU.add).then_inc(q["b2"], 1)
            else:
                v.wait_ge(s_ctx, b * 48 + 48)
                v.tensor_scalar(mrow[:].rearrange("p (h k) -> p h k", k=CK), mrow4[:].bitcast(U8).unsqueeze(1).to_broadcast([1, XH0, CK]),
                                -MASKED, MASKED, ALU.mult, ALU.add).then_inc(q["b2"], 1)
            v.wait_ge(q["uh"], b + 1)
            nu = cr.pairs // 2
            v.tensor_tensor(X["c_ul"][:, 0:cr.pairs, :].rearrange("p (g j) d -> p g (j d)", j=2), ps[:, 2:2 + nu, :],
                            f32(X["c_uh"][:, 0:cr.pairs, :]).rearrange("p (g j) d -> p g (j d)", j=2), ALU.subtract).then_inc(q["ul"], 1)

        def x_banks(cr, t):
            return ps[:, cr.nb * (t % 2):cr.nb * (t % 2) + cr.nb, :].rearrange("p a w -> p (a w)")

        def x_pe(pe, cr, b):
            q = cr.s
            pe.wait_ge(s_lo, ln_done(b, cr.n))
            pe.wait_ge(q["ul"], b + 1)
            pe.wait_ge(q["b2"], b + 1)

            def score(t):
                tok = slice(t * P, (t + 1) * P)
                if t >= 2:
                    pe.wait_ge(q["sm"], b * NT + t - 1)
                for n in range(cr.nb):
                    cols = slice(n * HALF, (n + 1) * HALF)
                    o = x_banks(cr, t)[:, cols]
                    for c in range(DC):
                        mm3(pe, o, xTh[:, c, tok], xTl[:, c, tok], X["c_mh"][:, c, cols], X["c_ml"][:, c, cols], c == 0, False)
                    if cr is C1:
                        last = pe.matmul(o, ones_r[0:2, :], X["c_b2"][0:2, cols], start=False, stop=True)
                    else:
                        last = pe.matmul(o, ones_b[:], mrow[:], start=False, stop=True)
                last.then_inc(q["sc"], 1)

            def turn(t):
                pe.wait_ge(q["pn"], b * NT + t + 1)
                if t >= 1:
                    pe.wait_ge(q["tl"], b * NT + t)
                for j in range(cr.pairs):
                    last = pe.transpose(ps[:, 4 + j // 4, (j % 4) * P:(j % 4 + 1) * P], X["c_pn"][:, t % 2, j * P:(j + 1) * P], idf[:])
                last.then_inc(q["tp"], 1)

            def pv(t):
                pe.wait_ge(q["tl"], b * NT + t + 1)
                if t >= 2:
                    pe.wait_ge(s_xu, b * (NPH * NT) + cr.n * NT + t - 1)
                o = ps[:, 6 + t % 2, 0:D]
                for j in range(cr.pairs):
                    cols = slice(j * P, (j + 1) * P)
                    last = mm3(pe, o, X["c_th"][:, t % 2, cols], X["c_tl"][:, t % 2, cols], X["c_uh"][:, j, :], X["c_ul"][:, j, :],
                               j == 0, j == cr.pairs - 1)
                last.then_inc(q["pv"], 1)

            score(0)
            score(1)
            for t in range(NT):
                turn(t)
                if t + 2 < NT:
                    score(t + 2)
                pv(t)

        def x_a(s, cr, b):
            q = cr.s
            nb4 = cr.pairs // 4

            def exp(t):
                s.wait_ge(q["sm"], b * NT + t + 1)
                if t >= 2:
                    s.wait_ge(q["pn"], b * NT + t - 1)
                s.activation(X["c_pe"][:, t % 2, 0:cr.W], X["c_sm"][:, t % 2, 0:cr.W], ACT.Exp).then_inc(q["ex"], 1)

            exp(0)
            exp(1)
            for t in range(NT):
                s.wait_ge(q["tp"], b * NT + t + 1)
                if t >= 2:
                    s.wait_ge(q["pv"], b * NT + t - 1)
                s.copy(X["c_th"][:, t % 2, 0:cr.W], ps[:, 4:4 + nb4, :].rearrange("p a w -> p (a w)")).then_inc(q["th"], 1)
                if t + 2 < NT:
                    exp(t + 2)

        def x_v(v, cr, b):
            q = cr.s
            nb4 = cr.pairs // 4

            def soft(t):
                v.wait_ge(q["sc"], b * NT + t + 1)
                src = x_banks(cr, t).rearrange("p (h k) -> p h k", k=CK)
                v.tensor_reduce(X["c_mx"][:, t % 2, 0:cr.h], src, AX.X, ALU.max).then_inc(q["mx"], 1)
                v.wait_ge(q["mx"], b * NT + t + 1)
                if t >= 2:
                    v.wait_ge(q["ex"], b * NT + t - 1)
                v.tensor_tensor(X["c_sm"][:, t % 2, 0:cr.W].rearrange("p (h k) -> p h k", k=CK), src,
                                X["c_mx"][:, t % 2, 0:cr.h].unsqueeze(2).to_broadcast([P, cr.h, CK]), ALU.subtract).then_inc(q["sm"], 1)

            def sum_(t):
                v.wait_ge(q["ex"], b * NT + t + 1)
                if t >= 2:
                    v.wait_ge(q["pn"], b * NT + t - 1)
                v.tensor_reduce(X["c_su"][:, t % 2, 0:cr.h], X["c_pe"][:, t % 2, 0:cr.W].rearrange("p (h k) -> p h k", k=CK), AX.X, ALU.add)
                v.drain()
                v.reciprocal(X["c_re"][:, t % 2, 0:cr.h], X["c_su"][:, t % 2, 0:cr.h]).then_inc(q["su"], 1)

            soft(0)
            soft(1)
            sum_(0)
            for t in range(NT):
                if t + 1 < NT:
                    sum_(t + 1)
                v.wait_ge(q["th"], b * NT + t + 1)
                if t >= 2:
                    v.wait_ge(q["pv"], b * NT + t - 1)
                v.tensor_tensor(X["c_tl"][:, t % 2, 0:cr.W], ps[:, 4:4 + nb4, :].rearrange("p a w -> p (a w)"),
                                f32(X["c_th"][:, t % 2, 0:cr.W]), ALU.subtract).then_inc(q["tl"], 1)
                if t + 2 < NT:
                    soft(t + 2)
                if t == 0:
                    v.wait_ge(s_xb, b * 4 + (2 if cr is C0 else 4))
                v.wait_ge(q["pv"], b * NT + t + 1)
                v.tensor_tensor(x[:, t, :], x[:, t, :], ps[:, 6 + t % 2, 0:D], ALU.add).then_inc(s_xu, 1)
                ln_step(v, b, cr.n + 1, x, t)

        def x_g(g, cr, b, bias):
            q = cr.s
            g.wait_ge(s_xn, b * (NPH * NT) + (cr.n + 1) * NT)
            g.tensor_tensor(x[:], x[:], bias[:].unsqueeze(1).to_broadcast([P, NT, D]), ALU.add).then_inc(s_xb, 1)
            for t in range(NT):
                g.wait_ge(q["su"], b * NT + t + 1)
                if t >= 2:
                    g.wait_ge(q["tp"], b * NT + t - 1)
                g.tensor_tensor(X["c_pn"][:, t % 2, 0:cr.W].rearrange("p (h k) -> p h k", k=CK),
                                X["c_pe"][:, t % 2, 0:cr.W].rearrange("p (h k) -> p h k", k=CK),
                                X["c_re"][:, t % 2, 0:cr.h].unsqueeze(2).to_broadcast([P, cr.h, CK]), ALU.mult).then_inc(q["pn"], 1)

        m_sem = {k: sem(f"m_{k}") for k in
                 ("mean", "meanv", "sc", "idx", "w1", "w2", "w1h", "w1l", "w2h", "w2l", "up", "h", "hh", "hl", "dn", "seen")}

        def m_pe(pe, b):
            pe.wait_ge(s_xn, b * (NPH * NT) + 3 * NT)
            pe.wait_ge(s_xu, b * (NPH * NT) + 2 * NT)
            for c in range(DC):
                for t in range(NT):
                    last = pe.matmul(ps[:, c, 0:1], xn[:, t, c * P:(c + 1) * P], ones_f[:, 0:1], start=t == 0, stop=t == NT - 1)
            last.then_inc(m_sem["mean"], 1)
            pe.wait_ge(m_sem["meanv"], b + 1)
            for c in range(DC):
                last = pe.matmul(ps[0:1, 2, 0:EXPERTS], M["m_mean"][:, c:c + 1], wr[:, c, :], start=c == 0, stop=c == DC - 1)
            last.then_inc(m_sem["sc"], 1)
            ln_pe(pe, b, 2)
            pe.wait_ge(s_lo, ln_done(b, 2))
            pe.wait_ge(m_sem["w1l"], b + 1)
            for hf in range(2):
                cols = slice(hf * HALF, (hf + 1) * HALF)
                for f in range(FC):
                    n = hf * FC + f
                    if n >= 4:
                        pe.wait_ge(m_sem["h"], b * 2 * FC + n - 3)
                    o = ps[:, n % 4, :]
                    fs = slice(f * P, (f + 1) * P)
                    for c in range(DC):
                        last = mm3(pe, o, M["m_w1h"][:, c, fs], M["m_w1l"][:, c, fs], xTh[:, c, cols], xTl[:, c, cols], c == 0, c == DC - 1)
                    last.then_inc(m_sem["up"], 1)
                if hf == 0:
                    pe.wait_ge(m_sem["w2l"], b + 1)
                pe.wait_ge(m_sem["hl"], b * 2 * FC + (hf + 1) * FC)
                for t in range(4):
                    n = hf * 4 + t
                    if n >= 2:
                        pe.wait_ge(s_xu, b * (NPH * NT) + 2 * NT + n - 1)
                    o = ps[:, 4 + n % 2, 0:D]
                    for f in range(FC):
                        tok = slice(t * P, (t + 1) * P)
                        last = mm3(pe, o, M["m_hh"][:, f, tok], M["m_hl"][:, f, tok], M["m_w2h"][:, f, :], M["m_w2l"][:, f, :],
                                   f == 0, f == FC - 1)
                    last.then_inc(m_sem["dn"], 1)

        def m_a(s, b):
            ln_a(s, b, 2)
            s.wait_ge(m_sem["w1"], b * 48 + 48)
            s.copy(M["m_w1h"][:], M["m_w1"][:]).then_inc(m_sem["w1h"], 1)
            s.wait_ge(m_sem["w2"], b * 16 + 16)
            s.copy(M["m_w2h"][:], M["m_w2"][:]).then_inc(m_sem["w2h"], 1)
            for n in range(2 * FC):
                s.wait_ge(m_sem["up"], b * 2 * FC + n + 1)
                if n >= 2:
                    s.wait_ge(m_sem["hl"], b * 2 * FC + n - 1)
                s.activation(M["m_h"][:, n % 2, :], ps[:, n % 4, :], ACT.Relu, bias=M["m_b1"][:, n % FC:n % FC + 1]).then_inc(m_sem["h"], 1)

        def m_v(v, b):
            v.wait_ge(m_sem["mean"], b + 1)
            v.tensor_scalar(M["m_mean"][:], ps[:, 0:2, 0], 1.0 / T, None, ALU.mult).then_inc(m_sem["meanv"], 1)
            v.wait_ge(m_sem["sc"], b + 1)
            v.tensor_tensor(M["m_sc"][:], ps[0:1, 2, 0:EXPERTS], br[:], ALU.add)
            v.drain()
            v.max(M["m_top"][:], M["m_sc"][:])
            v.drain()
            v.max_index(M["m_idx"][:], M["m_top"][:], M["m_sc"][:]).then_inc(m_sem["idx"], 1)
            ln_lo(v, b, 2)
            v.wait_ge(m_sem["w1h"], b + 1)
            v.tensor_tensor(M["m_w1l"][:], M["m_w1"][:], f32(M["m_w1h"][:]), ALU.subtract).then_inc(m_sem["w1l"], 1)
            v.wait_ge(m_sem["w2h"], b + 1)
            v.tensor_tensor(M["m_w2l"][:], M["m_w2"][:], f32(M["m_w2h"][:]), ALU.subtract).then_inc(m_sem["w2l"], 1)
            v.wait_ge(s_xb, b * 4 + 3)
            for n in range(2 * FC):
                v.wait_ge(m_sem["h"], b * 2 * FC + n + 1)
                if n == FC:
                    v.wait_ge(m_sem["dn"], b * NT + 4)
                v.tensor_copy(M["m_hh"][:, n % FC, :], M["m_h"][:, n % 2, :]).then_inc(m_sem["hh"], 1)
                v.wait_ge(m_sem["hh"], b * 2 * FC + n + 1)
                v.tensor_tensor(M["m_hl"][:, n % FC, :], M["m_h"][:, n % 2, :], f32(M["m_hh"][:, n % FC, :]), ALU.subtract).then_inc(m_sem["hl"], 1)
                if n % FC == FC - 1:
                    for t in range(4):
                        k = n // FC * 4 + t
                        v.wait_ge(m_sem["dn"], b * NT + k + 1)
                        v.tensor_tensor(x[:, k, :], x[:, k, :], ps[:, 4 + k % 2, 0:D], ALU.add).then_inc(s_xu, 1)
                        ln_step(v, b, 3, x, k)

        def m_g(g, b):
            g.wait_ge(s_xn, b * (NPH * NT) + 3 * NT)
            g.wait_ge(m_sem["w1"], b * 48 + 48)
            g.tensor_tensor(x[:], x[:], M["m_b2"][:].unsqueeze(1).to_broadcast([P, NT, D]), ALU.add).then_inc(s_xb, 1)

        def m_sp(sp, b):
            sp.wait_ge(m_sem["idx"], b + 1)
            sp.sem_inc(m_sem["seen"], 1)
            e = sp.value_load(M["m_idx"][0:1, 0:1], min_val=0, max_val=EXPERTS - 1)
            sp.dma_start(M["m_w1"][:], a["m_w1"][bass.ds(e, 1)].rearrange("o (c p) f -> p (o c) f", p=P)).then_inc(m_sem["w1"], 16)
            sp.dma_start(M["m_b1"][:], a["m_b1"][bass.ds(e, 1)].rearrange("o p f -> p (o f)")).then_inc(m_sem["w1"], 16)
            sp.dma_start(M["m_b2"][:], a["m_b2"][bass.ds(e, 1)].to_broadcast([P, D])).then_inc(m_sem["w1"], 16)
            sp.dma_start(M["m_w2"][:], a["m_w2"][bass.ds(e, 1)].rearrange("o (c p) f -> p (o c) f", p=P)).then_inc(m_sem["w2"], 16)

        AT1 = Attention("at1", SD, L["l_pe"], L["l_pt"], "exp", True)
        bl1 = blocks(2)
        l_sem = {k: sem(f"l_{k}") for k in ("w", "wh", "wl", "q", "k", "qh", "kh", "ql", "kl", "dup", "v", "va", "vr", "v2", "v3", "ot", "oh", "wo")}
        LQ = [L["l_q0"], L["l_q1"]]
        LK1 = [L["l_k10"], L["l_k11"]]
        LK2 = [L["l_k20"], L["l_k21"]]
        NB1 = len(bl1)

        def own(h):
            return (slice(0, 64), slice(64, 128)) if h == 0 else (slice(64, 128), slice(0, 64))

        def qk_banks(m):
            return ps[:, 0:2, :] if m == 0 else ps[:, 2:4, :]

        def wide(ap):
            return ap.rearrange("p (a w) -> p a w", a=2)

        def l_proj(pe, n, m, b):
            for hf in range(2):
                cols = slice(hf * HALF, (hf + 1) * HALF)
                for c in range(DC):
                    last = mm3(pe, qk_banks(m)[:, hf, :], L["l_wh"][:, m, c, :], L["l_wl"][:, m, c, :], xTh[:, c, cols], xTl[:, c, cols],
                               c == 0, c == DC - 1)
            last.then_inc(l_sem["q" if m == 0 else "k"], 1)

        def l_values(pe, g):
            for t in range(4):
                tok = slice((4 * g + t) * P, (4 * g + t + 1) * P)
                for c in range(DC):
                    last = mm3(pe, ps[:, 5 - g, t * P:(t + 1) * P], xTh[:, c, tok], xTl[:, c, tok], L["l_wh"][:, 2, c, :],
                               L["l_wl"][:, 2, c, :], c == 0, c == DC - 1)
            last.then_inc(l_sem["v"], 1)

        def l_w_a(s, n):
            s.wait_ge(l_sem["w"], n * 16 + 16)
            s.copy(L["l_wh"][:], L["l_w"][:]).then_inc(l_sem["wh"], 1)

        def l_w_v(v, n):
            v.wait_ge(l_sem["wh"], n + 1)
            v.tensor_tensor(L["l_wl"][:], L["l_w"][:], f32(L["l_wh"][:]), ALU.subtract).then_inc(l_sem["wl"], 1)

        def l_q_a(s, n):
            s.wait_ge(l_sem["q"], n + 1)
            for h in range(2):
                mine, _ = own(h)
                s.activation(wide(LQ[h][mine, :]), qk_banks(0)[mine], ACT.Copy, scale=0.125).then_inc(l_sem["qh"], 1)

        def l_k_a(s, n):
            s.wait_ge(l_sem["k"], n + 1)
            for h in range(2):
                mine, _ = own(h)
                s.copy(wide(LK1[h][mine, :]), qk_banks(1)[mine]).then_inc(l_sem["kh"], 1)

        def l_q_v(v, n):
            for h in range(2):
                mine, other = own(h)
                v.wait_ge(l_sem["qh"], n * 2 + h + 1)
                v.scalar_tensor_tensor(out=wide(LQ[h][other, :]), in0=qk_banks(0)[mine], scalar=0.125, in1=wide(f32(LQ[h][mine, :])),
                                       op0=ALU.mult, op1=ALU.subtract).then_inc(l_sem["ql"], 1)

        def l_k_v(v, n):
            for h in range(2):
                mine, _ = own(h)
                v.wait_ge(l_sem["kh"], n * 2 + h + 1)
                v.tensor_tensor(wide(LK2[h][mine, :]), qk_banks(1)[mine], wide(f32(LK1[h][mine, :])), ALU.subtract).then_inc(l_sem["kl"], 1)

        def l_k_sp(sp, n):
            for h in range(2):
                mine, other = own(h)
                sp.wait_ge(l_sem["kl"], n * 2 + h + 1)
                sp.dma_start(f32(LK1[h][other, :]), f32(LK1[h][mine, :])).then_inc(l_sem["dup"], 16)
                sp.dma_start(f32(LK2[h][other, :]), f32(LK2[h][mine, :])).then_inc(l_sem["dup"], 16)

        def l_v_a(s, n, pair_before):
            for g in range(2):
                s.wait_ge(l_sem["v"], n * 2 + g + 1)
                if pair_before is not None:
                    s.wait_ge(AT1.s["pv"], pair_before)
                s.copy(L["l_v"][:, 0, 4 * g:4 * g + 4, :].rearrange("p t d -> p (t d)"), ps[:, 5 - g, :]).then_inc(l_sem["va"], 1)

        def l_v_v(v, n):
            for g in range(2):
                t4 = slice(4 * g, 4 * g + 4)
                v.wait_ge(l_sem["va"], n * 2 + g + 1)
                v.tensor_tensor(L["l_vr"][:, t4, :].rearrange("p t d -> p (t d)"), ps[:, 5 - g, :],
                                L["l_v"][:, 0, t4, :].rearrange("p t d -> p (t d)"), ALU.subtract).then_inc(l_sem["vr"], 1)
                v.wait_ge(l_sem["vr"], n * 2 + g + 1)
                v.tensor_copy(L["l_v"][:, 1, t4, :], L["l_vr"][:, t4, :]).then_inc(l_sem["v2"], 1)

        def l_v_g(g_, n):
            for g in range(2):
                t4 = slice(4 * g, 4 * g + 4)
                g_.wait_ge(l_sem["v2"], n * 2 + g + 1)
                g_.tensor_tensor(L["l_v"][:, 2, t4, :], L["l_vr"][:, t4, :], L["l_v"][:, 1, t4, :], ALU.subtract).then_inc(l_sem["v3"], 1)

        def l_pe_first(pe, b):
            n = b * HP
            pe.wait_ge(s_lo, ln_done(b, 3))
            pe.wait_ge(l_sem["wl"], n + 2)
            l_proj(pe, n, 0, b)
            l_proj(pe, n, 1, b)
            l_values(pe, 0)
            l_values(pe, 1)

        def l_pe_body(pe, it, b, more):
            pe.wait_ge(l_sem["ql"], it * 2 + 2)
            pe.wait_ge(l_sem["dup"], it * 64 + 64)

            def before_turn():
                pe.wait_ge(l_sem["vr"], it * 2 + 2)

            def before_pv():
                pe.wait_ge(l_sem["v3"], it * 2 + 2)

            def before_pv0():
                before_pv()
                pe.wait_ge(l_sem["oh"], it * 2 + 2)

            def next_q():
                pe.wait_ge(l_sem["wl"], it + 3)
                pe.wait_ge(AT1.s["exp"], it * NB1 + NB1 - 1)
                l_proj(pe, it + 1, 0, b)

            def next_kv():
                pe.wait_ge(AT1.s["exp"], it * NB1 + NB1)
                l_proj(pe, it + 1, 1, b)
                l_values(pe, 0)

            hooks = {("turn", 0): before_turn, ("pv", 0): before_pv0}
            if more:
                hooks["end", NB1 - 3] = next_q
                hooks["end", NB1 - 2] = next_kv
            att_pe(pe, AT1, bl1, it, lambda h: LQ[h], lambda h: LK1[h], lambda h: LK2[h],
                   lambda h, j, part: L["l_v"][:, part, j, h * SD:(h + 1) * SD], hooks)
            if more:
                l_values(pe, 1)
            pe.wait_ge(AT1.s["o"], it * NB1 + NB1)
            for g in range(2):
                for t in range(4):
                    last = pe.transpose(ps[:, 6 + g, t * P:(t + 1) * P], L["l_o"][:, 4 * g + t, :], idf[:])
                last.then_inc(l_sem["ot"], 1)

        def l_a_first(s, b):
            n = b * HP
            l_w_a(s, n)
            l_q_a(s, n)
            l_k_a(s, n)
            l_v_a(s, n, None)

        def l_a_body(s, it, hp, more):
            hooks = {}
            if more:
                hooks = {5: lambda: l_w_a(s, it + 1), NB1 - 3: lambda: l_q_a(s, it + 1), NB1 - 2: lambda: l_k_a(s, it + 1)}
            att_a(s, AT1, bl1, it, banks_of, hooks)
            if more:
                l_v_a(s, it + 1, it * NB1 + NB1)
            for g in range(2):
                s.wait_ge(l_sem["ot"], it * 2 + g + 1)
                s.copy(L["l_oT"][:, bass.ds(hp, 1), g * HALF:(g + 1) * HALF].rearrange("p o w -> p (o w)"),
                       ps[:, 6 + g, :]).then_inc(l_sem["oh"], 1)

        def l_v_first(v, b):
            n = b * HP
            l_w_v(v, n)
            l_q_v(v, n)
            l_k_v(v, n)
            l_v_v(v, n)

        def l_v_body(v, it, more):
            def plain(k, i, n_):
                return banks_of(k)[:, 0:n_]

            def finish(k, h, i, o, r):
                return v.tensor_scalar(L["l_o"][:, i, h * SD:(h + 1) * SD], o, r, None, ALU.mult)

            hooks = {}
            if more:
                hooks = {5: lambda: l_w_v(v, it + 1), NB1 - 3: lambda: l_q_v(v, it + 1), NB1 - 2: lambda: l_k_v(v, it + 1)}
            att_v(v, AT1, bl1, it, plain, finish, hooks)
            if more:
                l_v_v(v, it + 1)

        def l_pe_end(pe, b):
            pe.wait_ge(l_sem["oh"], b * 2 * HP + 2 * HP + 2)
            for t in range(NT):
                tok = slice(t * P, (t + 1) * P)
                if t >= 2:
                    pe.wait_ge(s_xu, b * (NPH * NT) + 3 * NT + t - 1)
                for c in range(HP):
                    last = pe.matmul(ps[:, 6 + t % 2, 0:D], L["l_oT"][:, c, tok], wo[:, c, :], start=c == 0, stop=c == HP - 1)
                last.then_inc(l_sem["wo"], 1)

        def l_v_end(v, b):
            for t in range(NT):
                v.wait_ge(l_sem["wo"], b * NT + t + 1)
                v.tensor_tensor(x[:, t, :], x[:, t, :], ps[:, 6 + t % 2, 0:D], ALU.add).then_inc(s_xu, 1)
                ln_step(v, b, 4, x, t)

        g_sem = {k: sem(f"g_{k}") for k in ("xq", "tp", "xT", "gt", "up", "si", "gh", "h", "hq", "ht", "hT", "dn")}

        def psb(bank):
            return ps[:, bank, :].bitcast(BF16)

        def g_pe(pe, b):
            for g in range(2):
                pe.wait_ge(g_sem["xq"], b * NT + 4 * g + 4)
                o = psb(6 + g)
                for c in range(DC):
                    for t in range(4):
                        last = pe.transpose(o[:, c * HALF + t * P:c * HALF + (t + 1) * P], G["g_xq"][:, 4 * g + t, c * P:(c + 1) * P], idb[:])
                last.then_inc(g_sem["tp"], 1)
            pe.wait_ge(g_sem["xT"], b * 2 + 2)

            def updown(t):
                tok = slice(t * P, (t + 1) * P)
                for m, w in ((0, wg_q), (1, wu_q)):
                    if t >= 1:
                        pe.wait_ge(g_sem["si" if m == 0 else "gh"], b * NT + t)
                    for n in range(2):
                        for c in range(DC):
                            last = pe.matmul(ps[:, 2 * m + n, :], G["g_xT"][:, c, tok], w[:, c, n * HALF:(n + 1) * HALF],
                                             start=c == 0, stop=c == DC - 1)
                    last.then_inc(g_sem["gt" if m == 0 else "up"], 1)

            def rest(t):
                pe.wait_ge(g_sem["hq"], b * NT + t + 1)
                if t >= 2:
                    pe.wait_ge(g_sem["hT"], b * NT + t - 1)
                for f in range(FC):
                    last = pe.transpose(psb(4 + t % 2)[:, f * P:(f + 1) * P], G["g_hq"][:, t % 2, f * P:(f + 1) * P], idb[:])
                last.then_inc(g_sem["ht"], 1)
                pe.wait_ge(g_sem["hT"], b * NT + t + 1)
                if t >= 2:
                    pe.wait_ge(s_xu, b * (NPH * NT) + 5 * NT + t - 1)
                for f in range(FC):
                    last = pe.matmul(ps[:, 6 + t % 2, 0:D], G["g_hT"][:, t % 2, f * P:(f + 1) * P], wd_q[:, f, :], start=f == 0, stop=f == FC - 1)
                last.then_inc(g_sem["dn"], 1)

            updown(0)
            for t in range(NT):
                if t + 1 < NT:
                    updown(t + 1)
                rest(t)

        def g_v(v, b):
            v.drain()
            v.tensor_reduce(G["g_amx"][:], xn[:], AX.X, ALU.max, apply_absolute_value=True)
            v.drain()
            v.tensor_scalar(G["g_amx"][:], G["g_amx"][:], EPS, None, ALU.max)
            v.drain()
            v.tensor_scalar(G["g_inv"][:], G["g_amx"][:], 1.0 / 127.0, None, ALU.mult)
            v.drain()
            v.reciprocal(G["g_s"][:], G["g_inv"][:])
            v.tensor_scalar(G["g_ig"][:], G["g_inv"][:], wsc[:, 0:1], None, ALU.mult)
            v.tensor_scalar(G["g_iu"][:], G["g_inv"][:], wsc[:, 1:2], None, ALU.mult)
            v.drain()
            for t in range(NT):
                v.tensor_scalar(G["g_t"][:, t % 2, :], xn[:, t, :], G["g_s"][:, t:t + 1], MAGIC, ALU.mult, ALU.add)
                v.drain()
                v.tensor_scalar(G["g_xq"][:, t, :], G["g_t"][:, t % 2, :], MAGIC, 127.0, ALU.subtract, ALU.min).then_inc(g_sem["xq"], 1)

            def hidden(t):
                v.wait_ge(g_sem["up"], b * NT + t + 1)
                v.wait_ge(g_sem["si"], b * NT + t + 1)
                v.scalar_tensor_tensor(out=G["g_h"][:, t % 2, :], in0=ps[:, 2:4, :].rearrange("p a w -> p (a w)"), scalar=G["g_iu"][:, t:t + 1],
                                       in1=G["g_g"][:, t % 2, :], op0=ALU.mult, op1=ALU.mult).then_inc(g_sem["gh"], 1)
                hm, hs, hi = G["g_hm"][:, t % 2:t % 2 + 1], G["g_hs"][:, t % 2:t % 2 + 1], G["g_hi"][:, t % 2:t % 2 + 1]
                v.drain()
                v.tensor_reduce(hm, G["g_h"][:, t % 2, :], AX.X, ALU.max, apply_absolute_value=True)
                v.drain()
                v.tensor_scalar(hm, hm, EPS, 1.0 / 127.0, ALU.max, ALU.mult)
                v.drain()
                v.reciprocal(hs, hm)
                v.tensor_scalar(hi, hm, wsc[:, 2:3], None, ALU.mult)
                v.drain()
                v.tensor_scalar(G["g_r"][:, t % 2, :], G["g_h"][:, t % 2, :], hs, MAGIC, ALU.mult, ALU.add)
                v.drain()
                v.tensor_scalar(G["g_hq"][:, t % 2, :], G["g_r"][:, t % 2, :], MAGIC, 127.0, ALU.subtract, ALU.min).then_inc(g_sem["hq"], 1)

            hidden(0)
            for t in range(NT):
                if t + 1 < NT:
                    hidden(t + 1)
                v.wait_ge(g_sem["dn"], b * NT + t + 1)
                v.scalar_tensor_tensor(out=x[:, t, :], in0=ps[:, 6 + t % 2, 0:D], scalar=G["g_hi"][:, t % 2:t % 2 + 1],
                                       in1=x[:, t, :], op0=ALU.mult, op1=ALU.add).then_inc(s_xu, 1)

        def g_a(s, b):
            for g in range(2):
                s.wait_ge(g_sem["tp"], b * 2 + g + 1)
                s.copy(G["g_xT"][:, :, g * HALF:(g + 1) * HALF], psb(6 + g).rearrange("p (c w) -> p c w", c=DC)).then_inc(g_sem["xT"], 1)

            def silu(t):
                s.wait_ge(g_sem["gt"], b * NT + t + 1)
                if t >= 2:
                    s.wait_ge(g_sem["gh"], b * NT + t - 1)
                s.activation(G["g_g"][:, t % 2, :], ps[:, 0:2, :].rearrange("p a w -> p (a w)"), ACT.Silu,
                             scale=G["g_ig"][:, t:t + 1]).then_inc(g_sem["si"], 1)

            silu(0)
            for t in range(NT):
                if t + 1 < NT:
                    silu(t + 1)
                s.wait_ge(g_sem["ht"], b * NT + t + 1)
                if t >= 2:
                    s.wait_ge(g_sem["dn"], b * NT + t - 1)
                s.copy(G["g_hT"][:, t % 2, :], psb(4 + t % 2)).then_inc(g_sem["hT"], 1)

        loads = [
            (S["s_wsh"][:], a["a_wsh"].rearrange("(c p) n -> p c n", p=P)), (S["s_om"][:], a["a_om"]), (S["s_wc"][:], a["a_wc"]),
            (S["s_wv"][:], a["a_wv"].rearrange("(c p) n -> p c n", p=P)), (S["s_wo"][:], a["a_wo"].rearrange("(c p) n -> p c n", p=P)),
            (S["s_bv"][:], a["a_bv"]), (S["s_bo"][:], rows(a["a_bo"])), (S["s_lt"][:], rows(a["a_lt"])),
            (bsh[:], rows(a["a_bsh"])), (rbias[:], a["a_rb"].rearrange("(p o) -> p o", o=1)),
            (S["s_g"][:].rearrange("p (c n) -> p c n", c=DC), a["g_wg"].rearrange("(c p) n -> p c n", p=P)),
            (S["s_u"][:].rearrange("p (c n) -> p c n", c=DC), a["g_wu"].rearrange("(c p) n -> p c n", p=P)),
            (S["s_d"][:].rearrange("p (c n) -> p c n", c=FC), a["g_wd"].rearrange("(c p) n -> p c n", p=P)),
            (wo[:], a["l_wo"].rearrange("(c p) n -> p c n", p=P)),
            (x0_wq[:], a["x0_wq"].rearrange("(c p) n -> p c n", p=P)), (x0_wk[:, 0, :], a["x0_wk"][0:P]), (x0_wk[0:64, 1, :], a["x0_wk"][P:CTX]),
            (x0_wv[:, 0, :], a["x0_wv"][0:P]), (x0_wv[0:64, 1, :], a["x0_wv"][P:CTX]),
            (x0_wo[:], a["x0_wo"].rearrange("(c p) n -> p c n", p=P)), (x0_bo[:], rows(a["x0_bo"])),
            (x1_wq[:], a["x1_wq"].rearrange("(c p) n -> p c n", p=P)), (x1_wk[:, 0, :], a["x1_wk"][0:P]), (x1_wk[0:64, 1, :], a["x1_wk"][P:CTX]),
            (x1_wv[:, 0, :], a["x1_wv"][0:P]), (x1_wv[0:64, 1, :], a["x1_wv"][P:CTX]),
            (x1_wo[:], a["x1_wo"].rearrange("(c p) n -> p c n", p=P)), (x1_bo[:], rows(a["x1_bo"])),
            (x1_bk[:], a["x1_bk"]), (x1_bv[:], a["x1_bv"]),
            (x1_bq[:], a["x1_bq"]),
            (wr[:], a["m_wr"].rearrange("(c p) n -> p c n", p=P)), (br[:], a["m_br"].rearrange("(o n) -> o n", o=1)),
        ]

        def setup_g(g):
            g.iota(S["s_iota"][:], pattern=[[-1, T]], base=T - P, channel_multiplier=1)
            g.iota(S["s_pi"][:], pattern=[[0, 1]], base=0, channel_multiplier=1)
            g.memset(idf[:], 0.0).then_inc(s_gc, 1)
            g.memset(ones_f[:], 1.0).then_inc(s_gc, 1)
            g.memset(S["s_m"][:], 0.0).then_inc(s_gc, 1)
            g.memset(causal[:], 0.0).then_inc(s_gc, 1)
            g.memset(row01[:], 0.0).then_inc(s_gc, 1)
            g.memset(blk0[:], 1.0).then_inc(s_gc, 1)
            g.memset(blk1[:], 1.0).then_inc(s_gc, 1)
            g.memset(cosb[:], 0.0).then_inc(s_gc, 1)
            g.memset(ones_b[:], 1.0).then_inc(s_gc, 1)
            g.memset(coss[:], 1.0).then_inc(s_gc, 1)
            g.wait_ge(s_gc, 10)
            g.affine_select(out=idf[:], in_=idf[:], compare_op=ALU.not_equal, fill=1.0, base=0, pattern=[[-1, P]], channel_multiplier=1).then_inc(s_gc, 1)
            g.affine_select(out=causal[:], in_=causal[:], compare_op=ALU.is_ge, fill=NEG, base=0, pattern=[[-1, P]], channel_multiplier=1).then_inc(s_gc, 1)
            g.affine_select(out=row01[:], in_=row01[:], compare_op=ALU.not_equal, fill=1.0, base=0, pattern=[[-1, 2]], channel_multiplier=1).then_inc(s_gc, 1)
            for blk, n, w in ((blk0, 2, XD0), (blk1, 8, XD1)):
                g.affine_select(out=blk[:], in_=blk[:], compare_op=ALU.is_ge, fill=0.0, base=0, pattern=[[-w, n]], channel_multiplier=1).then_inc(s_gc, 1)
            g.affine_select(out=cosb[:], in_=cosb[:], compare_op=ALU.is_ge, fill=math.pi / 2, base=-RFF, pattern=[[0, 1]], channel_multiplier=1).then_inc(s_gc, 1)
            g.affine_select(out=coss[:], in_=coss[:], compare_op=ALU.is_ge, fill=-1.0, base=-RFF, pattern=[[0, 1]], channel_multiplier=1).then_inc(s_gc, 1)
            g.wait_ge(s_gc, 17)
            for blk, n, w in ((blk0, 2, XD0), (blk1, 8, XD1)):
                g.affine_select(out=blk[:], in_=blk[:], compare_op=ALU.is_ge, fill=0.0, base=w - 1, pattern=[[w, n]], channel_multiplier=-1).then_inc(s_gc, 1)
            g.tensor_copy(idb[:], idf[:]).then_inc(s_gc, 1)

        GC = 20

        def setup_a(s):
            s.wait_ge(s_w, 16 * len(loads))
            s.wait_ge(s_gc, GC)
            s.activation(S["s_t"][:, 0:1], S["s_lt"][:], ACT.Abs).then_inc(s_sa, 1)
            s.wait_ge(s_sa, 1)
            s.activation(S["s_t"][:, 1:2], S["s_t"][:, 0:1], ACT.Exp, scale=-1.0).then_inc(s_sa, 1)
            s.wait_ge(s_sa, 2)
            s.activation(S["s_t"][:, 2:3], S["s_t"][:, 1:2], ACT.Ln, bias=1.0).then_inc(s_sa, 1)
            s.wait_ge(s_sv, 1)
            s.activation(S["s_dist"][:], S["s_dist"][:], ACT.Abs)
            s.drain()
            s.activation(S["s_dist"][:], S["s_dist"][:], ACT.Exp, scale=-0.3 / 10.0).then_inc(s_sa, 1)
            s.copy(wsh_h[:], S["s_wsh"][:]).then_inc(s_sa, 1)
            s.copy(om_h[:], S["s_om"][:]).then_inc(s_sa, 1)
            s.wait_ge(s_sv, 2)
            s.copy(wc_h[:], S["s_wc"][:].rearrange("p m o -> p (m o)")).then_inc(s_sa, 1)
            s.copy(ones_r[:], ones_f[0:2, :]).then_inc(s_sa, 1)
            s.wait_ge(s_sp, 1)
            s.copy(wvo_h[:], ps[:, 0, :].rearrange("p (c d) -> p c d", c=DC)).then_inc(s_sa, 1)

        SA = 9

        def setup_v(v):
            v.wait_ge(s_w, 16 * len(loads))
            v.wait_ge(s_gc, GC)
            v.tensor_copy(S["s_dist"][:], S["s_iota"][:]).then_inc(s_sv, 1)
            scale = math.sqrt(2.0 / (2 * RFF)) * math.sqrt(math.exp(-0.5))
            for m in range(ORDERS):
                last = v.tensor_scalar(S["s_wc"][:, m, :], S["s_wc"][:, m, :], scale * math.sqrt(1.0 / math.factorial(m) + 1e-10), None, ALU.mult)
            last.then_inc(s_sv, 1)
            for c in range(DC):
                v.tensor_scalar(S["s_bvb"][:, c, :], ones_f[:], S["s_bv"][:, c:c + 1], None, ALU.mult)
                last = v.tensor_scalar(x1_bqb[:, c, :], ones_f[:], x1_bq[:, c:c + 1], None, ALU.mult)
            last.then_inc(s_sv, 1)
            v.wait_ge(s_sa, 4)
            v.tensor_scalar(S["s_t"][:, 3:4], S["s_lt"][:], 0.0, 0.1, ALU.max, ALU.add)
            v.drain()
            v.tensor_tensor(S["s_t"][:, 3:4], S["s_t"][:, 3:4], S["s_t"][:, 2:3], ALU.add)
            v.drain()
            v.reciprocal(S["s_t"][:, 0:1], S["s_t"][:, 3:4])
            v.drain()
            v.tensor_scalar(decay[:], S["s_dist"][:], S["s_t"][:, 0:1], None, ALU.mult)
            v.wait_ge(s_sa, 7)
            v.tensor_tensor(wsh_l[:], S["s_wsh"][:], f32(wsh_h[:]), ALU.subtract)
            v.tensor_tensor(om_l[:], S["s_om"][:], f32(om_h[:]), ALU.subtract)
            v.tensor_tensor(wc_l[:], S["s_wc"][:].rearrange("p m o -> p (m o)"), f32(wc_h[:]), ALU.subtract)
            for n, w in enumerate(("s_g", "s_u", "s_d")):
                last = v.tensor_reduce(S["s_abs"][:, n:n + 1], S[w][:], AX.X, ALU.add, apply_absolute_value=True)
            last.then_inc(s_sv, 1)
            v.wait_ge(s_sp, 1)
            v.tensor_scalar(wsc[:, 0:3], ps[:, 1, 0:3], 1.0 / (D * FF), EPS, ALU.mult, ALU.max)
            v.drain()
            v.reciprocal(S["s_i8"][:, 0:3], wsc[:, 0:3])
            v.drain()
            for n, (w, q) in enumerate((("s_g", wg_q), ("s_u", wu_q), ("s_d", wd_q))):
                v.tensor_scalar(S["s_q"][:], S[w][:], S["s_i8"][:, n:n + 1], MAGIC, ALU.mult, ALU.add)
                v.drain()
                v.tensor_scalar(S["s_q"][:], S["s_q"][:], MAGIC, 1.0, ALU.subtract, ALU.min)
                v.drain()
                v.tensor_scalar(q[:].rearrange("p c n -> p (c n)"), S["s_q"][:], -1.0, None, ALU.max)
                v.drain()
            v.wait_ge(s_sa, SA)
            v.tensor_tensor(wvo_l[:], ps[:, 0, :].rearrange("p (c d) -> p c d", c=DC), f32(wvo_h[:]), ALU.subtract)
            v.tensor_tensor(bvo[:], ps[:, 2, 0:D], S["s_bo"][:], ALU.add).then_inc(s_sv, 1)

        SV = 5

        def setup_pe(pe):
            pe.wait_ge(s_w, 16 * len(loads))
            pe.wait_ge(s_sv, 4)
            for c in range(DC):
                for k in range(DC):
                    pe.matmul(ps[:, 0, c * D:(c + 1) * D], S["s_wv"][:, k, c * P:(c + 1) * P], S["s_wo"][:, k, :], start=k == 0, stop=k == DC - 1)
            for k in range(DC):
                pe.matmul(ps[:, 2, 0:D], S["s_bvb"][:, k, :], S["s_wo"][:, k, :], start=k == 0, stop=k == DC - 1)
            pe.matmul(ps[:, 1, 0:3], ones_f[:], S["s_abs"][:, 0:3], start=True, stop=True).then_inc(s_sp, 1)

        block = ctx.enter_context(nc.Block())

        @block.sync
        def _(sp):
            for dst, src in loads:
                sp.dma_start(dst, src).then_inc(s_w, 16)
            sp.sem_inc(s_used, 1)
            sp.sem_inc(l_sem["wl"], 1)
            sp.sem_inc(l_sem["oh"], 2)
            with sp.Fori(0, B) as b:
                sp.wait_ge(s_used, b + 1)
                sp.dma_start(xin[:], a["x"][bass.ds(b, 1)].rearrange("o (t p) d -> p (o t) d", p=P)).then_inc(s_xin, 16)
                sp.dma_start(ctxT[:, 0, :], a["ctxT"][bass.ds(b, 1), 0:P].rearrange("o c k -> (o c) k")).then_inc(s_ctx, 16)
                sp.dma_start(ctxT[0:64, 1, :], a["ctxT"][bass.ds(b, 1), P:CTX].rearrange("o c k -> (o c) k")).then_inc(s_ctx, 16)
                sp.dma_start(mrow4[:], a["mask"][bass.ds(b, 1)]).then_inc(s_ctx, 16)
                m_sp(sp, b)
                with sp.Fori(0, HP) as hp:
                    sp.wait_ge(s_xu, b * (NPH * NT) + 3 * NT)
                    it = b * HP + hp
                    sp.wait_ge(l_sem["wl"], it + 1)
                    sp.dma_start(L["l_w"][:], a["l_w"][bass.ds(hp, 1)].rearrange("o p m c e -> p (o m) c e")).then_inc(l_sem["w"], 16)
                    l_k_sp(sp, it)
            sp.wait_ge(s_out, 16 * B + 16)

        @block.gpsimd
        def _(g):
            setup_g(g)
            g.wait_ge(s_sv, SV)
            g.sem_inc(s_out, 16)
            with g.Fori(0, B) as b:
                g.wait_ge(s_out, b * 16 + 16)
                g.wait_ge(s_xn, b * (NPH * NT) + NT)
                g.tensor_tensor(x[:], xin[:], bvo[:].unsqueeze(1).to_broadcast([P, NT, D]), ALU.add).then_inc(s_xb, 1)
                x_g(g, C0, b, x0_bo)
                m_g(g, b)
                with g.Fori(0, HP) as hp:
                    l_v_g(g, b * HP + hp)
                x_g(g, C1, b, x1_bo)

        @block.scalar
        def _(s):
            setup_a(s)
            s.wait_ge(s_sv, SV)
            with s.Fori(0, B) as b:
                ln_a(s, b, 0)
                a_a(s, b)
                x_a_prep(s, C0, b)
                ln_a(s, b, 1)
                x_a(s, C0, b)
                m_a(s, b)
                ln_a(s, b, 3)
                l_a_first(s, b)
                with s.Fori(0, HP - 1) as hp:
                    l_a_body(s, b * HP + hp, hp, True)
                l_a_body(s, b * HP + HP - 1, HP - 1, False)
                x_a_prep(s, C1, b)
                ln_a(s, b, 4)
                x_a(s, C1, b)
                g_a(s, b)
                s.wait_ge(s_xu, b * (NPH * NT) + NPH * NT)
                s.dma_start(out[bass.ds(b, 1)].rearrange("o (t p) d -> p (o t) d", p=P), x[:]).then_inc(s_out, 16)

        @block.vector
        def _(v):
            setup_v(v)
            with v.Fori(0, B) as b:
                ln_v(v, b, 0, xin)
                ln_lo(v, b, 0)
                a_v(v, b)
                x_v_prep(v, C0, b)
                ln_lo(v, b, 1)
                x_v(v, C0, b)
                m_v(v, b)
                ln_lo(v, b, 3)
                l_v_first(v, b)
                with v.Fori(0, HP - 1) as hp:
                    l_v_body(v, b * HP + hp, True)
                l_v_body(v, b * HP + HP - 1, False)
                l_v_end(v, b)
                x_v_prep(v, C1, b)
                ln_lo(v, b, 4)
                x_v(v, C1, b)
                g_v(v, b)

        @block.tensor
        def _(pe):
            setup_pe(pe)
            pe.wait_ge(s_sv, SV)
            with pe.Fori(0, B) as b:
                ln_pe(pe, b, 0)
                a_pe(pe, b)
                x_pe_prep(pe, C0, b)
                ln_pe(pe, b, 1)
                x_pe(pe, C0, b)
                m_pe(pe, b)
                ln_pe(pe, b, 3)
                l_pe_first(pe, b)
                with pe.Fori(0, HP - 1) as hp:
                    l_pe_body(pe, b * HP + hp, b, True)
                l_pe_body(pe, b * HP + HP - 1, b, False)
                l_pe_end(pe, b)
                x_pe_prep(pe, C1, b)
                ln_pe(pe, b, 4)
                x_pe(pe, C1, b)
                g_pe(pe, b)


def kernel(**inputs):
    import numpy as np
    import concourse.bacc as bacc
    from concourse.bass_utils import run_bass_kernel_spmd

    i = {k: np.asarray(v) for k, v in inputs.items()}
    c = np.ascontiguousarray
    la, lx, lf = "L0_attn_", "L0_xattn_", "L0_ffn_"
    kx, kf = "L1_xattn_", "L1_ffn_"
    wkv = i[kx + "Wkv"].reshape(XH1, 2, XD1, CTX)
    bkv = i[kx + "bkv"].reshape(XH1, 2, XD1)
    qkv = np.stack([i["L1_attn_" + n].reshape(HP, 2 * SD, DC, P) for n in ("w_q", "w_k", "w_v")])
    arrays = {
        "x": c(i["x"]),
        "ctxT": c(i["ctx_768"].transpose(0, 2, 1)),
        "mask": c(i["mask_BxS2_bk0"]).view(np.int32),
        "a_wsh": c(np.concatenate([i[la + "W_shell"], i[la + "W_charge"], i[la + "W_charge"]]).T),
        "a_bsh": c(np.concatenate([i[la + "b_shell"], i[la + "b_charge"], i[la + "b_charge"]])),
        "a_om": c(np.concatenate([i[la + "omega"]] * 4).T),
        "a_rb": c(np.concatenate([i[la + "rff_bias"]] * 2)),
        "a_wc": c(i[la + "W_combine"].reshape(COMB, ORDERS, SHELL).transpose(2, 1, 0)),
        "a_wv": c(i[la + "W_v"]),
        "a_wo": c(i[la + "W_out"].T),
        "a_bv": c(i[la + "b_v"].reshape(DC, P).T),
        "a_bo": c(i[la + "b_out"]),
        "a_lt": c(i[la + "log_temp"].reshape(1)),
        "x0_wq": c(i[lx + "W_q"].T),
        "x0_wk": c(i[lx + "W_k"]),
        "x0_wv": c(i[lx + "W_v"]),
        "x0_wo": c(i[lx + "W_o"]),
        "x0_bo": c(i[lx + "b_o"]),
        "m_wr": c(i[lf + "Wr"]),
        "m_br": c(i[lf + "br"]),
        "m_w1": c(i[lf + "W1"]),
        "m_b1": c(i[lf + "b1"].reshape(EXPERTS, FC, P).transpose(0, 2, 1)),
        "m_w2": c(i[lf + "W2"]),
        "m_b2": c(i[lf + "b2"]),
        "l_w": c(qkv.transpose(1, 4, 0, 3, 2)),
        "l_wo": c(i["L1_attn_w_o"].T),
        "x1_wq": c(i[kx + "Wq"]),
        "x1_bq": c(i[kx + "bq"].reshape(DC, P).T),
        "x1_wk": c(wkv[:, 0].reshape(D, CTX).T),
        "x1_wv": c(wkv[:, 1].reshape(D, CTX).T),
        "x1_bk": c(bkv[:, 0].reshape(DC, P).T),
        "x1_bv": c(bkv[:, 1].reshape(DC, P).T),
        "x1_wo": c(i[kx + "Wo"].T),
        "x1_bo": c(i[kx + "bo"]),
        "g_wg": c(i[kf + "w_gate"].T),
        "g_wu": c(i[kf + "w_up"].T),
        "g_wd": c(i[kf + "w_down"].T),
    }
    nc = bacc.Bacc("TRN2", target_bir_lowering=False, num_devices=1)
    given = {f"in_{k}": v for k, v in arrays.items()}
    aps = {k: nc.dram_tensor(f"in_{k}", v.shape, mybir.dt.from_np(v.dtype), kind="ExternalInput").ap() for k, v in arrays.items()}
    out = nc.dram_tensor("out_x", (B, T, D), F32, kind="ExternalOutput").ap()
    decoder_kernel(nc, aps, out)
    r = run_bass_kernel_spmd(nc, [given], core_ids=[0])
    return r.results[0]["out_x"]
```

```python
from contextlib import ExitStack
import math

import concourse.bass as bass
from concourse import mybir

P = 128
B, T, D = 4, 1024, 256
NT = T // P
DC = D // P
HALF = 512
CTX, CK = 192, 64
SHELL, RFF, ORDERS, COMB = 64, 32, 5, 64
FF = 1024
FC = FF // P
EXPERTS = 8
XH0, XD0 = 8, 64
XH1, XD1 = 16, 16
SD = 64
HP = 8
NPH = 6

NEG = -1.0e30
MASKED = -float(2.0 ** 127)
MAGIC = 12582912.0
TWO_PI_HI = 6.28125
TWO_PI_LO = 2.0 * math.pi - 6.28125
PI_BELOW = 3.1415925
EPS = 1e-5

F32 = mybir.dt.float32
F32R = mybir.dt.float32r
BF16 = mybir.dt.bfloat16
F16 = mybir.dt.float16
I32 = mybir.dt.int32
U32 = mybir.dt.uint32
U8 = mybir.dt.uint8
ALU = mybir.AluOpType
ACT = mybir.ActivationFunctionType
AX = mybir.AxisListType


def rows(ap):
    return ap.rearrange("(o n) -> o n", o=1).to_broadcast([P, ap.shape[0]])



def decoder_kernel(nc, a, out):
    ctx = ExitStack()
    with ctx:
        def sb(name, shape, dt=F32, stack=ctx):
            return stack.enter_context(nc.sbuf_tensor(name, shape, dt))

        def sem(name):
            return ctx.enter_context(nc.semaphore(name))

        xin = sb("xin", [P, NT, D])
        x = sb("x", [P, NT, D])
        xn = sb("xn", [P, NT, D])
        xTh = sb("xTh", [P, DC, T], F32R)
        xTl = sb("xTl", [P, DC, T], F32R)
        idf = sb("idf", [P, P])
        idb = sb("idb", [P, P], BF16)
        causal = sb("causal", [P, P], BF16)
        ones_b = sb("ones_b", [1, P], BF16)
        ones_r = sb("ones_r", [2, P], F32R)
        ones_f = sb("ones_f", [P, P])
        decay = sb("decay", [P, T])
        wsh_h = sb("wsh_h", [P, DC, 66], F32R)
        wsh_l = sb("wsh_l", [P, DC, 66], F32R)
        bsh = sb("bsh", [P, 66])
        om_h = sb("om_h", [SHELL, P], F32R)
        om_l = sb("om_l", [SHELL, P], F32R)
        rbias = sb("rbias", [SHELL, 1])
        cosb = sb("cosb", [SHELL, 1])
        coss = sb("coss", [SHELL, 1])
        wc_h = sb("wc_h", [SHELL, ORDERS * COMB], F32R)
        wc_l = sb("wc_l", [SHELL, ORDERS * COMB], F32R)
        wvo_h = sb("wvo_h", [P, DC, D], F32R)
        wvo_l = sb("wvo_l", [P, DC, D], F32R)
        bvo = sb("bvo", [P, D])
        x0_wq = sb("x0_wq", [P, 4, D])
        x0_wk = sb("x0_wk", [P, 2, 512])
        x0_wv = sb("x0_wv", [P, 2, 512])
        x0_wo = sb("x0_wo", [P, 4, D])
        x0_bo = sb("x0_bo", [P, D])
        x1_wq = sb("x1_wq", [P, 2, D])
        x1_wk = sb("x1_wk", [P, 2, D])
        x1_wv = sb("x1_wv", [P, 2, D])
        x1_wo = sb("x1_wo", [P, 2, D])
        x1_bo = sb("x1_bo", [P, D])
        x1_bk = sb("x1_bk", [P, 2])
        x1_bv = sb("x1_bv", [P, 2])
        x1_bq = sb("x1_bq", [P, 2])
        x1_bqb = sb("x1_bqb", [P, 2, P])
        blk0 = sb("blk0", [P, 2])
        blk1 = sb("blk1", [P, 8])
        row01 = sb("row01", [P, 2])
        wr = sb("wr", [P, DC, EXPERTS])
        br = sb("br", [1, EXPERTS])
        wg_q = sb("wg_q", [P, DC, FF], BF16)
        wu_q = sb("wu_q", [P, DC, FF], BF16)
        wd_q = sb("wd_q", [P, FC, D], BF16)
        wsc = sb("wsc", [P, 4])
        st = sb("st", [P, NT, 6])
        ag = sb("ag", [P, NT, 2])
        rsd = sb("rsd", [P, NT])
        nv = sb("nv", [P, NT])
        nt1 = sb("nt1", [P, NT])
        ctxT = sb("ctxT", [P, 2, CK])
        mrow4 = sb("mrow4", [1, CK // 4], I32)
        mrow = sb("mrow", [1, XH0 * CK], BF16)
        sums = sb("sums", [P, 4])
        nmax = sb("nmax", [P, 4])
        rec = sb("rec", [P, 4])
        recs = sb("recs", [P, 2, NT])
        ps = ctx.enter_context(nc.psum_tensor("ps", [P, 8, HALF], F32))

        def arena(names_shapes):
            with ExitStack() as phase:
                made = {n: phase.enter_context(nc.sbuf_tensor(n, s, d)) for n, s, d in names_shapes}
            return made

        S = arena([
            ("s_wsh", [P, DC, 66], F32), ("s_om", [SHELL, P], F32), ("s_wc", [SHELL, ORDERS, COMB], F32),
            ("s_wv", [P, DC, D], F32), ("s_wo", [P, DC, D], F32), ("s_bv", [P, DC], F32), ("s_bo", [P, D], F32),
            ("s_bvb", [P, DC, P], F32), ("s_lt", [P, 1], F32), ("s_t", [P, 4], F32),
            ("s_iota", [P, T], I32), ("s_dist", [P, T], F32),
            ("s_g", [P, 2048], F32), ("s_u", [P, 2048], F32), ("s_d", [P, 2048], F32),
            ("s_q", [P, 2048], F32), ("s_abs", [P, 4], F32), ("s_i8", [P, 8], F32)])
        A = arena([
            ("a_sh", [P, NT, 66], F32), ("a_sq", [P, NT, SHELL], F32), ("a_ss", [P, NT], F32),
            ("a_rn", [P, NT], F32), ("a_shn", [P, NT, P], F32),
            ("a_shTh", [SHELL, T], F32R), ("a_shTl", [SHELL, T], F32R),
            ("a_p", [SHELL, T], F32), ("a_k", [SHELL, T], F32), ("a_r", [SHELL, T], F32), ("a_phs", [SHELL, T], F32),
            ("a_phh", [SHELL, T], F32R), ("a_phl", [SHELL, T], F32R),
            ("a_y", [P, NT, ORDERS * COMB], F32), ("a_acc", [P, NT, COMB], F32), ("a_phi", [P, NT, P], F32),
            ("a_q", [P, NT], F32), ("a_v", [P, NT, D], F32),
            ("a_qs", [P, T], F32R), ("a_k1", [P, T], F32R), ("a_k2", [P, T], F32R),
            ("a_sm", [P, 2, T], F32), ("a_pe", [P, 2, T], F32), ("a_pt", [P, 2, T], F32)])
        X = arena([
            ("c_kT", [P, 4, CK], F32), ("c_vT", [P, 4, CK], F32),
            ("c_kB", [P, 4, P], F32), ("c_vB", [P, 4, P], F32), ("c_kC", [P, 2, HALF], F32), ("c_vC", [P, 2, HALF], F32),
            ("c_mh", [P, DC, 1024], F32R), ("c_ml", [P, DC, 1024], F32R),
            ("c_uh", [P, 8, D], F32R), ("c_ul", [P, 8, D], F32R),
            ("c_b2", [P, 1024], F32R), ("c_bh", [P, 1024], F32R), ("c_bl", [P, 1024], F32),
            ("c_mx", [P, 2, 16], F32), ("c_sm", [P, 2, 1024], F32), ("c_pe", [P, 2, 1024], F32),
            ("c_su", [P, 2, 16], F32), ("c_re", [P, 2, 16], F32), ("c_pn", [P, 2, 1024], F32),
            ("c_th", [P, 2, 1024], F32R), ("c_tl", [P, 2, 1024], F32R)])
        M = arena([
            ("m_mean", [P, DC], F32), ("m_sc", [1, EXPERTS], F32), ("m_top", [1, 8], F32), ("m_idx", [1, 8], U32),
            ("m_w1", [P, DC, FF], F32), ("m_w2", [P, FC, D], F32), ("m_b1", [P, FC], F32), ("m_b2", [P, D], F32),
            ("m_w1h", [P, DC, FF], F32R), ("m_w1l", [P, DC, FF], F32R),
            ("m_w2h", [P, FC, D], F32R), ("m_w2l", [P, FC, D], F32R),
            ("m_h", [P, 2, HALF], F32),
            ("m_hh", [P, FC, HALF], F32R), ("m_hl", [P, FC, HALF], F32R)])
        L = arena([
            ("l_w", [P, 3, DC, P], F32), ("l_wh", [P, 3, DC, P], F32R), ("l_wl", [P, 3, DC, P], F32R),
            ("l_q0", [P, T], F32R), ("l_q1", [P, T], F32R),
            ("l_k10", [P, T], F32R), ("l_k11", [P, T], F32R), ("l_k20", [P, T], F32R), ("l_k21", [P, T], F32R),
            ("l_ks", [P, T], F32), ("l_qs", [P, T], F32), ("l_vs", [P, NT, P], F32),
            ("l_v", [P, 3, NT, P], BF16), ("l_vr", [P, NT, SD], F32),
            ("l_pe", [P, 2, T], F32), ("l_pt", [P, 2, 2, T], F16), ("l_o", [P, NT, P], F32),
            ("l_oT", [P, T], F32), ("l_wo", [P, D], F32)])
        G = arena([
            ("g_amx", [P, NT], F32), ("g_s", [P, NT], F32), ("g_inv", [P, NT], F32), ("g_ig", [P, NT], F32), ("g_iu", [P, NT], F32),
            ("g_t", [P, NT, D], F32), ("g_xq", [P, NT, D], BF16), ("g_xT", [P, DC, T], BF16),
            ("g_g", [P, 2, FF], F32), ("g_h", [P, 2, FF], F32), ("g_r", [P, 2, FF], F32), ("g_hq", [P, 2, FF], BF16),
            ("g_hT", [P, 2, FF], BF16), ("g_hm", [P, NT], F32), ("g_hs", [P, NT], F32), ("g_hi", [P, NT], F32)])

        s_w = sem("s_w")
        s_wq = sem("s_wq")
        s_qa = sem("s_qa")
        s_qs = sem("s_qs")
        s_gc = sem("s_gc")
        s_sa = sem("s_sa")
        s_sv = sem("s_sv")
        s_sp = sem("s_sp")
        s_xin = sem("s_xin")
        s_ctx = sem("s_ctx")
        s_xu = sem("s_xu")
        s_xb = sem("s_xb")
        s_out = sem("s_out")
        s_used = sem("s_used")
        s_xn = sem("s_xn")
        s_tr = sem("s_tr")
        s_hi = sem("s_hi")
        s_lo = sem("s_lo")

        def mm3(pe, o, lh, ll, rh, rl, start, stop):
            pe.matmul(o, lh, rh, start=start, stop=False)
            pe.matmul(o, lh, rl, start=False, stop=False)
            return pe.matmul(o, ll, rh, start=False, stop=stop)

        def f32(ap):
            return ap.bitcast(F32)

        def rsqrt(v, dst, src):
            t1 = nt1[:, 0:src.shape[-1]]
            v.drain()
            v.tensor_scalar(dst.bitcast(I32), src.bitcast(I32), 1, None, ALU.logical_shift_right)
            v.drain()
            v.tensor_scalar(dst.bitcast(I32), dst.bitcast(I32), -1.0, 1597463007.0, ALU.mult, ALU.add)
            for _ in range(3):
                v.drain()
                v.tensor_tensor(t1, dst, dst, ALU.mult)
                v.drain()
                v.scalar_tensor_tensor(out=t1, in0=t1, scalar=-0.5, in1=src, op0=ALU.mult, op1=ALU.mult)
                v.drain()
                v.scalar_tensor_tensor(out=dst, in0=t1, scalar=1.5, in1=dst, op0=ALU.add, op1=ALU.mult)
            v.drain()

        NG = NT // 2

        def ln_order(n):
            return list(range(NT - 1, -1, -1)) if n == 1 else list(range(NT))

        def ln_step(v, b, n, src, k):
            order = ln_order(n)
            size = NT if n == 0 else NT // 2
            if n == 0:
                if k == 0:
                    v.wait_ge(s_xin, b * 16 + 16)
            else:
                v.wait_ge(s_xu, b * (NPH * NT) + (n - 1) * NT + k + 1)
            v.bn_stats(st[:, order[k], :], src[:, order[k], :])
            if k % size < size - 1:
                return
            group = order[k - size + 1:k + 1]
            lo = min(group)
            v.drain()
            for t in group:
                v.bn_aggr(ag[:, t, :], st[:, t, :])
            v.drain()
            v.tensor_scalar(nv[:, lo:lo + size], ag[:, lo:lo + size, 1], EPS, None, ALU.add)
            rsqrt(v, rsd[:, lo:lo + size], nv[:, lo:lo + size])
            for t in group:
                v.tensor_scalar(xn[:, t, :], src[:, t, :], ag[:, t, 0:1], rsd[:, t:t + 1],
                                ALU.subtract, ALU.mult).then_inc(s_xn, 1)

        def ln_v(v, b, n, src):
            for k in range(NT):
                ln_step(v, b, n, src, k)

        NTR = NPH - 1

        def ln_pe(pe, b, n, groups=range(NG)):
            for g in groups:
                pe.wait_ge(s_xn, b * (NPH * NT) + n * NT + 2 * g + 2)
                if g >= 2:
                    pe.wait_ge(s_lo, b * (NTR * NG) + n * NG + g - 1)
                bank = ps[:, 6 + g % 2, :]
                for c in range(DC):
                    for t in range(2):
                        o = bank[:, c * 256 + t * P:c * 256 + (t + 1) * P]
                        tile = min(ln_order(n)[2 * g:2 * g + 2]) + t
                        last = pe.transpose(o, xn[:, tile, c * P:(c + 1) * P], idf[:])
                last.then_inc(s_tr, 1)

        def ln_group(n, g):
            bank = ps[:, 6 + g % 2, :].rearrange("p (c t) -> p c t", c=DC)
            first = min(ln_order(n)[2 * g:2 * g + 2])
            cols = slice(first * P, (first + 2) * P)
            return bank, cols

        def ln_a(s, b, n):
            for g in range(NG):
                bank, cols = ln_group(n, g)
                s.wait_ge(s_tr, b * (NTR * NG) + n * NG + g + 1)
                s.copy(xTh[:, :, cols], bank).then_inc(s_hi, 1)

        def ln_lo(v, b, n):
            for g in range(NG):
                bank, cols = ln_group(n, g)
                v.wait_ge(s_hi, b * (NTR * NG) + n * NG + g + 1)
                v.tensor_tensor(xTl[:, :, cols], bank, f32(xTh[:, :, cols]), ALU.subtract).then_inc(s_lo, 1)

        def ln_done(b, n):
            return b * (NTR * NG) + n * NG + NG

        class Attention:
            def __init__(self, name, width, probs, probsT, free):
                self.w = width
                self.pe_, self.pt_ = probs, probsT
                self.free = free
                self.s = {k: sem(f"{name}_{k}") for k in ("score", "soft", "max", "exp", "tp", "eva", "evv", "pv", "o", "rc")}

        def blocks(heads):
            return [(h, i) for h in range(heads) for i in range(NT - 1, -1, -1)]

        def banks_of(k):
            return ps[:, 2 * (k % 2):2 * (k % 2) + 2, :].rearrange("p a b -> p (a b)")

        def pieces(i):
            n = i + 1
            return [(j0, min(n, j0 + 4), (j0 // 4 + i) % 2 == 0) for j0 in range(0, n, 4)]

        def count_pieces(bl, upto):
            act = sum(1 for _, i in bl[:upto] for p_ in pieces(i) if p_[2])
            vec = sum(1 for _, i in bl[:upto] for p_ in pieces(i) if not p_[2])
            return act, vec

        def att_pe(pe, at, bl, base, q, k1, k2, val, hooks={}):
            n_bl = len(bl)
            n_act, n_vec = count_pieces(bl, n_bl)

            def hook(name, k):
                if (name, k) in hooks:
                    hooks[name, k]()

            def score(k):
                h, i = bl[k]
                n = (i + 1) * P
                if k >= 2:
                    pe.wait_ge(at.s[at.free], base * n_bl + k - 1)
                s = banks_of(k)
                for c0 in range(0, n, HALF):
                    c1 = min(n, c0 + HALF)
                    lhs = q(h)[:, i * P:(i + 1) * P]
                    pe.matmul(s[:, c0:c1], lhs, k1(h)[:, c0:c1], start=True, stop=False)
                    last = pe.matmul(s[:, c0:c1], lhs, k2(h)[:, c0:c1], start=False, stop=c1 < n)
                last = pe.matmul(s[:, n - P:n], idb[:], causal[:], start=False, stop=True)
                last.then_inc(at.s["score"], 1)

            def copied(k):
                a, v = count_pieces(bl, k)
                if a:
                    pe.wait_ge(at.s["eva"], base * n_act + a)
                if v:
                    pe.wait_ge(at.s["evv"], base * n_vec + v)

            def turn(k):
                h, i = bl[k]
                pe.wait_ge(at.s["exp"], base * n_bl + k + 1)
                if k >= 1:
                    copied(k)
                for j in range(i + 1):
                    o = ps[:, 4 + j // 4, (j % 4) * P:(j % 4 + 1) * P]
                    last = pe.transpose(o, at.pe_[:, k % 2, j * P:(j + 1) * P], idf[:])
                last.then_inc(at.s["tp"], 1)

            def pv(k):
                h, i = bl[k]
                copied(k + 1)
                if k >= 2:
                    pe.wait_ge(at.s["o"], base * n_bl + k - 1)
                o = ps[:, 6 + k % 2, 0:at.w]
                for j in range(i + 1):
                    cols = slice(j * P, (j + 1) * P)
                    last = pe.matmul(o, at.pt_[:, k % 2, cols], val(h, j), start=j == 0, stop=j == i)
                last.then_inc(at.s["pv"], 1)

            score(0)
            score(1)
            hook("turn", 0)
            turn(0)
            score(2)
            for k in range(n_bl):
                if k + 1 < n_bl:
                    turn(k + 1)
                hook("pv", k)
                pv(k)
                if k + 3 < n_bl:
                    score(k + 3)
                hook("end", k)

        def att_a(s, at, bl, base, src, hooks={}):
            n_bl = len(bl)

            def exp(k):
                h, i = bl[k]
                n = (i + 1) * P
                s.wait_ge(at.s["max"], base * n_bl + k + 1)
                if k >= 2:
                    s.wait_ge(at.s["tp"], base * n_bl + k - 1)
                    s.wait_ge(at.s["rc"], base * n_bl + k - 1)
                ins = s.activation(at.pe_[:, k % 2, 0:n], src(k)[:, 0:n], ACT.Exp, bias=nmax[:, k % 2:k % 2 + 1],
                                   accum_out=sums[:, k % 2:k % 2 + 1])
                ins.then_inc(at.s["exp"], 1)

            def copy_out(k):
                for j0, j1, mine in pieces(bl[k][1]):
                    if mine:
                        s.wait_ge(at.s["tp"], base * n_bl + k + 1)
                        if k >= 2:
                            s.wait_ge(at.s["pv"], base * n_bl + k - 1)
                        s.copy(at.pt_[:, k % 2, j0 * P:j1 * P], ps[:, 4 + j0 // 4, 0:(j1 - j0) * P]).then_inc(at.s["eva"], 1)

            exp(0)
            exp(1)
            for k in range(n_bl):
                copy_out(k)
                if 1 <= k < n_bl - 1:
                    exp(k + 1)
                if k in hooks:
                    hooks[k]()

        def att_v(v, at, bl, base, scale_rows, finish, hooks={}):
            n_bl = len(bl)

            def maximum(k):
                h, i = bl[k]
                n = (i + 1) * P
                v.wait_ge(at.s["score"], base * n_bl + k + 1)
                if k >= 2:
                    v.wait_ge(at.s["exp"], base * n_bl + k - 1)
                src = scale_rows(k, i, n)
                v.tensor_reduce(nmax[:, k % 2:k % 2 + 1], src, AX.X, ALU.max, negate=True).then_inc(at.s["max"], 1)

            def copy_out(k):
                for j0, j1, mine in pieces(bl[k][1]):
                    if not mine:
                        v.wait_ge(at.s["tp"], base * n_bl + k + 1)
                        if k >= 2:
                            v.wait_ge(at.s["pv"], base * n_bl + k - 1)
                        v.tensor_copy(at.pt_[:, k % 2, j0 * P:j1 * P], ps[:, 4 + j0 // 4, 0:(j1 - j0) * P]).then_inc(at.s["evv"], 1)

            def inverse(k):
                v.wait_ge(at.s["exp"], base * n_bl + k + 1)
                if k >= 2:
                    v.wait_ge(at.s["o"], base * n_bl + k - 1)
                v.reciprocal(rec[:, k % 2:k % 2 + 1], sums[:, k % 2:k % 2 + 1]).then_inc(at.s["rc"], 1)

            def out_(k):
                v.wait_ge(at.s["rc"], base * n_bl + k + 1)
                v.wait_ge(at.s["pv"], base * n_bl + k + 1)
                finish(k, bl[k][0], bl[k][1], ps[:, 6 + k % 2, 0:at.w], rec[:, k % 2:k % 2 + 1]).then_inc(at.s["o"], 1)

            maximum(0)
            maximum(1)
            for k in range(n_bl):
                copy_out(k)
                inverse(k)
                if k + 2 < n_bl:
                    maximum(k + 2)
                if k >= 1:
                    out_(k - 1)
                if k in hooks:
                    hooks[k]()
            out_(n_bl - 1)

        a_sem = {k: sem(f"a_{k}") for k in
                 ("sh", "shv", "q", "shn", "st", "sth", "stl", "pr", "u", "ab", "sin", "ph", "y", "ya", "v", "va", "phd",
                  "pt", "k1", "qs", "phh")}
        AT0 = Attention("at0", D, A["a_pe"], A["a_pt"], "soft")
        Y_BANKS = (2, 3, 0, 1)
        bl0 = blocks(1)

        def a_pe(pe, b):
            pe.wait_ge(s_lo, ln_done(b, 0))
            for g in range(2):
                for t in range(4):
                    tok = slice((4 * g + t) * P, (4 * g + t + 1) * P)
                    o = ps[:, g, t * 66:(t + 1) * 66]
                    for c in range(DC):
                        last = mm3(pe, o, xTh[:, c, tok], xTl[:, c, tok], wsh_h[:, c, :], wsh_l[:, c, :], c == 0, c == DC - 1)
                last.then_inc(a_sem["sh"], 1)
            for g in range(4):
                if g >= 2:
                    pe.wait_ge(a_sem["va"], b * 4 + g - 1)
                for t in range(2):
                    tok = slice((2 * g + t) * P, (2 * g + t + 1) * P)
                    o = ps[:, 2 + g % 2, t * D:(t + 1) * D]
                    for c in range(DC):
                        last = mm3(pe, o, xTh[:, c, tok], xTl[:, c, tok], wvo_h[:, c, :], wvo_l[:, c, :], c == 0, c == DC - 1)
                last.then_inc(a_sem["v"], 1)
            pe.wait_ge(a_sem["shn"], b + 1)
            for g in range(2):
                for t in range(4):
                    last = pe.transpose(ps[:, 4 + g, t * P:(t + 1) * P], A["a_shn"][:, 4 * g + t, :], idf[:])
                last.then_inc(a_sem["st"], 1)
            pe.wait_ge(a_sem["stl"], b * 2 + 2)
            for g in range(2):
                cols = slice(g * HALF, (g + 1) * HALF)
                last = mm3(pe, ps[:, g, :], om_h[:], om_l[:], A["a_shTh"][:, cols], A["a_shTl"][:, cols], True, True)
                last.then_inc(a_sem["pr"], 1)
            x_pe_kv(pe, C0, b)
            x_pe_m(pe, C0, b)
            pe.wait_ge(a_sem["va"], b * 4 + 4)
            for t in range(NT):
                tok = slice(t * P, (t + 1) * P)
                if t % 4 == 0:
                    pe.wait_ge(a_sem["ph"], b * 2 + t // 4 + 1)
                if t == 3:
                    pe.wait_ge(a_sem["u"], b * 2 + 2)
                if t >= 4:
                    pe.wait_ge(a_sem["ya"], b * NT + t - 3)
                last = mm3(pe, ps[:, Y_BANKS[t % 4], 0:ORDERS * COMB], A["a_phh"][:, tok], A["a_phl"][:, tok], wc_h[:], wc_l[:], True, True)
                last.then_inc(a_sem["y"], 1)
            pe.wait_ge(a_sem["phd"], b + 1)
            for g in range(2):
                for t in range(4):
                    last = pe.transpose(ps[:, 4 + g, t * P:(t + 1) * P], A["a_phi"][:, 4 * g + t, :], idf[:])
                last.then_inc(a_sem["pt"], 1)
            pe.wait_ge(a_sem["qs"], b * 2 + 2)
            x_pe_u(pe, C0, b)
            hooks = {("turn", 0): lambda: pe.wait_ge(C0.s["ul"], b + 1),
                     ("pv", 0): lambda: pe.wait_ge(C0.s["ml"], b + 1)}
            att_pe(pe, AT0, bl0, b, lambda h: A["a_qs"], lambda h: A["a_k1"], lambda h: A["a_k2"],
                   lambda h, j: A["a_v"][:, j, :], hooks)

        def a_a(s, b):
            for g in range(4):
                s.wait_ge(a_sem["v"], b * 4 + g + 1)
                s.copy(A["a_v"][:, 2 * g:2 * g + 2, :].rearrange("p t d -> p (t d)"), ps[:, 2 + g % 2, :]).then_inc(a_sem["va"], 1)
            s.wait_ge(a_sem["shv"], b * 2 + 2)
            s.activation(A["a_q"][:], A["a_sh"][:, :, 64], ACT.Tanh).then_inc(a_sem["q"], 1)
            for g in range(2):
                s.wait_ge(a_sem["st"], b * 2 + g + 1)
                s.copy(A["a_shTh"][:, g * HALF:(g + 1) * HALF], ps[0:SHELL, 4 + g, :]).then_inc(a_sem["sth"], 1)
            x_a_kv(s, C0, b)
            for g in range(2):
                cols = slice(g * HALF, (g + 1) * HALF)
                s.wait_ge(a_sem["u"], b * 2 + g + 1)
                s.activation(A["a_r"][0:RFF, cols], A["a_r"][0:RFF, cols], ACT.Abs).then_inc(a_sem["ab"], 1)
                s.wait_ge(a_sem["ab"], b * 2 + g + 1)
                s.activation(A["a_phs"][:, cols], A["a_r"][:, cols], ACT.Sin, bias=cosb[:], scale=coss[:]).then_inc(a_sem["sin"], 1)
                s.wait_ge(a_sem["sin"], b * 2 + g + 1)
                s.copy(A["a_phh"][:, cols], A["a_phs"][:, cols]).then_inc(a_sem["phh"], 1)
            for t in range(NT):
                s.wait_ge(a_sem["y"], b * NT + t + 1)
                s.copy(A["a_y"][:, t, :], ps[:, Y_BANKS[t % 4], 0:ORDERS * COMB]).then_inc(a_sem["ya"], 1)
            for g in range(2):
                cols = slice(g * HALF, (g + 1) * HALF)
                s.wait_ge(a_sem["pt"], b * 2 + g + 1)
                s.copy(A["a_k1"][:, cols], ps[:, 4 + g, :]).then_inc(a_sem["k1"], 1)
            s.wait_ge(a_sem["k1"], b * 2 + 2)
            s.copy(A["a_qs"][0:64, :], f32(A["a_k1"][0:64, :])).then_inc(a_sem["qs"], 1)
            x_a_m(s, C0, b)
            x_a_u(s, C0, b)
            att_a(s, AT0, bl0, b, lambda k: A["a_sm"][:, k % 2, :])

        def a_v(v, b):
            for g in range(2):
                v.wait_ge(a_sem["sh"], b * 2 + g + 1)
                v.tensor_tensor(A["a_sh"][:, 4 * g:4 * g + 4, :], ps[:, g, 0:4 * 66].rearrange("p (t n) -> p t n", t=4),
                                bsh[:].unsqueeze(1).to_broadcast([P, 4, 66]), ALU.add).then_inc(a_sem["shv"], 1)
            v.drain()
            v.tensor_tensor(A["a_sq"][:], A["a_sh"][:, :, 0:SHELL], A["a_sh"][:, :, 0:SHELL], ALU.mult)
            v.drain()
            v.tensor_reduce(A["a_ss"][:], A["a_sq"][:], AX.X, ALU.add)
            v.drain()
            v.tensor_scalar(A["a_ss"][:], A["a_ss"][:], 1e-24, None, ALU.max)
            rsqrt(v, A["a_rn"][:], A["a_ss"][:])
            for o in (slice(0, SHELL), slice(SHELL, P)):
                last = v.tensor_tensor(A["a_shn"][:, :, o], A["a_sh"][:, :, 0:SHELL],
                                       A["a_rn"][:].unsqueeze(2).to_broadcast([P, NT, SHELL]), ALU.mult)
            last.then_inc(a_sem["shn"], 1)
            for g in range(2):
                cols = slice(g * HALF, (g + 1) * HALF)
                v.wait_ge(a_sem["sth"], b * 2 + g + 1)
                v.tensor_tensor(A["a_shTl"][:, cols], ps[0:SHELL, 4 + g, :], f32(A["a_shTh"][:, cols]),
                                ALU.subtract).then_inc(a_sem["stl"], 1)
            for g in range(2):
                cols = slice(g * HALF, (g + 1) * HALF)
                angle, turns = A["a_p"][:, cols], A["a_k"][:, cols]
                v.wait_ge(a_sem["pr"], b * 2 + g + 1)
                v.tensor_scalar(angle, ps[0:SHELL, g, :], rbias[:, 0:1], None, ALU.add)
                v.drain()
                v.tensor_scalar(turns, angle, 1.0 / (2.0 * math.pi), MAGIC, ALU.mult, ALU.add)
                v.drain()
                v.tensor_scalar(turns, turns, MAGIC, None, ALU.subtract)
                v.drain()
                v.scalar_tensor_tensor(out=angle, in0=turns, scalar=-TWO_PI_HI, in1=angle, op0=ALU.mult, op1=ALU.add)
                v.drain()
                v.scalar_tensor_tensor(out=angle, in0=turns, scalar=-TWO_PI_LO, in1=angle, op0=ALU.mult, op1=ALU.add)
                v.drain()
                v.tensor_scalar(A["a_r"][:, cols], angle, -PI_BELOW, PI_BELOW, ALU.max, ALU.min).then_inc(a_sem["u"], 1)
            for g in range(2):
                cols = slice(g * HALF, (g + 1) * HALF)
                v.wait_ge(a_sem["phh"], b * 2 + g + 1)
                v.tensor_tensor(A["a_phl"][:, cols], A["a_phs"][:, cols], f32(A["a_phh"][:, cols]), ALU.subtract).then_inc(a_sem["ph"], 1)
            v.wait_ge(a_sem["q"], b + 1)
            for m in range(ORDERS - 2, -1, -1):
                for t in range(NT):
                    if m == ORDERS - 2:
                        v.wait_ge(a_sem["ya"], b * NT + t + 1)
                    src = A["a_y"][:, t, (m + 1) * COMB:(m + 2) * COMB] if m == ORDERS - 2 else A["a_acc"][:, t, :]
                    dst = A["a_phi"][:, t, 0:COMB] if m == 0 else A["a_acc"][:, t, :]
                    v.scalar_tensor_tensor(out=dst, in0=src, scalar=A["a_q"][:, t:t + 1],
                                           in1=A["a_y"][:, t, m * COMB:(m + 1) * COMB], op0=ALU.mult, op1=ALU.add)
                v.drain()
            v.tensor_copy(A["a_phi"][:, :, COMB:2 * COMB], A["a_phi"][:, :, 0:COMB]).then_inc(a_sem["phd"], 1)
            for g in range(2):
                cols = slice(g * HALF, (g + 1) * HALF)
                v.wait_ge(a_sem["k1"], b * 2 + g + 1)
                v.tensor_tensor(A["a_k2"][:, cols], ps[:, 4 + g, :], f32(A["a_k1"][:, cols]), ALU.subtract)
            v.drain()
            v.tensor_copy(A["a_qs"][64:128, :], f32(A["a_k2"][64:128, :])).then_inc(a_sem["qs"], 1)
            x_v_m(v, C0, b)
            x_v_bias(v, C0, b)
            x_v_u(v, C0, b)
            v.wait_ge(s_xb, b * 4 + 1)

            def rows_scaled(k, i, n):
                v.tensor_tensor(A["a_sm"][:, k % 2, 0:n], banks_of(k)[:, 0:n], decay[:, T - n:T], ALU.mult).then_inc(AT0.s["soft"], 1)
                v.wait_ge(AT0.s["soft"], b * len(bl0) + k + 1)
                return A["a_sm"][:, k % 2, 0:n]

            def finish(k, h, i, o, r):
                v.scalar_tensor_tensor(out=x[:, i, :], in0=o, scalar=r, in1=x[:, i, :], op0=ALU.mult, op1=ALU.add).then_inc(s_xu, 1)
                return v.drain()

            att_v(v, AT0, bl0, b, rows_scaled, finish,
                  hooks={k: (lambda k=k: ln_step(v, b, 1, x, k - 1)) for k in range(1, NT)})
            ln_step(v, b, 1, x, NT - 1)

        class Cross:
            def __init__(self, name, n, heads, hd, kv_bank, m_bank, u_bank):
                self.n, self.h, self.hd = n, heads, hd
                self.kv_bank, self.m_bank, self.u_bank = kv_bank, m_bank, u_bank
                self.hpc = P // hd
                self.nc_ = heads // self.hpc
                self.W = heads * CK
                self.nb = self.W // HALF
                self.pairs = heads // 2
                self.s = {k: sem(f"{name}_{k}") for k in
                          ("kv", "kvT", "bd", "m", "mh", "ml", "u", "uh", "ul", "br", "bh", "b2",
                           "sc", "mx", "sm", "ex", "su", "pn", "tp", "th", "tl", "pv")}

        C0 = Cross("x0", 1, XH0, XD0, 4, 6, 4)
        C1 = Cross("x1", 4, XH1, XD1, 0, 2, 2)

        def cross_w(cr):
            if cr is C0:
                return x0_wq, x0_wk, x0_wv, x0_wo, X["c_kB"], X["c_vB"], blk0
            return x1_wq, x1_wk, x1_wv, x1_wo, X["c_kC"], X["c_vC"], blk1

        def x_pe_kv(pe, cr, b):
            _, wk, wv, _, _, _, _ = cross_w(cr)
            pe.wait_ge(s_ctx, b * 48 + 48)
            for j, w in enumerate((wk, wv)):
                for c in range(cr.nc_):
                    o = ps[:, cr.kv_bank + j, c * CK:(c + 1) * CK]
                    pe.matmul(o, w[:, 0, c * P:(c + 1) * P], ctxT[:, 0, :], start=True, stop=False)
                    last = pe.matmul(o, w[0:64, 1, c * P:(c + 1) * P], ctxT[0:64, 1, :], start=False, stop=True)
            last.then_inc(cr.s["kv"], 1)

        def x_pe_m(pe, cr, b):
            wq, _, _, _, kB, _, _ = cross_w(cr)
            q = cr.s
            pe.wait_ge(q["bd"], b * 2 + 2)
            cw = cr.hpc * CK
            for dc in range(DC):
                for c in range(cr.nc_):
                    col = c * cw
                    o = ps[:, cr.m_bank + dc * cr.nb + col // HALF, col % HALF:col % HALF + cw]
                    last = pe.matmul(o, wq[:, c, dc * P:(dc + 1) * P], kB[:, c, 0:cw], start=True, stop=True)
            last.then_inc(q["m"], 1)

        def x_pe_bias(pe, cr, b):
            _, _, _, _, kB, _, _ = cross_w(cr)
            for c in range(2):
                last = pe.matmul(ps[:, c, :], x1_bqb[:, c, :], kB[:, c, :], start=True, stop=True)
            last.then_inc(cr.s["br"], 1)

        def x_pe_u(pe, cr, b):
            _, _, _, wo, _, vB, _ = cross_w(cr)
            for g in range(cr.pairs // 2):
                for j in (2 * g, 2 * g + 1):
                    c, off = (2 * j) // cr.hpc, ((2 * j) % cr.hpc) * CK
                    o = ps[:, cr.u_bank + g, (j % 2) * D:(j % 2 + 1) * D]
                    last = pe.matmul(o, vB[:, c, off:off + P], wo[:, c, :], start=True, stop=True)
            last.then_inc(cr.s["u"], 1)

        def x_m_ps(cr):
            return ps[:, cr.m_bank:cr.m_bank + DC * cr.nb, :].rearrange("p (c n) w -> p c (n w)", c=DC)

        def x_u_ps(cr):
            return ps[:, cr.u_bank:cr.u_bank + cr.pairs // 2, :]

        def x_u_sb(cr, name):
            return X[name][:, 0:cr.pairs, :].rearrange("p (g j) d -> p g (j d)", j=2)

        def x_a_m(s, cr, b):
            q = cr.s
            sc = float(cr.hd) ** -0.5
            s.wait_ge(q["m"], b + 1)
            s.activation(X["c_mh"][:, :, 0:cr.W], x_m_ps(cr), ACT.Copy, scale=sc).then_inc(q["mh"], 1)
            if cr is C1:
                s.wait_ge(q["br"], b + 1)
                s.activation(X["c_bh"][:], ps[:, 0:2, :].rearrange("p a w -> p (a w)"), ACT.Copy, scale=sc).then_inc(q["bh"], 1)

        def x_a_u(s, cr, b):
            s.wait_ge(cr.s["u"], b + 1)
            s.copy(x_u_sb(cr, "c_uh"), x_u_ps(cr)).then_inc(cr.s["uh"], 1)

        def x_kv_ps(cr, j):
            return ps[:, cr.kv_bank + j, 0:cr.nc_ * CK].rearrange("p (c k) -> p c k", k=CK)

        def x_diagonal(eng, cr, b):
            _, _, _, _, kB, vB, blk = cross_w(cr)
            for src, dst in ((X["c_kT"], kB), (X["c_vT"], vB)):
                for c in range(cr.nc_):
                    o = dst[:, c, 0:cr.hpc * CK].rearrange("p (h k) -> p h k", k=CK)
                    last = eng.tensor_tensor(o, src[:, c, :].unsqueeze(1).to_broadcast([P, cr.hpc, CK]),
                                             blk[:].unsqueeze(2).to_broadcast([P, cr.hpc, CK]), ALU.mult)
                last.then_inc(cr.s["bd"], 1)

        def x_v_kv(v, cr, b):
            v.wait_ge(cr.s["kv"], b + 1)
            for c in range(2):
                v.tensor_scalar(X["c_kT"][:, c, :], x_kv_ps(cr, 0)[:, c, :], x1_bk[:, c:c + 1], None, ALU.add)
                v.tensor_scalar(X["c_vT"][:, c, :], x_kv_ps(cr, 1)[:, c, :], x1_bv[:, c:c + 1], None, ALU.add)
            v.drain().then_inc(s_used, 1)
            x_diagonal(v, cr, b)

        def x_a_kv(s, cr, b):
            s.wait_ge(cr.s["kv"], b + 1)
            s.copy(X["c_kT"][:, 0:cr.nc_, :], x_kv_ps(cr, 0)).then_inc(cr.s["kvT"], 1)
            s.copy(X["c_vT"][:, 0:cr.nc_, :], x_kv_ps(cr, 1)).then_inc(cr.s["kvT"], 1)

        def x_v_m(v, cr, b):
            q = cr.s
            sc = float(cr.hd) ** -0.5
            v.wait_ge(q["mh"], b + 1)
            for dc in range(DC):
                last = v.scalar_tensor_tensor(out=X["c_ml"][:, dc, 0:cr.W], in0=x_m_ps(cr)[:, dc, :], scalar=sc, in1=f32(X["c_mh"][:, dc, 0:cr.W]),
                                              op0=ALU.mult, op1=ALU.subtract)
            last.then_inc(q["ml"], 1)

        def x_v_bias(v, cr, b):
            q = cr.s
            sc = float(cr.hd) ** -0.5
            if cr is C1:
                v.wait_ge(q["bh"], b + 1)
                v.scalar_tensor_tensor(out=X["c_bl"][:], in0=ps[:, 0:2, :].rearrange("p a w -> p (a w)"), scalar=sc,
                                       in1=f32(X["c_bh"][:]), op0=ALU.mult, op1=ALU.subtract)
                v.drain()
                v.tensor_scalar(X["c_bl"][:], X["c_bl"][:], row01[:, 1:2], None, ALU.mult)
                v.drain()
                v.scalar_tensor_tensor(out=X["c_b2"][:], in0=f32(X["c_bh"][:]), scalar=row01[:, 0:1], in1=X["c_bl"][:],
                                       op0=ALU.mult, op1=ALU.add).then_inc(q["b2"], 1)
            else:
                v.wait_ge(s_ctx, b * 48 + 48)
                v.tensor_scalar(mrow[:].rearrange("p (h k) -> p h k", k=CK), mrow4[:].bitcast(U8).unsqueeze(1).to_broadcast([1, XH0, CK]),
                                -MASKED, MASKED, ALU.mult, ALU.add).then_inc(q["b2"], 1)

        def x_v_u(v, cr, b):
            v.wait_ge(cr.s["uh"], b + 1)
            v.tensor_tensor(x_u_sb(cr, "c_ul"), x_u_ps(cr), x_u_sb_f32(cr), ALU.subtract).then_inc(cr.s["ul"], 1)

        def x_u_sb_f32(cr):
            return f32(X["c_uh"][:, 0:cr.pairs, :]).rearrange("p (g j) d -> p g (j d)", j=2)

        def x_banks(cr, t):
            return ps[:, cr.nb * (t % 2):cr.nb * (t % 2) + cr.nb, :].rearrange("p a w -> p (a w)")

        def x_pe(pe, cr, b):
            q = cr.s
            pe.wait_ge(s_lo, ln_done(b, cr.n))
            pe.wait_ge(q["b2"], b + 1)

            def score(t):
                tok = slice(t * P, (t + 1) * P)
                if t >= 2:
                    pe.wait_ge(q["sm"], b * NT + t - 1)
                for n in range(cr.nb):
                    cols = slice(n * HALF, (n + 1) * HALF)
                    o = x_banks(cr, t)[:, cols]
                    for c in range(DC):
                        mm3(pe, o, xTh[:, c, tok], xTl[:, c, tok], X["c_mh"][:, c, cols], X["c_ml"][:, c, cols], c == 0, False)
                    if cr is C1:
                        last = pe.matmul(o, ones_r[0:2, :], X["c_b2"][0:2, cols], start=False, stop=True)
                    else:
                        last = pe.matmul(o, ones_b[:], mrow[:], start=False, stop=True)
                last.then_inc(q["sc"], 1)

            def turn(t):
                pe.wait_ge(q["pn"], b * NT + t + 1)
                if t >= 1:
                    pe.wait_ge(q["tl"], b * NT + t)
                for j in range(cr.pairs):
                    last = pe.transpose(ps[:, 4 + j // 4, (j % 4) * P:(j % 4 + 1) * P], X["c_pn"][:, t % 2, j * P:(j + 1) * P], idf[:])
                last.then_inc(q["tp"], 1)

            def pv(t):
                pe.wait_ge(q["tl"], b * NT + t + 1)
                if t >= 2:
                    pe.wait_ge(s_xu, b * (NPH * NT) + cr.n * NT + t - 1)
                o = ps[:, 6 + t % 2, 0:D]
                for j in range(cr.pairs):
                    cols = slice(j * P, (j + 1) * P)
                    last = mm3(pe, o, X["c_th"][:, t % 2, cols], X["c_tl"][:, t % 2, cols], X["c_uh"][:, j, :], X["c_ul"][:, j, :],
                               j == 0, j == cr.pairs - 1)
                last.then_inc(q["pv"], 1)

            score(0)
            pe.wait_ge(q["ul"], b + 1)
            score(1)
            score(2)
            turn(0)
            for t in range(NT):
                if t + 1 < NT:
                    turn(t + 1)
                pv(t)
                if t + 3 < NT:
                    score(t + 3)

        def x_a(s, cr, b):
            q = cr.s
            nb4 = cr.pairs // 4

            def exp(t):
                s.wait_ge(q["sm"], b * NT + t + 1)
                if t >= 2:
                    s.wait_ge(q["pn"], b * NT + t - 1)
                s.activation(X["c_pe"][:, t % 2, 0:cr.W], X["c_sm"][:, t % 2, 0:cr.W], ACT.Exp).then_inc(q["ex"], 1)

            exp(0)
            exp(1)
            for t in range(NT):
                s.wait_ge(q["tp"], b * NT + t + 1)
                if t >= 2:
                    s.wait_ge(q["pv"], b * NT + t - 1)
                s.copy(X["c_th"][:, t % 2, 0:cr.W], ps[:, 4:4 + nb4, :].rearrange("p a w -> p (a w)")).then_inc(q["th"], 1)
                if t + 2 < NT:
                    exp(t + 2)

        def x_v(v, cr, b):
            q = cr.s
            nb4 = cr.pairs // 4

            def soft(t):
                v.wait_ge(q["sc"], b * NT + t + 1)
                src = x_banks(cr, t).rearrange("p (h k) -> p h k", k=CK)
                v.tensor_reduce(X["c_mx"][:, t % 2, 0:cr.h], src, AX.X, ALU.max).then_inc(q["mx"], 1)
                v.wait_ge(q["mx"], b * NT + t + 1)
                if t >= 2:
                    v.wait_ge(q["ex"], b * NT + t - 1)
                v.tensor_tensor(X["c_sm"][:, t % 2, 0:cr.W].rearrange("p (h k) -> p h k", k=CK), src,
                                X["c_mx"][:, t % 2, 0:cr.h].unsqueeze(2).to_broadcast([P, cr.h, CK]), ALU.subtract).then_inc(q["sm"], 1)

            def sum_(t):
                v.wait_ge(q["ex"], b * NT + t + 1)
                if t >= 2:
                    v.wait_ge(q["pn"], b * NT + t - 1)
                v.tensor_reduce(X["c_su"][:, t % 2, 0:cr.h], X["c_pe"][:, t % 2, 0:cr.W].rearrange("p (h k) -> p h k", k=CK), AX.X, ALU.add)
                v.drain()
                v.reciprocal(X["c_re"][:, t % 2, 0:cr.h], X["c_su"][:, t % 2, 0:cr.h]).then_inc(q["su"], 1)

            def add(t):
                v.wait_ge(q["pv"], b * NT + t + 1)
                v.tensor_tensor(x[:, t, :], x[:, t, :], ps[:, 6 + t % 2, 0:D], ALU.add).then_inc(s_xu, 1)
                ln_step(v, b, cr.n + 1, x, t)

            soft(0)
            soft(1)
            sum_(0)
            sum_(1)
            for t in range(NT):
                v.wait_ge(q["th"], b * NT + t + 1)
                if t >= 2:
                    v.wait_ge(q["pv"], b * NT + t - 1)
                v.tensor_tensor(X["c_tl"][:, t % 2, 0:cr.W], ps[:, 4:4 + nb4, :].rearrange("p a w -> p (a w)"),
                                f32(X["c_th"][:, t % 2, 0:cr.W]), ALU.subtract).then_inc(q["tl"], 1)
                if t + 2 < NT:
                    soft(t + 2)
                if t == 0:
                    v.wait_ge(s_xb, b * 4 + (2 if cr is C0 else 4))
                else:
                    add(t - 1)
                if t + 2 < NT:
                    sum_(t + 2)
            add(NT - 1)

        def x_g(g, cr, b, bias):
            q = cr.s
            g.wait_ge(s_xn, b * (NPH * NT) + (cr.n + 1) * NT)
            g.tensor_tensor(x[:], x[:], bias[:].unsqueeze(1).to_broadcast([P, NT, D]), ALU.add).then_inc(s_xb, 1)
            for t in range(NT):
                g.wait_ge(q["su"], b * NT + t + 1)
                if t >= 2:
                    g.wait_ge(q["tp"], b * NT + t - 1)
                g.tensor_tensor(X["c_pn"][:, t % 2, 0:cr.W].rearrange("p (h k) -> p h k", k=CK),
                                X["c_pe"][:, t % 2, 0:cr.W].rearrange("p (h k) -> p h k", k=CK),
                                X["c_re"][:, t % 2, 0:cr.h].unsqueeze(2).to_broadcast([P, cr.h, CK]), ALU.mult).then_inc(q["pn"], 1)

        m_sem = {k: sem(f"m_{k}") for k in
                 ("mean", "meanv", "sc", "idx", "w1a", "w1", "w2", "w1h", "w1l", "w2h", "w2l", "up", "h", "hh", "hl", "dn", "seen")}

        def m_pe(pe, b):
            pe.wait_ge(C0.s["sm"], b * NT + NT)
            for t in range(NT):
                if t == NT // 2:
                    pe.wait_ge(s_xu, b * (NPH * NT) + 2 * NT)
                    ln_pe(pe, b, 2, range(NG // 2))
                if t % 4 == 0:
                    pe.wait_ge(s_xn, b * (NPH * NT) + 2 * NT + t + 4)
                for c in range(DC):
                    last = pe.matmul(ps[:, c, 0:1], xn[:, t, c * P:(c + 1) * P], ones_f[:, 0:1], start=t == 0, stop=t == NT - 1)
            last.then_inc(m_sem["mean"], 1)
            pe.wait_ge(m_sem["meanv"], b + 1)
            for c in range(DC):
                last = pe.matmul(ps[0:1, 2, 0:EXPERTS], M["m_mean"][:, c:c + 1], wr[:, c, :], start=c == 0, stop=c == DC - 1)
            last.then_inc(m_sem["sc"], 1)
            ln_pe(pe, b, 2, range(NG // 2, NG))
            pe.wait_ge(s_lo, ln_done(b, 2))
            for hf in range(2):
                cols = slice(hf * HALF, (hf + 1) * HALF)
                for f in range(FC):
                    n = hf * FC + f
                    if n >= 4:
                        pe.wait_ge(m_sem["h"], b * 2 * FC + n - 3)
                    o = ps[:, n % 4, :]
                    fs = slice(f * P, (f + 1) * P)
                    if hf == 0 and f % (FC // 2) == 0:
                        pe.wait_ge(m_sem["w1l"], b * 2 + 2 * f // FC + 1)
                    for c in range(DC):
                        last = mm3(pe, o, M["m_w1h"][:, c, fs], M["m_w1l"][:, c, fs], xTh[:, c, cols], xTl[:, c, cols], c == 0, c == DC - 1)
                    last.then_inc(m_sem["up"], 1)
                if hf == 0:
                    pe.wait_ge(m_sem["w2l"], b + 1)
                pe.wait_ge(m_sem["hl"], b * 2 * FC + (hf + 1) * FC)
                for t in range(4):
                    n = hf * 4 + t
                    if n >= 2:
                        pe.wait_ge(s_xu, b * (NPH * NT) + 2 * NT + n - 1)
                    o = ps[:, 4 + n % 2, 0:D]
                    for f in range(FC):
                        tok = slice(t * P, (t + 1) * P)
                        last = mm3(pe, o, M["m_hh"][:, f, tok], M["m_hl"][:, f, tok], M["m_w2h"][:, f, :], M["m_w2l"][:, f, :],
                                   f == 0, f == FC - 1)
                    last.then_inc(m_sem["dn"], 1)

        def m_a(s, b):
            ln_a(s, b, 2)
            for f in range(2):
                if f == 0:
                    s.wait_ge(m_sem["w1a"], b * 16 + 16)
                else:
                    s.wait_ge(m_sem["w1"], b * 48 + 48)
                s.copy(M["m_w1h"][:, :, f * HALF:(f + 1) * HALF], M["m_w1"][:, :, f * HALF:(f + 1) * HALF]).then_inc(m_sem["w1h"], 1)
            s.wait_ge(m_sem["w2"], b * 16 + 16)
            s.copy(M["m_w2h"][:], M["m_w2"][:]).then_inc(m_sem["w2h"], 1)
            for n in range(2 * FC):
                s.wait_ge(m_sem["up"], b * 2 * FC + n + 1)
                if n >= 2:
                    s.wait_ge(m_sem["hl"], b * 2 * FC + n - 1)
                s.activation(M["m_h"][:, n % 2, :], ps[:, n % 4, :], ACT.Relu, bias=M["m_b1"][:, n % FC:n % FC + 1]).then_inc(m_sem["h"], 1)

        def m_v(v, b):
            v.wait_ge(m_sem["mean"], b + 1)
            v.tensor_scalar(M["m_mean"][:], ps[:, 0:2, 0], 1.0 / T, None, ALU.mult).then_inc(m_sem["meanv"], 1)
            v.wait_ge(m_sem["sc"], b + 1)
            v.tensor_tensor(M["m_sc"][:], ps[0:1, 2, 0:EXPERTS], br[:], ALU.add)
            v.drain()
            v.max(M["m_top"][:], M["m_sc"][:])
            v.drain()
            v.max_index(M["m_idx"][:], M["m_top"][:], M["m_sc"][:]).then_inc(m_sem["idx"], 1)
            ln_lo(v, b, 2)
            for f in range(2):
                cols = slice(f * HALF, (f + 1) * HALF)
                v.wait_ge(m_sem["w1h"], b * 2 + f + 1)
                v.tensor_tensor(M["m_w1l"][:, :, cols], M["m_w1"][:, :, cols], f32(M["m_w1h"][:, :, cols]), ALU.subtract).then_inc(m_sem["w1l"], 1)
            v.wait_ge(m_sem["w2h"], b + 1)
            v.tensor_tensor(M["m_w2l"][:], M["m_w2"][:], f32(M["m_w2h"][:]), ALU.subtract).then_inc(m_sem["w2l"], 1)
            v.wait_ge(s_xb, b * 4 + 3)
            for n in range(2 * FC):
                v.wait_ge(m_sem["h"], b * 2 * FC + n + 1)
                if n == FC:
                    v.wait_ge(m_sem["dn"], b * NT + 4)
                v.tensor_copy(M["m_hh"][:, n % FC, :], M["m_h"][:, n % 2, :]).then_inc(m_sem["hh"], 1)
                v.wait_ge(m_sem["hh"], b * 2 * FC + n + 1)
                v.tensor_tensor(M["m_hl"][:, n % FC, :], M["m_h"][:, n % 2, :], f32(M["m_hh"][:, n % FC, :]), ALU.subtract).then_inc(m_sem["hl"], 1)
                if n % FC == FC - 1:
                    for t in range(4):
                        k = n // FC * 4 + t
                        v.wait_ge(m_sem["dn"], b * NT + k + 1)
                        v.tensor_tensor(x[:, k, :], x[:, k, :], ps[:, 4 + k % 2, 0:D], ALU.add).then_inc(s_xu, 1)
                        ln_step(v, b, 3, x, k)

        def m_g(g, b):
            g.wait_ge(s_xn, b * (NPH * NT) + 3 * NT)
            g.wait_ge(m_sem["w1"], b * 48 + 48)
            g.tensor_tensor(x[:], x[:], M["m_b2"][:].unsqueeze(1).to_broadcast([P, NT, D]), ALU.add).then_inc(s_xb, 1)

        def m_sp(sp, b):
            sp.wait_ge(m_sem["idx"], b + 1)
            sp.sem_inc(m_sem["seen"], 1)
            e = sp.value_load(M["m_idx"][0:1, 0:1], min_val=0, max_val=EXPERTS - 1)
            sp.dma_start(M["m_w1"][:, :, 0:HALF], a["m_w1"][bass.ds(e, 1), :, 0:HALF].rearrange("o (c p) f -> p (o c) f", p=P)).then_inc(m_sem["w1a"], 16)
            sp.dma_start(M["m_w1"][:, :, HALF:FF], a["m_w1"][bass.ds(e, 1), :, HALF:FF].rearrange("o (c p) f -> p (o c) f", p=P)).then_inc(m_sem["w1"], 16)
            sp.dma_start(M["m_b1"][:], a["m_b1"][bass.ds(e, 1)].rearrange("o p f -> p (o f)")).then_inc(m_sem["w1"], 16)
            sp.dma_start(M["m_b2"][:], a["m_b2"][bass.ds(e, 1)].to_broadcast([P, D])).then_inc(m_sem["w1"], 16)
            sp.dma_start(M["m_w2"][:], a["m_w2"][bass.ds(e, 1)].rearrange("o (c p) f -> p (o c) f", p=P)).then_inc(m_sem["w2"], 16)

        bl1 = [(h, i) for h in range(2) for i in range(NT - 1, -1, -1)]
        NB1 = len(bl1)
        l_sem = {k: sem(f"l_{k}") for k in (
            "w", "wh", "wl",
            "k", "ks", "kh", "kl", "dup0", "dup1",
            "q", "qs", "qh", "ql",
            "v", "vs", "v1", "vr", "v2", "v3",
            "score", "max", "exp", "rc",
            "tp", "p1", "p2", "pv",
            "o", "ot", "oh",
            "wod", "wo", "xo")}
        q_ = l_sem
        LQ = [L["l_q0"], L["l_q1"]]
        LK1 = [L["l_k10"], L["l_k11"]]
        LK2 = [L["l_k20"], L["l_k21"]]

        def banks_in(i):
            return i // 4 + 1

        def parts(k):
            return sum(banks_in(bl1[j % NB1][1]) for j in range(k))

        NP1 = parts(NB1)

        def own(h):
            return (slice(0, 64), slice(64, 128)) if h == 0 else (slice(64, 128), slice(0, 64))

        def halves(hf):
            return slice(hf * HALF, (hf + 1) * HALF)

        def part_cols(i, j):
            return slice(j * HALF, min((j + 1) * HALF, (i + 1) * P))

        def l_proj(pe, m, hf, bank, done):
            for c in range(DC):
                last = mm3(pe, ps[:, bank, :], L["l_wh"][:, m, c, :], L["l_wl"][:, m, c, :], xTh[:, c, halves(hf)], xTl[:, c, halves(hf)],
                           c == 0, c == DC - 1)
            last.then_inc(done, 1)

        def l_values(pe, g, bank):
            for t in range(4):
                tok = slice((4 * g + t) * P, (4 * g + t + 1) * P)
                for c in range(DC):
                    last = mm3(pe, ps[:, bank, t * P:(t + 1) * P], xTh[:, c, tok], xTl[:, c, tok], L["l_wh"][:, 2, c, :],
                               L["l_wl"][:, 2, c, :], c == 0, c == DC - 1)
            last.then_inc(q_["v"], 1)

        def l_turn_o(pe, g, bank):
            for t in range(4):
                last = pe.transpose(ps[:, bank, t * P:(t + 1) * P], L["l_o"][:, 4 * g + t, :], idf[:])
            last.then_inc(q_["ot"], 1)

        def l_out(pe, g, bank):
            for t in range(2):
                tok = slice((2 * g + t) * P, (2 * g + t + 1) * P)
                last = pe.matmul(ps[:, bank, t * D:(t + 1) * D], L["l_oT"][:, tok], L["l_wo"][:], start=True, stop=True)
            last.then_inc(q_["wo"], 1)

        def l_score(pe, it, k, first=False):
            h, i = bl1[k % NB1]
            n = (i + 1) * P
            pair = it + k // NB1
            if k % NB1 == 0 or k % NB1 == NT:
                pe.wait_ge(q_["ql"], pair * 2 + h + 1)
                pe.wait_ge(q_[f"dup{h}"], pair * 32 + 32)
            if not (first and k < 2):
                pe.wait_ge(q_["exp"], it * NB1 + k - 1)
            s = banks_of(k)
            for c0 in range(0, n, HALF):
                c1 = min(n, c0 + HALF)
                lhs = LQ[h][:, i * P:(i + 1) * P]
                pe.matmul(s[:, c0:c1], lhs, LK1[h][:, c0:c1], start=True, stop=False)
                pe.matmul(s[:, c0:c1], lhs, LK2[h][:, c0:c1], start=False, stop=c1 < n)
            pe.matmul(s[:, n - P:n], idb[:], causal[:], start=False, stop=True).then_inc(q_["score"], 1)

        def l_turn(pe, it, k, first=False):
            _, i = bl1[k % NB1]
            pe.wait_ge(q_["exp"], it * NB1 + k + 1)
            for j in range(i + 1):
                if j % 4 == 0 and not (first and k == 0) and j // 4 < banks_in(bl1[(k - 1) % NB1][1]):
                    pe.wait_ge(q_["p2"], it * NP1 + parts(k - 1) + j // 4 + 1)
                o = ps[:, 4 + j // 4, (j % 4) * P:(j % 4 + 1) * P]
                last = pe.transpose(o, L["l_pe"][:, k % 2, j * P:(j + 1) * P], idf[:])
                if j == i or j % 4 == 3:
                    last.then_inc(q_["tp"], 1)

        def l_pv(pe, it, k, first, more):
            h, i = bl1[k]
            if k == 0:
                pe.wait_ge(q_["v3"], it * 2 + 1)
                pe.wait_ge(q_["xo"], it * 4 - 3 if not first else it * 4 + 1)
            if k == NT:
                pe.wait_ge(q_["v3"], it * 2 + 2)
                if more:
                    pe.wait_ge(q_["qs"], it * 2 + 4)
                else:
                    pe.wait_ge(q_["oh"], it * 2)
            pe.wait_ge(q_["p2"], it * NP1 + parts(k + 1))
            o = ps[:, 6 + h, i * SD:(i + 1) * SD]
            products = [(0, 0), (0, 1), (0, 2), (1, 0), (1, 1)]
            for j in range(i + 1):
                for n, (pp, vv) in enumerate(products):
                    last = pe.matmul(o, L["l_pt"][:, k % 2, pp, j * P:(j + 1) * P], L["l_v"][:, vv, j, h * SD:(h + 1) * SD],
                                     start=j == 0 and n == 0, stop=j == i and n == len(products) - 1)
            last.then_inc(q_["pv"], 1)

        def l_pe_first(pe, b):
            n = b * HP
            pe.wait_ge(s_lo, ln_done(b, 3))
            pe.wait_ge(q_["wl"], n + 2)
            for hf in range(2):
                l_proj(pe, 1, hf, 2 + hf, q_["k"])
            for hf in range(2):
                l_proj(pe, 0, hf, 4 + hf, q_["q"])
            for g in range(2):
                l_values(pe, g, 6 + g)
            l_score(pe, n, 0, True)
            l_score(pe, n, 1, True)
            l_turn(pe, n, 0, True)
            l_score(pe, n, 2, True)

        def l_pe_body(pe, it, first, more):
            for k in range(NB1):
                if k + 1 < NB1 or more:
                    l_turn(pe, it, k + 1)
                l_pv(pe, it, k, first, more)
                if k + 3 < NB1 or more:
                    l_score(pe, it, k + 3)
                if not first and k == 1:
                    pe.wait_ge(q_["o"], it * 2)
                    l_turn_o(pe, 0, 7)
                if not first and k == 2:
                    pe.wait_ge(q_["oh"], it * 2 - 1)
                    l_turn_o(pe, 1, 7)
                if more and k == 3:
                    pe.wait_ge(q_["wl"], it + 3)
                    if first:
                        pe.wait_ge(q_["vs"], it * 2 + 2)
                    else:
                        pe.wait_ge(q_["oh"], it * 2)
                    l_proj(pe, 1, 0, 7, q_["k"])
                if more and k == 4:
                    pe.wait_ge(q_["ks"], it * 2 + 3)
                    l_proj(pe, 1, 1, 7, q_["k"])
                if more and k == 5:
                    pe.wait_ge(q_["ks"], it * 2 + 4)
                    l_proj(pe, 0, 0, 7, q_["q"])
                if more and k == 6:
                    pe.wait_ge(q_["qs"], it * 2 + 3)
                    l_proj(pe, 0, 1, 7, q_["q"])
                if k == 9:
                    pe.wait_ge(q_["o"], it * 2 + 1)
                if more and k == 9:
                    l_values(pe, 0, 6)
                if more and k == 10:
                    pe.wait_ge(q_["vs"], it * 2 + 3)
                    l_values(pe, 1, 6)
                if not first and k == 11:
                    if more:
                        pe.wait_ge(q_["vs"], it * 2 + 4)
                    pe.wait_ge(q_["oh"], it * 2)
                    pe.wait_ge(q_["wod"], it * 16)
                if not first and 11 <= k < 15:
                    if k > 11:
                        pe.wait_ge(q_["xo"], it * 4 - 3 + k - 11)
                    l_out(pe, k - 11, 6)

        def l_pe_end(pe, b):
            last_pair = b * HP + HP - 1
            pe.wait_ge(q_["o"], last_pair * 2 + 2)
            for g in range(2):
                l_turn_o(pe, g, 7 - g)
            x_pe_kv(pe, C1, b)
            pe.wait_ge(q_["wod"], last_pair * 16 + 16)
            pe.wait_ge(q_["oh"], last_pair * 2 + 2)
            for g in range(4):
                if g == 2:
                    x_pe_m(pe, C1, b)
                if g >= 2:
                    pe.wait_ge(s_xu, b * (NPH * NT) + 3 * NT + 2 * g - 2)
                l_out(pe, g, 7 - g % 2)
            x_pe_bias(pe, C1, b)
            pe.wait_ge(C1.s["ml"], b + 1)
            x_pe_u(pe, C1, b)

        def l_exp(s, it, k, first=False):
            _, i = bl1[k % NB1]
            n = (i + 1) * P
            s.wait_ge(q_["max"], it * NB1 + k + 1)
            if not (first and k < 2):
                s.wait_ge(q_["tp"], it * NP1 + parts(k - 1))
                s.wait_ge(q_["rc"], it * NB1 + k - 1)
            s.activation(L["l_pe"][:, k % 2, 0:n], banks_of(k)[:, 0:n], ACT.Exp, bias=nmax[:, k % 2:k % 2 + 1],
                         accum_out=sums[:, k % 2:k % 2 + 1]).then_inc(q_["exp"], 1)

        def l_upper(s, it, k, first):
            _, i = bl1[k]
            if not (first and k < 2):
                s.wait_ge(q_["pv"], it * NB1 + k - 1)
            for j in range(banks_in(i)):
                here = part_cols(i, j)
                s.wait_ge(q_["tp"], it * NP1 + parts(k) + j + 1)
                s.copy(L["l_pt"][:, k % 2, 0, here], ps[:, 4 + j, 0:here.stop - here.start]).then_inc(q_["p1"], 1)

        def l_w_a(s, n):
            s.wait_ge(q_["w"], n * 16 + 16)
            s.copy(L["l_wh"][:], L["l_w"][:]).then_inc(q_["wh"], 1)

        def l_key_upper(s, n, h):
            mine, _ = own(h)
            s.wait_ge(q_["ks"], n * 2 + 2)
            s.copy(LK1[h][mine, :], L["l_ks"][mine, :]).then_inc(q_["kh"], 1)

        def l_query_upper(s, n, h):
            mine, _ = own(h)
            s.wait_ge(q_["qs"], n * 2 + 2)
            s.copy(LQ[h][mine, :], L["l_qs"][mine, :]).then_inc(q_["qh"], 1)

        def l_value_upper(s, n, h):
            s.wait_ge(q_["vs"], n * 2 + 2)
            s.copy(L["l_v"][:, 0, :, h * SD:(h + 1) * SD], L["l_vs"][:, :, h * SD:(h + 1) * SD]).then_inc(q_["v1"], 1)

        def l_stage(s, n, m, hf, bank):
            made, staged = (("k", "ks"), ("q", "qs"), ("v", "vs"))[m]
            s.wait_ge(q_[made], n * 2 + hf + 1)
            if m == 0:
                s.copy(L["l_ks"][:, halves(hf)], ps[:, bank, :]).then_inc(q_[staged], 1)
            elif m == 1:
                s.activation(L["l_qs"][:, halves(hf)], ps[:, bank, :], ACT.Copy, scale=0.125).then_inc(q_[staged], 1)
            else:
                s.copy(L["l_vs"][:, 4 * hf:4 * hf + 4, :].rearrange("p t d -> p (t d)"), ps[:, bank, :]).then_inc(q_[staged], 1)

        def l_a_first(s, b):
            n = b * HP
            l_w_a(s, n)
            for m in range(2):
                for hf in range(2):
                    l_stage(s, n, m, hf, 2 + 2 * m + hf)
                if m == 0:
                    l_key_upper(s, n, 0)
                else:
                    l_query_upper(s, n, 0)
            for hf in range(2):
                l_stage(s, n, 2, hf, 6 + hf)
            l_value_upper(s, n, 0)
            l_exp(s, n, 0, True)
            l_key_upper(s, n, 1)
            l_query_upper(s, n, 1)

        def l_copy_o(s, pair, g, bank):
            s.wait_ge(q_["ot"], pair * 2 + g + 1)
            s.copy(L["l_oT"][:, halves(g)], ps[:, bank, :]).then_inc(q_["oh"], 1)

        def l_a_body(s, it, hp, first, more):
            for k in range(NB1):
                l_upper(s, it, k, first)
                if k + 1 < NB1 or more:
                    l_exp(s, it, k + 1, first)
                if k == 0:
                    if not first:
                        s.wait_ge(q_["pv"], it * NB1)
                    l_value_upper(s, it, 1)
                if not first and k == 2:
                    s.wait_ge(q_["ot"], it * 2 - 1)
                    s.wait_ge(q_["xo"], it * 4 - 3)
                    s.copy(L["l_oT"][:, halves(0)], ps[:, 7, :]).then_inc(q_["oh"], 1)
                if not first and k == 3:
                    s.wait_ge(q_["ot"], it * 2)
                    s.copy(L["l_oT"][:, halves(1)], ps[:, 7, :]).then_inc(q_["oh"], 1)
                if more and k == 1:
                    s.wait_ge(q_["v"], it * 2 + 2)
                    l_w_a(s, it + 1)
                if more and k == 4:
                    s.wait_ge(q_["kl"], it * 2 + 2)
                    l_stage(s, it + 1, 0, 0, 7)
                if more and k == 5:
                    l_stage(s, it + 1, 0, 1, 7)
                if more and k == 6:
                    s.wait_ge(q_["score"], it * NB1 + NT)
                    l_key_upper(s, it + 1, 0)
                    s.wait_ge(q_["ql"], it * 2 + 2)
                    l_stage(s, it + 1, 1, 0, 7)
                if more and k == 7:
                    l_stage(s, it + 1, 1, 1, 7)
                if more and k == 8:
                    l_query_upper(s, it + 1, 0)
                if more and k == 10:
                    s.wait_ge(q_["v3"], it * 2 + 2)
                    l_stage(s, it + 1, 2, 0, 6)
                if more and k == 11:
                    l_stage(s, it + 1, 2, 1, 6)
                    s.wait_ge(q_["pv"], it * NB1 + NT)
                    l_value_upper(s, it + 1, 0)
                if more and k == 13:
                    s.wait_ge(q_["score"], it * NB1 + NB1)
                    l_key_upper(s, it + 1, 1)
                if more and k == 14:
                    l_query_upper(s, it + 1, 1)
                if k == 15:
                    s.wait_ge(q_["xo"], it * 4 + 1)
                    s.dma_start(L["l_wo"][:], a["l_wo"][bass.ds(hp, 1)].rearrange("o p d -> p (o d)")).then_inc(q_["wod"], 16)

        def l_a_end(s, b):
            last_pair = b * HP + HP - 1
            for g in range(2):
                l_copy_o(s, last_pair, g, 7 - g)

        def l_max(v, it, k, first=False):
            _, i = bl1[k % NB1]
            v.wait_ge(q_["score"], it * NB1 + k + 1)
            if not (first and k < 2):
                v.wait_ge(q_["exp"], it * NB1 + k - 1)
            v.tensor_reduce(nmax[:, k % 2:k % 2 + 1], banks_of(k)[:, 0:(i + 1) * P], AX.X, ALU.max, negate=True).then_inc(q_["max"], 1)

        def l_lower(v, it, k):
            _, i = bl1[k]
            for j in range(banks_in(i)):
                here = part_cols(i, j)
                v.wait_ge(q_["p1"], it * NP1 + parts(k) + j + 1)
                v.tensor_tensor(L["l_pt"][:, k % 2, 1, here], ps[:, 4 + j, 0:here.stop - here.start],
                                L["l_pt"][:, k % 2, 0, here], ALU.subtract).then_inc(q_["p2"], 1)

        def l_inverse(v, it, k, first):
            h, i = bl1[k]
            v.wait_ge(q_["exp"], it * NB1 + k + 1)
            if k % NT == 0 and not first:
                v.wait_ge(q_["o"], it * 2 - 1 + h)
            v.reciprocal(recs[:, h, i:i + 1], sums[:, k % 2:k % 2 + 1]).then_inc(q_["rc"], 1)

        def l_finish(v, pair, h):
            v.wait_ge(q_["rc"], pair * NB1 + (h + 1) * NT)
            v.wait_ge(q_["pv"], pair * NB1 + (h + 1) * NT)
            v.tensor_tensor(L["l_o"][:, :, h * SD:(h + 1) * SD], ps[:, 6 + h, :].rearrange("p (i d) -> p i d", d=SD),
                            recs[:, h, :].unsqueeze(2).to_broadcast([P, NT, SD]), ALU.mult).then_inc(q_["o"], 1)

        def l_w_v(v, n):
            v.wait_ge(q_["wh"], n + 1)
            v.tensor_tensor(L["l_wl"][:], L["l_w"][:], f32(L["l_wh"][:]), ALU.subtract).then_inc(q_["wl"], 1)

        def l_query_lower(v, n, h):
            mine, other = own(h)
            v.wait_ge(q_["qh"], n * 2 + h + 1)
            v.tensor_tensor(LQ[h][other, :], L["l_qs"][mine, :], f32(LQ[h][mine, :]), ALU.subtract).then_inc(q_["ql"], 1)

        def l_v_first(v, b):
            n = b * HP
            l_w_v(v, n)
            l_query_lower(v, n, 0)
            l_max(v, n, 0, True)
            l_max(v, n, 1, True)

        def l_v_body(v, it, first, more):
            for k in range(NB1):
                l_lower(v, it, k)
                l_inverse(v, it, k, first)
                if k + 2 < NB1 or more:
                    l_max(v, it, k + 2)
                if not first and k == 0:
                    l_finish(v, it - 1, 1)
                if more and k == 1:
                    l_w_v(v, it + 1)
                if k == 8:
                    l_finish(v, it, 0)
                if more and k == 9:
                    l_query_lower(v, it + 1, 0)
                if not first and k >= 12:
                    g = k - 12
                    v.wait_ge(q_["wo"], it * 4 - 3 + g)
                    v.tensor_tensor(x[:, 2 * g:2 * g + 2, :].rearrange("p t d -> p (t d)"), x[:, 2 * g:2 * g + 2, :].rearrange("p t d -> p (t d)"),
                                    ps[:, 6, :], ALU.add).then_inc(q_["xo"], 1)
                if k == 2:
                    l_query_lower(v, it, 1)

        def l_v_end(v, b):
            last_pair = b * HP + HP - 1
            l_finish(v, last_pair, 1)
            x_v_kv(v, C1, b)
            for t in range(NT):
                if t == NT // 2:
                    x_v_m(v, C1, b)
                v.wait_ge(q_["wo"], last_pair * 4 + t // 2 + 1)
                v.tensor_tensor(x[:, t, :], x[:, t, :], ps[:, 7 - (t // 2) % 2, (t % 2) * D:(t % 2 + 1) * D], ALU.add).then_inc(s_xu, 1)
                ln_step(v, b, 4, x, t)
            v.sem_inc(q_["xo"], 4)

        def l_key_lower(g, n, h):
            mine, _ = own(h)
            g.wait_ge(q_["kh"], n * 2 + h + 1)
            if h == 1:
                g.wait_ge(q_["v3"], n * 2 + 1)
            g.tensor_tensor(LK2[h][mine, :], L["l_ks"][mine, :], f32(LK1[h][mine, :]), ALU.subtract).then_inc(q_["kl"], 1)

        def l_value_lower(g, n, h):
            cols = slice(h * SD, (h + 1) * SD)
            g.wait_ge(q_["v1"], n * 2 + h + 1)
            if h == 1:
                g.wait_ge(q_["kl"], n * 2 + 2)
            g.tensor_tensor(L["l_vr"][:], L["l_vs"][:, :, cols], L["l_v"][:, 0, :, cols], ALU.subtract).then_inc(q_["vr"], 1)
            g.tensor_tensor(L["l_v"][:, 1, :, cols], L["l_vs"][:, :, cols], L["l_v"][:, 0, :, cols], ALU.subtract).then_inc(q_["v2"], 1)
            g.wait_ge(q_["vr"], n * 2 + h + 1)
            g.wait_ge(q_["v2"], n * 2 + h + 1)
            g.tensor_tensor(L["l_v"][:, 2, :, cols], L["l_vr"][:], L["l_v"][:, 1, :, cols], ALU.subtract).then_inc(q_["v3"], 1)

        def l_g_first(g, b):
            l_key_lower(g, b * HP, 0)
            l_value_lower(g, b * HP, 0)
            l_key_lower(g, b * HP, 1)

        def l_g_body(g, it, more):
            l_value_lower(g, it, 1)
            if more:
                l_key_lower(g, it + 1, 0)
                l_value_lower(g, it + 1, 0)
                l_key_lower(g, it + 1, 1)

        def l_sp_body(sp, b, hp):
            it = b * HP + hp
            sp.wait_ge(s_xu, b * (NPH * NT) + 3 * NT)
            sp.wait_ge(q_["wl"], it + 1)
            sp.dma_start(L["l_w"][:], a["l_w"][bass.ds(hp, 1)].rearrange("o p m c e -> p (o m) c e")).then_inc(q_["w"], 16)
            for h in range(2):
                mine, other = own(h)
                sp.wait_ge(q_["kl"], it * 2 + h + 1)
                sp.dma_start(f32(LK1[h][other, :]), f32(LK1[h][mine, :])).then_inc(q_[f"dup{h}"], 16)
                sp.dma_start(f32(LK2[h][other, :]), f32(LK2[h][mine, :])).then_inc(q_[f"dup{h}"], 16)

        g_sem = {k: sem(f"g_{k}") for k in ("xq", "tp", "xT", "gt", "up", "si", "gh", "hq", "ht", "hT", "dn", "hs", "gr")}

        def psb(bank):
            return ps[:, bank, :].bitcast(BF16)

        def g_pe(pe, b):
            def turn_x(g):
                pe.wait_ge(g_sem["xq"], b * 2 + g + 1)
                o = psb(6 + g)
                for c in range(DC):
                    for t in range(4):
                        last = pe.transpose(o[:, c * HALF + t * P:c * HALF + (t + 1) * P], G["g_xq"][:, 4 * g + t, c * P:(c + 1) * P], idb[:])
                last.then_inc(g_sem["tp"], 1)

            def updown(t):
                tok = slice(t * P, (t + 1) * P)
                for m, w in ((0, wg_q), (1, wu_q)):
                    if t >= 1:
                        pe.wait_ge(g_sem["si" if m == 0 else "gh"], b * NT + t)
                    for n in range(2):
                        for c in range(DC):
                            last = pe.matmul(ps[:, 2 * m + n, :], G["g_xT"][:, c, tok], w[:, c, n * HALF:(n + 1) * HALF],
                                             start=c == 0, stop=c == DC - 1)
                    last.then_inc(g_sem["gt" if m == 0 else "up"], 1)

            def turn(t):
                pe.wait_ge(g_sem["hq"], b * NT + t + 1)
                if t >= 2:
                    pe.wait_ge(g_sem["hT"], b * NT + t - 1)
                for f in range(FC):
                    last = pe.transpose(psb(4 + t % 2)[:, f * P:(f + 1) * P], G["g_hq"][:, t % 2, f * P:(f + 1) * P], idb[:])
                last.then_inc(g_sem["ht"], 1)

            def down(t):
                pe.wait_ge(g_sem["hT"], b * NT + t + 1)
                if t >= 2:
                    pe.wait_ge(s_xu, b * (NPH * NT) + 5 * NT + t - 1)
                for f in range(FC):
                    last = pe.matmul(ps[:, 6 + t % 2, 0:D], G["g_hT"][:, t % 2, f * P:(f + 1) * P], wd_q[:, f, :], start=f == 0, stop=f == FC - 1)
                last.then_inc(g_sem["dn"], 1)

            turn_x(0)
            pe.wait_ge(g_sem["xT"], b * 2 + 1)
            updown(0)
            turn_x(1)
            updown(1)
            pe.wait_ge(g_sem["xT"], b * 2 + 2)
            for t in range(NT):
                if t + 2 < NT:
                    updown(t + 2)
                turn(t)
                down(t)

        def g_v(v, b):
            for g in range(2):
                four = slice(4 * g, 4 * g + 4)
                v.drain()
                v.tensor_reduce(G["g_amx"][:, four], xn[:, four, :], AX.X, ALU.max, apply_absolute_value=True)
                v.drain()
                v.tensor_scalar(G["g_inv"][:, four], G["g_amx"][:, four], EPS, 1.0 / 127.0, ALU.max, ALU.mult)
                v.drain()
                v.reciprocal(G["g_s"][:, four], G["g_inv"][:, four])
                v.tensor_scalar(G["g_ig"][:, four], G["g_inv"][:, four], wsc[:, 0:1], None, ALU.mult)
                v.tensor_scalar(G["g_iu"][:, four], G["g_inv"][:, four], wsc[:, 1:2], None, ALU.mult)
                v.drain()
                for t in range(4 * g, 4 * g + 4):
                    v.tensor_scalar(G["g_t"][:, t, :], xn[:, t, :], G["g_s"][:, t:t + 1], MAGIC, ALU.mult, ALU.add)
                v.drain()
                v.tensor_scalar(G["g_xq"][:, four, :], G["g_t"][:, four, :], MAGIC, 127.0, ALU.subtract, ALU.min).then_inc(g_sem["xq"], 1)

            def hidden(t):
                v.wait_ge(g_sem["up"], b * NT + t + 1)
                v.wait_ge(g_sem["si"], b * NT + t + 1)
                if t >= 2:
                    v.wait_ge(g_sem["gr"], b * NT + t - 1)
                v.scalar_tensor_tensor(out=G["g_h"][:, t % 2, :], in0=ps[:, 2:4, :].rearrange("p a w -> p (a w)"), scalar=G["g_iu"][:, t:t + 1],
                                       in1=G["g_g"][:, t % 2, :], op0=ALU.mult, op1=ALU.mult).then_inc(g_sem["gh"], 1)
                hm, hs, hi = G["g_hm"][:, t:t + 1], G["g_hs"][:, t:t + 1], G["g_hi"][:, t:t + 1]
                v.drain()
                v.tensor_reduce(hm, G["g_h"][:, t % 2, :], AX.X, ALU.max, apply_absolute_value=True)
                v.drain()
                v.tensor_scalar(hm, hm, EPS, 1.0 / 127.0, ALU.max, ALU.mult)
                v.drain()
                v.reciprocal(hs, hm).then_inc(g_sem["hs"], 1)
                v.tensor_scalar(hi, hm, wsc[:, 2:3], None, ALU.mult)

            def add(t):
                v.wait_ge(g_sem["dn"], b * NT + t + 1)
                v.scalar_tensor_tensor(out=x[:, t, :], in0=ps[:, 6 + t % 2, 0:D], scalar=G["g_hi"][:, t:t + 1],
                                       in1=x[:, t, :], op0=ALU.mult, op1=ALU.add).then_inc(s_xu, 1)

            hidden(0)
            for t in range(NT):
                if t + 1 < NT:
                    hidden(t + 1)
                v.wait_ge(g_sem["gr"], b * NT + t + 1)
                if t >= 2:
                    v.wait_ge(g_sem["ht"], b * NT + t - 1)
                v.tensor_scalar(G["g_hq"][:, t % 2, :], G["g_r"][:, t % 2, :], MAGIC, 127.0, ALU.subtract, ALU.min).then_inc(g_sem["hq"], 1)
                if t >= 1:
                    add(t - 1)
            add(NT - 1)

        def g_a(s, b):
            def copy_x(g):
                s.wait_ge(g_sem["tp"], b * 2 + g + 1)
                s.copy(G["g_xT"][:, :, g * HALF:(g + 1) * HALF], psb(6 + g).rearrange("p (c w) -> p c w", c=DC)).then_inc(g_sem["xT"], 1)

            def silu(t):
                s.wait_ge(g_sem["gt"], b * NT + t + 1)
                if t >= 2:
                    s.wait_ge(g_sem["gh"], b * NT + t - 1)
                s.activation(G["g_g"][:, t % 2, :], ps[:, 0:2, :].rearrange("p a w -> p (a w)"), ACT.Silu,
                             scale=G["g_ig"][:, t:t + 1]).then_inc(g_sem["si"], 1)

            copy_x(0)
            silu(0)
            copy_x(1)
            silu(1)
            for t in range(NT):
                s.wait_ge(g_sem["hs"], b * NT + t + 1)
                if t >= 2:
                    s.wait_ge(g_sem["hq"], b * NT + t - 1)
                s.activation(G["g_r"][:, t % 2, :], G["g_h"][:, t % 2, :], ACT.Copy, bias=MAGIC, scale=G["g_hs"][:, t:t + 1]).then_inc(g_sem["gr"], 1)
                if t + 2 < NT:
                    silu(t + 2)
                s.wait_ge(g_sem["ht"], b * NT + t + 1)
                if t >= 2:
                    s.wait_ge(g_sem["dn"], b * NT + t - 1)
                s.copy(G["g_hT"][:, t % 2, :], psb(4 + t % 2)).then_inc(g_sem["hT"], 1)

        quant_loads = [
            (S["s_g"][:].rearrange("p (c n) -> p c n", c=DC), a["g_wg"].rearrange("(c p) n -> p c n", p=P)),
            (S["s_u"][:].rearrange("p (c n) -> p c n", c=DC), a["g_wu"].rearrange("(c p) n -> p c n", p=P)),
            (S["s_d"][:].rearrange("p (c n) -> p c n", c=FC), a["g_wd"].rearrange("(c p) n -> p c n", p=P)),
        ]
        loads = [
            (S["s_wsh"][:], a["a_wsh"].rearrange("(c p) n -> p c n", p=P)), (S["s_om"][:], a["a_om"]), (S["s_wc"][:], a["a_wc"]),
            (S["s_wv"][:], a["a_wv"].rearrange("(c p) n -> p c n", p=P)), (S["s_wo"][:], a["a_wo"].rearrange("(c p) n -> p c n", p=P)),
            (S["s_bv"][:], a["a_bv"]), (S["s_bo"][:], rows(a["a_bo"])), (S["s_lt"][:], rows(a["a_lt"])),
            (bsh[:], rows(a["a_bsh"])), (rbias[:], a["a_rb"].rearrange("(p o) -> p o", o=1)),
            (x0_wq[:], a["x0_wq"].rearrange("(c p) n -> p c n", p=P)), (x0_wk[:, 0, :], a["x0_wk"][0:P]), (x0_wk[0:64, 1, :], a["x0_wk"][P:CTX]),
            (x0_wv[:, 0, :], a["x0_wv"][0:P]), (x0_wv[0:64, 1, :], a["x0_wv"][P:CTX]),
            (x0_wo[:], a["x0_wo"].rearrange("(c p) n -> p c n", p=P)), (x0_bo[:], rows(a["x0_bo"])),
            (x1_wq[:], a["x1_wq"].rearrange("(c p) n -> p c n", p=P)), (x1_wk[:, 0, :], a["x1_wk"][0:P]), (x1_wk[0:64, 1, :], a["x1_wk"][P:CTX]),
            (x1_wv[:, 0, :], a["x1_wv"][0:P]), (x1_wv[0:64, 1, :], a["x1_wv"][P:CTX]),
            (x1_wo[:], a["x1_wo"].rearrange("(c p) n -> p c n", p=P)), (x1_bo[:], rows(a["x1_bo"])),
            (x1_bk[:], a["x1_bk"]), (x1_bv[:], a["x1_bv"]),
            (x1_bq[:], a["x1_bq"]),
            (wr[:], a["m_wr"].rearrange("(c p) n -> p c n", p=P)), (br[:], a["m_br"].rearrange("(o n) -> o n", o=1)),
        ]

        def setup_g(g):
            g.iota(S["s_iota"][:], pattern=[[-1, T]], base=T - P, channel_multiplier=1)
            g.memset(idf[:], 0.0).then_inc(s_gc, 1)
            g.memset(ones_f[:], 1.0).then_inc(s_gc, 1)
            g.memset(causal[:], 0.0).then_inc(s_gc, 1)
            g.memset(row01[:], 0.0).then_inc(s_gc, 1)
            g.memset(blk0[:], 1.0).then_inc(s_gc, 1)
            g.memset(blk1[:], 1.0).then_inc(s_gc, 1)
            g.memset(cosb[:], 0.0).then_inc(s_gc, 1)
            g.memset(ones_b[:], 1.0).then_inc(s_gc, 1)
            g.memset(coss[:], 1.0).then_inc(s_gc, 1)
            g.wait_ge(s_gc, 9)
            g.affine_select(out=idf[:], in_=idf[:], compare_op=ALU.not_equal, fill=1.0, base=0, pattern=[[-1, P]], channel_multiplier=1).then_inc(s_gc, 1)
            g.affine_select(out=causal[:], in_=causal[:], compare_op=ALU.is_ge, fill=NEG, base=0, pattern=[[-1, P]], channel_multiplier=1).then_inc(s_gc, 1)
            g.affine_select(out=row01[:], in_=row01[:], compare_op=ALU.not_equal, fill=1.0, base=0, pattern=[[-1, 2]], channel_multiplier=1).then_inc(s_gc, 1)
            for blk, n, w in ((blk0, 2, XD0), (blk1, 8, XD1)):
                g.affine_select(out=blk[:], in_=blk[:], compare_op=ALU.is_ge, fill=0.0, base=0, pattern=[[-w, n]], channel_multiplier=1).then_inc(s_gc, 1)
            g.affine_select(out=cosb[:], in_=cosb[:], compare_op=ALU.is_ge, fill=math.pi / 2, base=-RFF, pattern=[[0, 1]], channel_multiplier=1).then_inc(s_gc, 1)
            g.affine_select(out=coss[:], in_=coss[:], compare_op=ALU.is_ge, fill=-1.0, base=-RFF, pattern=[[0, 1]], channel_multiplier=1).then_inc(s_gc, 1)
            g.wait_ge(s_gc, 16)
            for blk, n, w in ((blk0, 2, XD0), (blk1, 8, XD1)):
                g.affine_select(out=blk[:], in_=blk[:], compare_op=ALU.is_ge, fill=0.0, base=w - 1, pattern=[[w, n]], channel_multiplier=-1).then_inc(s_gc, 1)
            g.tensor_copy(idb[:], idf[:]).then_inc(s_gc, 1)

        GC = 19

        def setup_a(s):
            s.wait_ge(s_w, 16 * len(loads))
            s.wait_ge(s_gc, GC)
            s.activation(S["s_t"][:, 0:1], S["s_lt"][:], ACT.Abs).then_inc(s_sa, 1)
            s.wait_ge(s_sa, 1)
            s.activation(S["s_t"][:, 1:2], S["s_t"][:, 0:1], ACT.Exp, scale=-1.0).then_inc(s_sa, 1)
            s.wait_ge(s_sa, 2)
            s.activation(S["s_t"][:, 2:3], S["s_t"][:, 1:2], ACT.Ln, bias=1.0).then_inc(s_sa, 1)
            s.wait_ge(s_sv, 1)
            s.activation(S["s_dist"][:], S["s_dist"][:], ACT.Abs)
            s.drain()
            s.activation(S["s_dist"][:], S["s_dist"][:], ACT.Exp, scale=-0.3 / 10.0).then_inc(s_sa, 1)
            s.copy(wsh_h[:], S["s_wsh"][:]).then_inc(s_sa, 1)
            s.copy(om_h[:], S["s_om"][:]).then_inc(s_sa, 1)
            s.wait_ge(s_sv, 2)
            s.copy(wc_h[:], S["s_wc"][:].rearrange("p m o -> p (m o)")).then_inc(s_sa, 1)
            s.copy(ones_r[:], ones_f[0:2, :]).then_inc(s_sa, 1)
            s.wait_ge(s_sp, 1)
            s.copy(wvo_h[:], ps[:, 0, :].rearrange("p (c d) -> p c d", c=DC)).then_inc(s_sa, 1)

        SA = 9

        def setup_v(v):
            v.wait_ge(s_gc, GC)
            v.tensor_copy(S["s_dist"][:], S["s_iota"][:]).then_inc(s_sv, 1)
            v.wait_ge(s_wq, 16 * len(quant_loads))
            for n, w in enumerate(("s_g", "s_u", "s_d")):
                v.tensor_reduce(S["s_abs"][:, n:n + 1], S[w][:], AX.X, ALU.add, apply_absolute_value=True).then_inc(s_qa, 1)
            v.wait_ge(s_qs, 1)
            v.tensor_scalar(wsc[:, 0:3], ps[:, 1, 0:3], 1.0 / (D * FF), EPS, ALU.mult, ALU.max)
            v.drain()
            v.reciprocal(S["s_i8"][:, 0:3], wsc[:, 0:3])
            v.drain()
            for n, (w, q) in enumerate((("s_g", wg_q), ("s_u", wu_q), ("s_d", wd_q))):
                v.tensor_scalar(S["s_q"][:], S[w][:], S["s_i8"][:, n:n + 1], MAGIC, ALU.mult, ALU.add)
                v.drain()
                v.tensor_scalar(S["s_q"][:], S["s_q"][:], MAGIC, 1.0, ALU.subtract, ALU.min)
                v.drain()
                v.tensor_scalar(q[:].rearrange("p c n -> p (c n)"), S["s_q"][:], -1.0, None, ALU.max)
                v.drain()
            v.wait_ge(s_w, 16 * len(loads))
            scale = math.sqrt(2.0 / (2 * RFF)) * math.sqrt(math.exp(-0.5))
            for m in range(ORDERS):
                last = v.tensor_scalar(S["s_wc"][:, m, :], S["s_wc"][:, m, :], scale * math.sqrt(1.0 / math.factorial(m) + 1e-10), None, ALU.mult)
            last.then_inc(s_sv, 1)
            for c in range(DC):
                v.tensor_scalar(S["s_bvb"][:, c, :], ones_f[:], S["s_bv"][:, c:c + 1], None, ALU.mult)
                last = v.tensor_scalar(x1_bqb[:, c, :], ones_f[:], x1_bq[:, c:c + 1], None, ALU.mult)
            last.then_inc(s_sv, 1)
            v.wait_ge(s_sa, 4)
            v.tensor_scalar(S["s_t"][:, 3:4], S["s_lt"][:], 0.0, 0.1, ALU.max, ALU.add)
            v.drain()
            v.tensor_tensor(S["s_t"][:, 3:4], S["s_t"][:, 3:4], S["s_t"][:, 2:3], ALU.add)
            v.drain()
            v.reciprocal(S["s_t"][:, 0:1], S["s_t"][:, 3:4])
            v.drain()
            v.tensor_scalar(decay[:], S["s_dist"][:], S["s_t"][:, 0:1], None, ALU.mult)
            v.wait_ge(s_sa, 7)
            v.tensor_tensor(wsh_l[:], S["s_wsh"][:], f32(wsh_h[:]), ALU.subtract)
            v.tensor_tensor(om_l[:], S["s_om"][:], f32(om_h[:]), ALU.subtract)
            v.tensor_tensor(wc_l[:], S["s_wc"][:].rearrange("p m o -> p (m o)"), f32(wc_h[:]), ALU.subtract)
            v.wait_ge(s_sa, SA)
            v.wait_ge(s_sp, 1)
            v.tensor_tensor(wvo_l[:], ps[:, 0, :].rearrange("p (c d) -> p c d", c=DC), f32(wvo_h[:]), ALU.subtract)
            v.tensor_tensor(bvo[:], ps[:, 2, 0:D], S["s_bo"][:], ALU.add).then_inc(s_sv, 1)

        SV = 4

        def setup_pe(pe):
            pe.wait_ge(s_gc, GC)
            pe.wait_ge(s_qa, 3)
            pe.matmul(ps[:, 1, 0:3], ones_f[:], S["s_abs"][:, 0:3], start=True, stop=True).then_inc(s_qs, 1)
            pe.wait_ge(s_w, 16 * len(loads))
            pe.wait_ge(s_sv, 3)
            for c in range(DC):
                for k in range(DC):
                    pe.matmul(ps[:, 0, c * D:(c + 1) * D], S["s_wv"][:, k, c * P:(c + 1) * P], S["s_wo"][:, k, :], start=k == 0, stop=k == DC - 1)
            for k in range(DC):
                last = pe.matmul(ps[:, 2, 0:D], S["s_bvb"][:, k, :], S["s_wo"][:, k, :], start=k == 0, stop=k == DC - 1)
            last.then_inc(s_sp, 1)

        block = ctx.enter_context(nc.Block())

        @block.sync
        def _(sp):
            for dst, src in quant_loads:
                sp.dma_start(dst, src).then_inc(s_wq, 16)
            for dst, src in loads:
                sp.dma_start(dst, src).then_inc(s_w, 16)
            sp.sem_inc(s_used, 1)
            sp.sem_inc(l_sem["wl"], 1)
            sp.sem_inc(l_sem["xo"], 1)
            with sp.Fori(0, B) as b:
                sp.wait_ge(s_used, b + 1)
                sp.dma_start(xin[:], a["x"][bass.ds(b, 1)].rearrange("o (t p) d -> p (o t) d", p=P)).then_inc(s_xin, 16)
                sp.dma_start(ctxT[:, 0, :], a["ctxT"][bass.ds(b, 1), 0:P].rearrange("o c k -> (o c) k")).then_inc(s_ctx, 16)
                sp.dma_start(ctxT[0:64, 1, :], a["ctxT"][bass.ds(b, 1), P:CTX].rearrange("o c k -> (o c) k")).then_inc(s_ctx, 16)
                sp.dma_start(mrow4[:], a["mask"][bass.ds(b, 1)]).then_inc(s_ctx, 16)
                m_sp(sp, b)
                with sp.Fori(0, HP) as hp:
                    l_sp_body(sp, b, hp)
            sp.wait_ge(s_out, 16 * B + 16)

        @block.gpsimd
        def _(g):
            setup_g(g)
            g.wait_ge(s_sv, SV)
            g.sem_inc(s_out, 16)
            with g.Fori(0, B) as b:
                g.wait_ge(s_out, b * 16 + 16)
                g.wait_ge(s_xn, b * (NPH * NT) + NT)
                g.tensor_tensor(x[:], xin[:], bvo[:].unsqueeze(1).to_broadcast([P, NT, D]), ALU.add).then_inc(s_xb, 1)
                g.wait_ge(C0.s["kvT"], b * 2 + 2)
                x_diagonal(g, C0, b)
                x_g(g, C0, b, x0_bo)
                m_g(g, b)
                l_g_first(g, b)
                with g.Fori(0, HP - 1) as hp:
                    l_g_body(g, b * HP + hp, True)
                l_g_body(g, b * HP + HP - 1, False)
                x_g(g, C1, b, x1_bo)

        @block.scalar
        def _(s):
            setup_a(s)
            s.wait_ge(s_sv, SV)
            with s.Fori(0, B) as b:
                ln_a(s, b, 0)
                a_a(s, b)
                ln_a(s, b, 1)
                x_a(s, C0, b)
                m_a(s, b)
                ln_a(s, b, 3)
                l_a_first(s, b)
                l_a_body(s, b * HP, 0, True, True)
                with s.Fori(1, HP - 1) as hp:
                    l_a_body(s, b * HP + hp, hp, False, True)
                l_a_body(s, b * HP + HP - 1, HP - 1, False, False)
                l_a_end(s, b)
                x_a_m(s, C1, b)
                x_a_u(s, C1, b)
                ln_a(s, b, 4)
                x_a(s, C1, b)
                g_a(s, b)
                s.wait_ge(s_xu, b * (NPH * NT) + NPH * NT)
                s.dma_start(out[bass.ds(b, 1)].rearrange("o (t p) d -> p (o t) d", p=P), x[:]).then_inc(s_out, 16)

        @block.vector
        def _(v):
            setup_v(v)
            with v.Fori(0, B) as b:
                ln_v(v, b, 0, xin)
                ln_lo(v, b, 0)
                a_v(v, b)
                ln_lo(v, b, 1)
                x_v(v, C0, b)
                m_v(v, b)
                ln_lo(v, b, 3)
                l_v_first(v, b)
                l_v_body(v, b * HP, True, True)
                with v.Fori(1, HP - 1) as hp:
                    l_v_body(v, b * HP + hp, False, True)
                l_v_body(v, b * HP + HP - 1, False, False)
                l_v_end(v, b)
                x_v_bias(v, C1, b)
                ln_lo(v, b, 4)
                x_v_u(v, C1, b)
                x_v(v, C1, b)
                g_v(v, b)

        @block.tensor
        def _(pe):
            setup_pe(pe)
            pe.wait_ge(s_sv, SV)
            with pe.Fori(0, B) as b:
                ln_pe(pe, b, 0)
                a_pe(pe, b)
                pe.wait_ge(s_xu, b * (NPH * NT) + 1 * NT)
                ln_pe(pe, b, 1)
                x_pe(pe, C0, b)
                m_pe(pe, b)
                ln_pe(pe, b, 3)
                l_pe_first(pe, b)
                l_pe_body(pe, b * HP, True, True)
                with pe.Fori(1, HP - 1) as hp:
                    l_pe_body(pe, b * HP + hp, False, True)
                l_pe_body(pe, b * HP + HP - 1, False, False)
                l_pe_end(pe, b)
                pe.wait_ge(s_xu, b * (NPH * NT) + 4 * NT)
                ln_pe(pe, b, 4)
                x_pe(pe, C1, b)
                g_pe(pe, b)


def kernel(**inputs):
    import numpy as np
    import concourse.bacc as bacc
    from concourse.bass_utils import run_bass_kernel_spmd

    i = {k: np.asarray(v) for k, v in inputs.items()}
    c = np.ascontiguousarray
    la, lx, lf = "L0_attn_", "L0_xattn_", "L0_ffn_"
    kx, kf = "L1_xattn_", "L1_ffn_"
    wkv = i[kx + "Wkv"].reshape(XH1, 2, XD1, CTX)
    bkv = i[kx + "bkv"].reshape(XH1, 2, XD1)
    qkv = np.stack([i["L1_attn_" + n].reshape(HP, 2 * SD, DC, P) for n in ("w_q", "w_k", "w_v")])
    arrays = {
        "x": c(i["x"]),
        "ctxT": c(i["ctx_768"].transpose(0, 2, 1)),
        "mask": c(i["mask_BxS2_bk0"]).view(np.int32),
        "a_wsh": c(np.concatenate([i[la + "W_shell"], i[la + "W_charge"], i[la + "W_charge"]]).T),
        "a_bsh": c(np.concatenate([i[la + "b_shell"], i[la + "b_charge"], i[la + "b_charge"]])),
        "a_om": c(np.concatenate([i[la + "omega"]] * 4).T),
        "a_rb": c(np.concatenate([i[la + "rff_bias"]] * 2)),
        "a_wc": c(i[la + "W_combine"].reshape(COMB, ORDERS, SHELL).transpose(2, 1, 0)),
        "a_wv": c(i[la + "W_v"]),
        "a_wo": c(i[la + "W_out"].T),
        "a_bv": c(i[la + "b_v"].reshape(DC, P).T),
        "a_bo": c(i[la + "b_out"]),
        "a_lt": c(i[la + "log_temp"].reshape(1)),
        "x0_wq": c(i[lx + "W_q"].T),
        "x0_wk": c(i[lx + "W_k"]),
        "x0_wv": c(i[lx + "W_v"]),
        "x0_wo": c(i[lx + "W_o"]),
        "x0_bo": c(i[lx + "b_o"]),
        "m_wr": c(i[lf + "Wr"]),
        "m_br": c(i[lf + "br"]),
        "m_w1": c(i[lf + "W1"]),
        "m_b1": c(i[lf + "b1"].reshape(EXPERTS, FC, P).transpose(0, 2, 1)),
        "m_w2": c(i[lf + "W2"]),
        "m_b2": c(i[lf + "b2"]),
        "l_w": c(qkv.transpose(1, 4, 0, 3, 2)),
        "l_wo": c(i["L1_attn_w_o"].T).reshape(HP, P, D),
        "x1_wq": c(i[kx + "Wq"]),
        "x1_bq": c(i[kx + "bq"].reshape(DC, P).T),
        "x1_wk": c(wkv[:, 0].reshape(D, CTX).T),
        "x1_wv": c(wkv[:, 1].reshape(D, CTX).T),
        "x1_bk": c(bkv[:, 0].reshape(DC, P).T),
        "x1_bv": c(bkv[:, 1].reshape(DC, P).T),
        "x1_wo": c(i[kx + "Wo"].T),
        "x1_bo": c(i[kx + "bo"]),
        "g_wg": c(i[kf + "w_gate"].T),
        "g_wu": c(i[kf + "w_up"].T),
        "g_wd": c(i[kf + "w_down"].T),
    }
    nc = bacc.Bacc("TRN2", target_bir_lowering=False, num_devices=1)
    given = {f"in_{k}": v for k, v in arrays.items()}
    aps = {k: nc.dram_tensor(f"in_{k}", v.shape, mybir.dt.from_np(v.dtype), kind="ExternalInput").ap() for k, v in arrays.items()}
    out = nc.dram_tensor("out_x", (B, T, D), F32, kind="ExternalOutput").ap()
    decoder_kernel(nc, aps, out)
    r = run_bass_kernel_spmd(nc, [given], core_ids=[0])
    return r.results[0]["out_x"]
```
